# Optimizing a Trainium2 kernel written in Bass

```python
import numpy as np
import jax
import jax.numpy as jnp

def _softmax(x, axis=-1):
    return jax.nn.softmax(x, axis=axis)

def _gelu(x):
    return jax.nn.gelu(x, approximate=True)

def _silu(x):
    return jax.nn.silu(x)

def _sigmoid(x):
    return jax.nn.sigmoid(x)

def _layernorm(x, axis=-1, eps=1e-05):
    m = jnp.mean(x, axis=axis, keepdims=True)
    v = jnp.var(x, axis=axis, keepdims=True)
    return (x - m) / jnp.sqrt(v + eps)

def _scatter_add(tgt, idx, src, axis=0):
    return tgt.at[idx].add(src)

def _segment_sum(src, seg, n):
    return jax.ops.segment_sum(src, seg, n)
kernel_name = 'mk_decoder_preln_d1_seqx_r8_a67906'

def setup_inputs(seed: int=0):
    np.random.seed(seed)
    _w = jnp.asarray

    def _rec_inputs():
        import jax
        import jax.numpy as jnp
        _rk = jax.random.key(seed)
        x = -0.0002928 + 1 * jax.random.normal(jax.random.fold_in(_rk, 1), (1, 1024, 128), jnp.float32)
        _lenS = 1024 - jax.random.randint(jax.random.fold_in(_rk, 7), (1,), 0, max(1, 1024 // 4) + 1, jnp.int32)
        _lenS2 = 6404 - jax.random.randint(jax.random.fold_in(_rk, 8), (1,), 0, max(1, 6404 // 4) + 1, jnp.int32)
        _ctx_1024P = jax.random.normal(jax.random.fold_in(_rk, 11), (1, 16, 128), jnp.float32)
        _ctx_1024c = jax.random.dirichlet(jax.random.fold_in(_rk, 511), 0.3 * jnp.ones((16,), jnp.float32), (1, 6404))
        _ctx_1024t = jnp.einsum('bsk,bkd->bsd', _ctx_1024c, _ctx_1024P)
        _ctx_1024t = _ctx_1024t * jax.lax.rsqrt(jnp.mean(jnp.square(_ctx_1024t)) + 1e-12) * 0.953939
        ctx_1024 = 0.00222621 + 0.99962 * (_ctx_1024t + 0.3 * jax.random.normal(jax.random.fold_in(_rk, 611), (1, 6404, 128), jnp.float32))
        itok_BxS_0_255 = jax.random.randint(jax.random.fold_in(_rk, 12), (1, 1024), 0, 32, jnp.int32)
        return (x, ctx_1024, itok_BxS_0_255)
    x, ctx_1024, itok_BxS_0_255 = _rec_inputs()

    def _L0_attn_setup():
        import jax, jax.numpy as jnp
        import numpy as np
        WINDOW_SIZE = [4, 16, 64, 32]
        B, L, H = (8, 256, 128)
        D1 = 32
        key = jax.random.key(seed)
        ks = jax.random.split(key, 8)
        s = 0.02
        return {'query': jax.random.normal(ks[0], (B, L, H), jnp.float32), 'key_in': jax.random.normal(ks[1], (B, L, H), jnp.float32), 'value': jax.random.normal(ks[2], (B, L, H), jnp.float32), 'qkv_w': jax.random.normal(ks[3], (3 * H, H), jnp.float32) * s, 'qkv_b': jnp.zeros((3 * H,), jnp.float32), 'off_w': jax.random.normal(ks[4], (D1, H), jnp.float32) * s, 'lin2_w': jax.random.normal(ks[5], (1, D1), jnp.float32) * s, 'lin2_b': jnp.zeros((1,), jnp.float32)}
    _L0_attn_all = _L0_attn_setup()
    _L0_attn_in = {k: v for k, v in _L0_attn_all.items() if k in ('key_in', 'value', 'qkv_w', 'qkv_b', 'off_w', 'lin2_w', 'lin2_b')}
    del _L0_attn_all

    def _L0_xattn_setup():
        import jax, jax.numpy as jnp
        import numpy as np
        N_LAYERS = 4
        H = 16
        LOOKBACK = 128
        EPS = 1e-06
        ROPE_BASE = 10000.0
        NEG = jnp.float32(-1e+30)

        def rmsnorm(x, w):
            return x * jax.lax.rsqrt(jnp.mean(x * x, axis=-1, keepdims=True) + EPS) * w

        def rope_cache(L, hd):
            inv = 1.0 / ROPE_BASE ** (jnp.arange(0, hd, 2, dtype=jnp.float32) / hd)
            t = jnp.arange(L, dtype=jnp.float32)
            f = t[:, None] * inv[None, :]
            emb = jnp.concatenate([f, f], axis=-1)
            return (jnp.cos(emb), jnp.sin(emb))

        def apply_rope(x, cos, sin):
            d = x.shape[-1]
            x1, x2 = (x[..., :d // 2], x[..., d // 2:])
            rot = jnp.concatenate([-x2, x1], axis=-1)
            return x * cos + rot * sin

        def split_heads(x, n_heads):
            B, L, D = x.shape
            return x.reshape(B, L, n_heads, D // n_heads).transpose(0, 2, 1, 3)

        def merge_heads(x):
            B, h, L, d = x.shape
            return x.transpose(0, 2, 1, 3).reshape(B, L, h * d)

        def sdpa(q, k, v, bias):
            scale = q.shape[-1] ** (-0.5)
            s = jnp.einsum('bhqd,bhkd->bhqk', q, k) * scale + bias
            p = jax.nn.softmax(s, axis=-1)
            return jnp.einsum('bhqk,bhkd->bhqd', p, v)

        def forward(x, memory, seg_ids, Wqkv, bqkv, Wo, bo, Wq_c, Wkv_c, Wo_c, Wg, Wu, Wd, n1, n2, n3, nf):
            B, L, D = x.shape
            S = memory.shape[1]
            hd = D // H
            cos, sin = rope_cache(L, hd)
            i = jnp.arange(L)
            causal_bias = jnp.where(i[None, :] <= i[:, None], 0.0, NEG)[None, None]
            j = jnp.arange(S)
            allowed = (j[None, None, :] <= seg_ids[:, :, None]) & (j[None, None, :] > seg_ids[:, :, None] - LOOKBACK)
            cross_bias = jnp.where(allowed, 0.0, NEG)[:, None]
            for l in range(N_LAYERS):
                h = rmsnorm(x, n1[l])
                qkv = h @ Wqkv[l].T + bqkv[l]
                q, k, v = jnp.split(qkv, 3, axis=-1)
                q = apply_rope(split_heads(q, H), cos, sin)
                k = apply_rope(split_heads(k, H), cos, sin)
                v = split_heads(v, H)
                o = merge_heads(sdpa(q, k, v, causal_bias)) @ Wo[l].T + bo[l]
                x = x + o
                h2 = rmsnorm(x, n2[l])
                qc = split_heads(h2 @ Wq_c[l].T, H)
                kv = memory @ Wkv_c[l].T
                kc, vc = jnp.split(kv, 2, axis=-1)
                kc, vc = (split_heads(kc, H), split_heads(vc, H))
                oc = merge_heads(sdpa(qc, kc, vc, cross_bias)) @ Wo_c[l].T
                x = x + oc
                h3 = rmsnorm(x, n3[l])
                x = x + jax.nn.silu(h3 @ Wg[l].T) * (h3 @ Wu[l].T) @ Wd[l].T
            return rmsnorm(x, nf)
        key = jax.random.key(seed)
        ks = jax.random.split(key, 16)
        B, L, S, D, F = (2, 256, 32, 128, 512)
        w = 0.02
        inp = {'x': jax.random.normal(ks[0], (B, L, D), jnp.float32), 'memory': jax.random.normal(ks[1], (B, S, D), jnp.float32), 'seg_ids': jnp.sort(jax.random.randint(ks[2], (B, L), 0, S), axis=-1), 'Wqkv': jax.random.normal(ks[3], (N_LAYERS, 3 * D, D), jnp.float32) * w, 'bqkv': jnp.zeros((N_LAYERS, 3 * D), jnp.float32), 'Wo': jax.random.normal(ks[4], (N_LAYERS, D, D), jnp.float32) * w, 'bo': jnp.zeros((N_LAYERS, D), jnp.float32), 'Wq_c': jax.random.normal(ks[5], (N_LAYERS, D, D), jnp.float32) * w, 'Wkv_c': jax.random.normal(ks[6], (N_LAYERS, 2 * D, D), jnp.float32) * w, 'Wo_c': jax.random.normal(ks[7], (N_LAYERS, D, D), jnp.float32) * w, 'Wg': jax.random.normal(ks[8], (N_LAYERS, F, D), jnp.float32) * w, 'Wu': jax.random.normal(ks[9], (N_LAYERS, F, D), jnp.float32) * w, 'Wd': jax.random.normal(ks[10], (N_LAYERS, D, F), jnp.float32) * w, 'n1': jnp.ones((N_LAYERS, D), jnp.float32), 'n2': jnp.ones((N_LAYERS, D), jnp.float32), 'n3': jnp.ones((N_LAYERS, D), jnp.float32), 'nf': jnp.ones((D,), jnp.float32)}
        return inp
    _L0_xattn_all = _L0_xattn_setup()
    _L0_xattn_in = {k: v for k, v in _L0_xattn_all.items() if k in ('Wqkv', 'bqkv', 'Wo', 'bo', 'Wq_c', 'Wkv_c', 'Wo_c', 'Wg', 'Wu', 'Wd', 'n1', 'n2', 'n3', 'nf')}
    del _L0_xattn_all

    def _L0_ffn_setup():
        import jax, jax.numpy as jnp
        import numpy as np
        import math
        E = 8
        K = 2
        CF = 1.2
        D = 128
        H = 512
        key = jax.random.key(seed)
        k0, k1, k2, k3 = jax.random.split(key, 4)
        B, T = (8, 256)
        x_btd = jax.random.normal(k0, (B, T, D), jnp.float32)
        Wr = jax.random.normal(k1, (D, E), jnp.float32) / np.sqrt(D)
        br = jnp.zeros((E,), jnp.float32)
        W1 = jax.random.normal(k2, (E, D, H), jnp.float32) / np.sqrt(D)
        b1 = jnp.zeros((E, H), jnp.float32)
        W2 = jax.random.normal(k3, (E, H, D), jnp.float32) / np.sqrt(H)
        b2 = jnp.zeros((E, D), jnp.float32)
        return dict(x_btd=x_btd, Wr=Wr, br=br, W1=W1, b1=b1, W2=W2, b2=b2)
    _L0_ffn_all = _L0_ffn_setup()
    _L0_ffn_in = {k: v for k, v in _L0_ffn_all.items() if k in ('Wr', 'br', 'W1', 'b1', 'W2', 'b2')}
    del _L0_ffn_all
    return {'x': x, 'ctx_1024': ctx_1024, 'itok_BxS_0_255': itok_BxS_0_255, 'L0_attn_key_in': _L0_attn_in['key_in'], 'L0_attn_value': _L0_attn_in['value'], 'L0_attn_qkv_w': _L0_attn_in['qkv_w'], 'L0_attn_qkv_b': _L0_attn_in['qkv_b'], 'L0_attn_off_w': _L0_attn_in['off_w'], 'L0_attn_lin2_w': _L0_attn_in['lin2_w'], 'L0_attn_lin2_b': _L0_attn_in['lin2_b'], 'L0_xattn_Wqkv': _L0_xattn_in['Wqkv'], 'L0_xattn_bqkv': _L0_xattn_in['bqkv'], 'L0_xattn_Wo': _L0_xattn_in['Wo'], 'L0_xattn_bo': _L0_xattn_in['bo'], 'L0_xattn_Wq_c': _L0_xattn_in['Wq_c'], 'L0_xattn_Wkv_c': _L0_xattn_in['Wkv_c'], 'L0_xattn_Wo_c': _L0_xattn_in['Wo_c'], 'L0_xattn_Wg': _L0_xattn_in['Wg'], 'L0_xattn_Wu': _L0_xattn_in['Wu'], 'L0_xattn_Wd': _L0_xattn_in['Wd'], 'L0_xattn_n1': _L0_xattn_in['n1'], 'L0_xattn_n2': _L0_xattn_in['n2'], 'L0_xattn_n3': _L0_xattn_in['n3'], 'L0_xattn_nf': _L0_xattn_in['nf'], 'L0_ffn_Wr': _L0_ffn_in['Wr'], 'L0_ffn_br': _L0_ffn_in['br'], 'L0_ffn_W1': _L0_ffn_in['W1'], 'L0_ffn_b1': _L0_ffn_in['b1'], 'L0_ffn_W2': _L0_ffn_in['W2'], 'L0_ffn_b2': _L0_ffn_in['b2']}

def reference(x, ctx_1024, itok_BxS_0_255, L0_attn_key_in, L0_attn_value, L0_attn_qkv_w, L0_attn_qkv_b, L0_attn_off_w, L0_attn_lin2_w, L0_attn_lin2_b, L0_xattn_Wqkv, L0_xattn_bqkv, L0_xattn_Wo, L0_xattn_bo, L0_xattn_Wq_c, L0_xattn_Wkv_c, L0_xattn_Wo_c, L0_xattn_Wg, L0_xattn_Wu, L0_xattn_Wd, L0_xattn_n1, L0_xattn_n2, L0_xattn_n3, L0_xattn_nf, L0_ffn_Wr, L0_ffn_br, L0_ffn_W1, L0_ffn_b1, L0_ffn_W2, L0_ffn_b2):
    import jax
    import jax.numpy as jnp

    def _L0_attn_ref(query, key_in, value, qkv_w, qkv_b, off_w, lin2_w, lin2_b):
        import jax, jax.numpy as jnp
        import numpy as np
        WINDOW_SIZE = [4, 16, 64, 32]
        B, L, H = (8, 256, 128)
        D1 = 32
        Bq, Lq, Hq = query.shape
        G = len(WINDOW_SIZE)
        d = Hq // G
        qkv = (query @ qkv_w.T + qkv_b).reshape(Bq, Lq, 3, Hq).transpose(2, 0, 1, 3)
        idx = jnp.arange(Lq)
        absdiff = jnp.abs(idx[:, None] - idx[None, :]).astype(jnp.float32)
        win_mask = jnp.where(idx[None, :] < idx[:, None], 1e+18, absdiff)
        dx_base = jax.nn.sigmoid(jax.nn.relu(query) @ off_w.T @ lin2_w.T + lin2_b) * Lq
        scale = 1.0 / np.sqrt(Lq)
        outs = []
        for i, ws in enumerate(WINDOW_SIZE):
            q = qkv[0, :, :, i * d:(i + 1) * d]
            k = qkv[1, :, :, i * d:(i + 1) * d]
            v = qkv[2, :, :, i * d:(i + 1) * d]
            dx = dx_base + ws
            scores = jnp.einsum('bld,bmd->blm', q, k) * scale
            scores = jnp.where(win_mask[None, :, :] > dx, -1e+18, scores) + scores
            attn = jax.nn.softmax(scores, axis=-1)
            outs.append(jnp.einsum('blm,bmd->bld', attn, v))
        return jnp.concatenate(outs, axis=-1)

    def _L0_xattn_ref(x, memory, seg_ids, Wqkv, bqkv, Wo, bo, Wq_c, Wkv_c, Wo_c, Wg, Wu, Wd, n1, n2, n3, nf):
        import jax, jax.numpy as jnp
        import numpy as np
        N_LAYERS = 4
        H = 16
        LOOKBACK = 128
        EPS = 1e-06
        ROPE_BASE = 10000.0
        NEG = jnp.float32(-1e+30)

        def rmsnorm(x, w):
            return x * jax.lax.rsqrt(jnp.mean(x * x, axis=-1, keepdims=True) + EPS) * w

        def rope_cache(L, hd):
            inv = 1.0 / ROPE_BASE ** (jnp.arange(0, hd, 2, dtype=jnp.float32) / hd)
            t = jnp.arange(L, dtype=jnp.float32)
            f = t[:, None] * inv[None, :]
            emb = jnp.concatenate([f, f], axis=-1)
            return (jnp.cos(emb), jnp.sin(emb))

        def apply_rope(x, cos, sin):
            d = x.shape[-1]
            x1, x2 = (x[..., :d // 2], x[..., d // 2:])
            rot = jnp.concatenate([-x2, x1], axis=-1)
            return x * cos + rot * sin

        def split_heads(x, n_heads):
            B, L, D = x.shape
            return x.reshape(B, L, n_heads, D // n_heads).transpose(0, 2, 1, 3)

        def merge_heads(x):
            B, h, L, d = x.shape
            return x.transpose(0, 2, 1, 3).reshape(B, L, h * d)

        def sdpa(q, k, v, bias):
            scale = q.shape[-1] ** (-0.5)
            s = jnp.einsum('bhqd,bhkd->bhqk', q, k) * scale + bias
            p = jax.nn.softmax(s, axis=-1)
            return jnp.einsum('bhqk,bhkd->bhqd', p, v)

        def forward(x, memory, seg_ids, Wqkv, bqkv, Wo, bo, Wq_c, Wkv_c, Wo_c, Wg, Wu, Wd, n1, n2, n3, nf):
            B, L, D = x.shape
            S = memory.shape[1]
            hd = D // H
            cos, sin = rope_cache(L, hd)
            i = jnp.arange(L)
            causal_bias = jnp.where(i[None, :] <= i[:, None], 0.0, NEG)[None, None]
            j = jnp.arange(S)
            allowed = (j[None, None, :] <= seg_ids[:, :, None]) & (j[None, None, :] > seg_ids[:, :, None] - LOOKBACK)
            cross_bias = jnp.where(allowed, 0.0, NEG)[:, None]
            for l in range(N_LAYERS):
                h = rmsnorm(x, n1[l])
                qkv = h @ Wqkv[l].T + bqkv[l]
                q, k, v = jnp.split(qkv, 3, axis=-1)
                q = apply_rope(split_heads(q, H), cos, sin)
                k = apply_rope(split_heads(k, H), cos, sin)
                v = split_heads(v, H)
                o = merge_heads(sdpa(q, k, v, causal_bias)) @ Wo[l].T + bo[l]
                x = x + o
                h2 = rmsnorm(x, n2[l])
                qc = split_heads(h2 @ Wq_c[l].T, H)
                kv = memory @ Wkv_c[l].T
                kc, vc = jnp.split(kv, 2, axis=-1)
                kc, vc = (split_heads(kc, H), split_heads(vc, H))
                oc = merge_heads(sdpa(qc, kc, vc, cross_bias)) @ Wo_c[l].T
                x = x + oc
                h3 = rmsnorm(x, n3[l])
                x = x + jax.nn.silu(h3 @ Wg[l].T) * (h3 @ Wu[l].T) @ Wd[l].T
            return rmsnorm(x, nf)
        return forward(x, memory, seg_ids, Wqkv, bqkv, Wo, bo, Wq_c, Wkv_c, Wo_c, Wg, Wu, Wd, n1, n2, n3, nf)

    def _L0_ffn_ref(x_btd, Wr, br, W1, b1, W2, b2):
        import jax, jax.numpy as jnp
        import numpy as np
        import math
        E = 8
        K = 2
        CF = 1.2
        D = 128
        H = 512
        B, T, Dm = x_btd.shape
        N = B * T
        x = x_btd.reshape(N, Dm)
        cap = int(math.ceil(CF * N / E))
        probs = jax.nn.softmax(x @ Wr + br, axis=-1)
        gates, ids = jax.lax.top_k(probs, K)
        flat_ids = ids.reshape(-1)
        flat_g = gates.reshape(-1)
        M = N * K
        order = jnp.lexsort((-flat_g, flat_ids))
        s_ids = flat_ids[order]
        s_tok = (order // K).astype(jnp.int32)
        s_g = flat_g[order]
        counts = jnp.bincount(flat_ids, length=E)
        starts = jnp.concatenate([jnp.zeros((1,), counts.dtype), jnp.cumsum(counts)[:-1]])
        rank = jnp.arange(M) - starts[s_ids]
        valid = rank < cap
        pos = jnp.where(valid, s_ids * cap + rank, E * cap)
        disp_tok = jnp.zeros((E * cap + 1,), jnp.int32).at[pos].set(s_tok)[:E * cap]
        disp_g = jnp.zeros((E * cap + 1,), x.dtype).at[pos].set(s_g)[:E * cap]
        xg = x[disp_tok].reshape(E, cap, Dm)
        h = jax.nn.silu(jnp.einsum('ecd,edh->ech', xg, W1) + b1[:, None, :])
        out = jnp.einsum('ech,ehd->ecd', h, W2) + b2[:, None, :]
        gated = out * disp_g.reshape(E, cap, 1)
        y = jnp.zeros((N, Dm), x.dtype).at[disp_tok].add(gated.reshape(E * cap, Dm))
        return y.reshape(B, T, Dm)
    x = x + _L0_attn_ref(_layernorm(x, axis=-1), L0_attn_key_in, L0_attn_value, L0_attn_qkv_w, L0_attn_qkv_b, L0_attn_off_w, L0_attn_lin2_w, L0_attn_lin2_b)
    x = x + _L0_xattn_ref(_layernorm(x, axis=-1), ctx_1024, itok_BxS_0_255, L0_xattn_Wqkv, L0_xattn_bqkv, L0_xattn_Wo, L0_xattn_bo, L0_xattn_Wq_c, L0_xattn_Wkv_c, L0_xattn_Wo_c, L0_xattn_Wg, L0_xattn_Wu, L0_xattn_Wd, L0_xattn_n1, L0_xattn_n2, L0_xattn_n3, L0_xattn_nf)
    x = x + _L0_ffn_ref(_layernorm(x, axis=-1), L0_ffn_Wr, L0_ffn_br, L0_ffn_W1, L0_ffn_b1, L0_ffn_W2, L0_ffn_b2)
    return x

_drawn_inputs = setup_inputs


def setup_inputs(seed=0):
    import zlib

    import numpy as np

    out = dict(_drawn_inputs(seed))
    spreads = {'L0_attn_qkv_b': (0.0, 0.1),
     'L0_xattn_bqkv': (0.0, 0.36),
     'L0_xattn_bo': (0.0, 0.1),
     'L0_xattn_n1': (1.0, 0.6),
     'L0_xattn_n2': (1.0, 0.6),
     'L0_xattn_n3': (1.0, 0.6),
     'L0_xattn_nf': (1.0, 0.2),
     'L0_ffn_br': (0.0, 0.302),
     'L0_ffn_b1': (0.0, 0.651),
     'L0_ffn_b2': (0.0, 0.408)}
    factors = {'L0_attn_qkv_w': 2.973,
     'L0_attn_off_w': 8.0,
     'L0_attn_lin2_w': 8.0,
     'L0_xattn_Wqkv': 5.332,
     'L0_xattn_Wq_c': 27.164,
     'L0_xattn_Wg': 3.695,
     'L0_xattn_Wu': 3.792,
     'L0_xattn_Wd': 3.835}
    for name, (base, spread) in spreads.items():
        noise = np.random.default_rng([zlib.crc32(name.encode()), seed]).standard_normal(out[name].shape)
        drawn = base * np.exp(spread * noise) if base else spread * noise
        out[name] = jnp.asarray(drawn.astype(out[name].dtype))
    for name, factor in factors.items():
        out[name] = (out[name] * factor).astype(out[name].dtype)
    return out
```

```python
from contextlib import ExitStack

import numpy as np

import concourse.bass as bass
from concourse import mybir

ALU = mybir.AluOpType
ACT = mybir.ActivationFunctionType
F32 = mybir.dt.float32
BF16 = mybir.dt.bfloat16
I32 = mybir.dt.int32
AX_X = mybir.AxisListType.X

P = 128
T = 1024
D = 128
NT = T // P
CH = 512
NCH = T // CH
TPC = CH // P
WINDOWS = (4, 16, 64, 32)
WH = len(WINDOWS)
WD = D // WH
LAYERS = 4
H = 16
HD = D // H
QUADS = H // 4
S_MEM = 6404
KEYS = P
MEM_BLOCKS = -(-S_MEM // KEYS)
NEAR = 32
LOOKBACK = 128
F = 512
FT = F // P
NEG = -float(2 ** 100)
NEG_PAD = -float(2 ** 120)
WIN_NEG = -float(2 ** 60)
E = 8
TOPK = 2
CAP = 154
MF = 512
MT = MF // P

Q_PART = (0, 1, 2, 0, 1, 0)
K_PART = (0, 0, 0, 1, 1, 2)
SLOTS = len(Q_PART)
ZERO_ROWS = 24
MAX_ROW = SLOTS * HD + ZERO_ROWS
KROWS = MAX_ROW + 3

C_ID, C_MEAN, C_MASKT, C_MASKQ, C_NEGI, C_HM, C_REL = 0, 128, 256, 384, 512, 640, 644
C_EPS5, C_EPS6, C_ONE = 644 + T, 645 + T, 646 + T
C_COLS = 647 + T
R_COS, R_SIN, R_HM16, R_VMASK, R_IOTA, R_TRI, R_OFFD = 0, T, 2 * T, 2 * T + 16, 2 * T + 16 + D * QUADS, 2 * T + 144 + D * QUADS, 2 * T + 272 + D * QUADS
R_EREV = 2 * T + 400 + D * QUADS
R_COLS = R_EREV + E
WA_QK, WA_V, WA_BV, WA_SM = 0, 4 * D, 5 * D, 6 * D
SM_N1, SM_BQ, SM_BQR, SM_BK, SM_BKR = 0, 1, 2, 3, 4
WA_COLS = 6 * D + 5
WB_O, WB_QC, WB_KC, WB_VC, WB_OC, WB_SM = 0, D, 2 * D, 3 * D, 4 * D, 5 * D
SM_BO, SM_N2, SM_N3 = 0, 1, 2
WB_G, WB_U, WB_DN = 5 * D + 3, 5 * D + 3 + F, 5 * D + 3 + 2 * F
WB_COLS = 5 * D + 3 + 3 * F
WW_Q, WW_K, WW_V, WW_BV, WW_OFF, WW_SM = 0, D, 2 * D, 3 * D, 4 * D, 4 * D + WD
WW_COLS = 4 * D + WD + 4
RT_W, RT_B, RT_B1 = 0, E, 2 * E
RT_COLS = 2 * E + E * MT


def attention_steps():
    def maxima(g):
        for t in range(NT):
            if t >= TPC:
                for j in range(4):
                    yield ("max", g, t, ((j, 0, CH, 0),), 1)
            first = (t // TPC) * CH
            width = P * (t % TPC + 1)
            per = CH // width
            for j0 in range(0, 4, per):
                yield ("max", g, t, tuple((j0 + i, first, width, i * width) for i in range(per)), 0)
        yield ("maxT", g)

    def products(g):
        items = [(c, kb) for c in range(NCH) for kb in range(TPC * (c + 1))]
        out = []
        for i, (c, kb) in enumerate(items):
            out += [("score", g, c, kb, 0), ("score", g, c, kb, 1)]
            if i:
                out.append(("value", g, *items[i - 1]))
            if i and items[i - 1][0] != c:
                pend = ("outT", g, items[i - 1][0])
            if i == TPC + 2:
                out.append(pend)
        out += [("value", g, *items[-1])]
        return out, ("outT", g, NCH - 1)

    lead = 8
    order, tail = [], []
    for s in range(QUADS + 1):
        a = list(maxima(s)) if s < QUADS else []
        b, last = products(s - 1) if s else ([], None)
        order += a[:lead]
        if tail:
            order += tail
            tail = []
        a = a[lead:]
        n = max(len(a), len(b))
        for i in range(n):
            order += a[i * len(a) // n:(i + 1) * len(a) // n]
            order += b[i * len(b) // n:(i + 1) * len(b) // n]
        if last:
            tail = [last]
    order += tail

    n = m = item = 0
    steps = []
    for o in order:
        if o[0] in ("max", "maxT", "outT"):
            steps.append((o[0], n, *o[1:]))
            n += 1
        elif o[0] == "score":
            steps.append(("score", m, m // 2, *o[1:]))
            m += 1
        else:
            _, g, c, kb = o
            steps.append(("value", item, g, c, kb, kb == TPC * (c + 1) - 1))
            item += 1
    return steps


def build(nc, x_t, seg_row, seg_col, consts, tables, win_w, mem_t, layer_a, layer_b, router, w1, w2,
          b2, nf, out):
    ctx = ExitStack()

    def sb(name, shape, dt=F32):
        return ctx.enter_context(nc.sbuf_tensor(name, shape, dt))

    with ctx:
        ps = ctx.enter_context(nc.psum_tensor("ps", [P, 8, CH], F32))
        con = sb("con", [P, C_COLS])
        tab = sb("tab", [P, R_COLS])
        id_b = sb("id_b", [P, P], BF16)
        mask_t = sb("mask_t", [P, P], BF16)
        mask_q = sb("mask_q", [P, P], BF16)
        neg_i = sb("neg_i", [P, P], BF16)
        ident, mean_w = con[:, C_ID:C_ID + P], con[:, C_MEAN:C_MEAN + P]
        head_mask = con[:, C_HM:C_HM + WH]
        rel = con[:, C_REL:C_REL + T]
        eps5, eps6 = con[:, C_EPS5:C_EPS5 + 1], con[:, C_EPS6:C_EPS6 + 1]
        cos_t, sin_t = tab[:, R_COS:R_COS + T], tab[:, R_SIN:R_SIN + T]
        wa = sb("wa", [P, WA_COLS])
        wb = sb("wb", [P, WB_COLS])
        nf_col = sb("nf_col", [P, 1])
        x_res = sb("x_res", [P, T])
        x_dec = sb("x_dec", [P, T])
        h = sb("h", [P, T])
        cen = sb("cen", [P, T])
        sq = sb("sq", [P, T])
        rs = sb("rs", [P, T])
        big = sb("big", [P, 32 * T], BF16)
        q_x = big[:, 0:16 * T].rearrange("p (h t) -> p h t", h=H)
        k_x = big[:, 16 * T:32 * T].rearrange("p (h t) -> p h t", h=H)
        parts = sb("parts", [P, 2, 3, T], BF16)
        qk = sb("qk", [P, 2, T])
        tmp = sb("tmp", [P, 2, CH])
        v_aug = sb("v_aug", [P, NT, H, 32])
        prob = sb("prob", [P, 4, 2, CH])
        o_t = sb("o_t", [P, CH])
        o_n = sb("o_n", [P, NT, D])
        o_d = sb("o_d", [P, T])
        max_q = sb("max_q", [P, 4, NT])
        max_f = sb("max_f", [P, 4, NT])
        max_s = sb("max_s", [32, 2, P])
        max_p = sb("max_p", [32, 3, P], BF16)
        den = sb("den", [P, 4, 4])
        seg_q = sb("seg_q", [P, NT])
        mask_near = sb("mask_near", [P, NT, NEAR], BF16)
        flag = sb("flag", [1, 8])
        flag_i = sb("flag_i", [1, 1], I32)

        names = {}

        def sem(name):
            if name not in names:
                names[name] = pool[len(names)]
            return names[name]

        pool = [ctx.enter_context(nc.semaphore(f"phase_sem{i}")) for i in range(32)]
        first_sem, last_sem = pool[0].num, pool[-1].num

        def phase():
            names.clear()
            return nc.Block(no_gpsimd_drain=True)

        def end_phase():
            nc.all_engine_barrier(sems_to_clear=range(first_sem, last_sem + 1))

        def chain(eng, name):
            s, n = sem(name), [0]

            def link(ins):
                n[0] += 1
                ins.then_inc(s, 1)
                eng.wait_ge(s, n[0])
            return link

        def chunk(c):
            return slice(c * CH, (c + 1) * CH)

        def tile(t):
            return slice(t * P, (t + 1) * P)

        def norm_phase(src, dst, layer, eps, weight=None):
            with phase() as block:
                centred, squared = sem("centred"), sem("squared")
                mean_ps, var_ps = sem("mean_ps"), sem("var_ps")
                logged, root = sem("logged"), sem("root")

                @block.tensor
                def _(pe):
                    if layer:
                        for c in range(NCH):
                            nc.tensor.matmul(ps[:, c, :], mean_w, src[:, chunk(c)], start=True,
                                             stop=True).then_inc(mean_ps, 1)
                    for c in range(NCH):
                        pe.wait_ge(squared, c + 1)
                        nc.tensor.matmul(ps[:, 2 + c, :], mean_w, sq[:, chunk(c)], start=True,
                                         stop=True).then_inc(var_ps, 1)

                @block.scalar
                def _(act):
                    for c in range(NCH):
                        if layer:
                            act.wait_ge(centred, c + 1)
                        x = cen if layer else src
                        nc.scalar.activation(sq[:, chunk(c)], x[:, chunk(c)], ACT.Square).then_inc(squared, 1)
                    for c in range(NCH):
                        act.wait_ge(var_ps, c + 1)
                        nc.scalar.activation(rs[:, chunk(c)], ps[:, 2 + c, :], ACT.Ln,
                                             bias=eps).then_inc(logged, 1)
                    for c in range(NCH):
                        act.wait_ge(logged, c + 1)
                        nc.scalar.activation(rs[:, chunk(c)], rs[:, chunk(c)], ACT.Exp,
                                             scale=-0.5).then_inc(root, 1)

                @block.vector
                def _(dve):
                    if layer:
                        for c in range(NCH):
                            dve.wait_ge(mean_ps, c + 1)
                            nc.vector.tensor_tensor(cen[:, chunk(c)], src[:, chunk(c)], ps[:, c, :],
                                                    ALU.subtract).then_inc(centred, 1)
                        dve.wait_ge(centred, NCH)
                    for c in range(NCH):
                        x = cen if layer else src
                        dve.wait_ge(root, c + 1)
                        if weight is None:
                            nc.vector.tensor_tensor(dst[:, chunk(c)], x[:, chunk(c)], rs[:, chunk(c)],
                                                    ALU.mult)
                        else:
                            nc.vector.scalar_tensor_tensor(dst[:, chunk(c)], x[:, chunk(c)], weight,
                                                           rs[:, chunk(c)], ALU.mult, ALU.mult)
            end_phase()

        def load_phase(win):
            with phase() as block:
                got, cast = sem("got"), sem("cast")
                seg_i = tmp[:, 0, 0:NT].bitcast(I32)
                seg_r = sq[0:1, :].bitcast(I32)

                @block.sync
                def _(sp):
                    sp.dma_start(x_res[:, :], x_t).then_inc(got, 16)
                    sp.dma_start(con[:, :], consts).then_inc(got, 16)
                    sp.dma_start(win[:, :], win_w).then_inc(got, 16)
                    sp.dma_start(seg_i, seg_col).then_inc(got, 16)
                    sp.dma_start(seg_r, seg_row).then_inc(got, 16)
                    sp.dma_start(tab[:, :], tables[:, 0:R_COLS]).then_inc(got, 16)
                    sp.dma_start(nf_col[:, :], nf).then_inc(got, 16)
                    sp.dma_start(wa[:, :], layer_a[0]).then_inc(got, 16)
                    sp.wait_ge(got, 16 * 8)

                @block.gpsimd
                def _(pool_):
                    link = chain(pool_, "pool_step")
                    link(nc.gpsimd.memset(v_aug[:, :, :, :], 0.0))
                    nc.gpsimd.memset(v_aug[:, :, :, HD:HD + 1], 1.0)

                @block.vector
                def _(dve):
                    link = chain(dve, "dve_step")
                    dve.wait_ge(got, 16 * 8)
                    nc.vector.tensor_copy(id_b[:, :], ident)
                    nc.vector.tensor_copy(mask_t[:, :], con[:, C_MASKT:C_MASKT + P])
                    nc.vector.tensor_copy(mask_q[:, :], con[:, C_MASKQ:C_MASKQ + P])
                    nc.vector.tensor_copy(neg_i[:, :], con[:, C_NEGI:C_NEGI + P])
                    link(nc.vector.tensor_copy(seg_q[:, :], seg_i))
                    for t in range(NT):
                        nc.vector.tensor_scalar(mask_near[:, t, :], tab[:, R_IOTA:R_IOTA + NEAR],
                                                seg_q[:, t:t + 1], NEG, ALU.is_gt, ALU.mult)
                    link(nc.vector.tensor_copy(rs[0:1, :], seg_r))
                    link(nc.vector.tensor_reduce(flag[:, 0:1], rs[0:1, :], AX_X, ALU.max))
                    link(nc.vector.tensor_reduce(flag[:, 1:2], rs[0:1, :], AX_X, ALU.min))
                    link(nc.vector.tensor_scalar(flag[:, 2:3], flag[:, 0:1], float(NEAR - 1), None, ALU.is_gt))
                    link(nc.vector.tensor_scalar(flag[:, 3:4], flag[:, 1:2], 0.0, None, ALU.is_lt))
                    link(nc.vector.tensor_tensor(flag[:, 4:5], flag[:, 2:3], flag[:, 3:4], ALU.max))
                    nc.vector.tensor_copy(flag_i[:, :], flag[:, 4:5])
            end_phase()

        def window_phase(win):
            q_m = [big[:, 2 * T * i:2 * T * (i + 1)].bitcast(F32) for i in range(WH)]
            k_t = big[:, 8 * T:10 * T].bitcast(F32)
            v_n = big[:, 10 * T:12 * T].bitcast(F32).rearrange("p (t d) -> p t d", t=NT)
            relu = big[:, 12 * T:14 * T].bitcast(F32)
            prob_q = [big[:, 14 * T + 2 * T * i:16 * T + 2 * T * i].bitcast(F32) for i in range(3)]
            hide = [big[:, (20 + i) * T:(21 + i) * T] for i in range(3)]
            off = big[0:WD, 24 * T:26 * T].bitcast(F32)
            prob_t = prob[:, :, :, :].rearrange("p a b c -> p (a b) c")
            dx = sb("dx", [P, 1 + WH, NT])
            bq_m = sb("bq_m", [P, WH])
            wmax = sb("wmax", [P, 2, WH * NT])
            wbias = sb("wbias", [P, WH * NT])
            wsum = sb("wsum", [P, WH * NT])
            wrec = sb("wrec", [P, WH * NT])
            scale = 2.0 / float(np.sqrt(T))
            units = [(t, i) for t in range(NT) for i in range(WH)]

            with phase() as block:
                proj, proj_out = sem("proj"), sem("proj_out")
                relu_ok, off_ps, off_ok, z_ps, dx_ok = (sem(x) for x in ("relu_ok", "off_ps", "off_ok", "z_ps", "dx_ok"))
                hide_ok, s_ps, p_ok, p_n = sem("hide_ok"), sem("s_ps"), sem("p_ok"), sem("p_n")
                m_ok, pt_ps, pt_ok, o_ps, o_ok = (sem(x) for x in ("m_ok", "pt_ps", "pt_ok", "o_ps", "o_ok"))

                groups = []
                for n, (t, i) in enumerate(units):
                    w = NT - t
                    for b in range(0, w, 4):
                        groups.append((len(groups), n, b, min(4, w - b)))
                by_unit = {n: [g for g in groups if g[1] == n] for n in range(len(units))}

                @block.tensor
                def _(pe):
                    for j, col in enumerate((WW_K, WW_Q)):
                        for c in range(NCH):
                            nc.tensor.matmul(ps[:, 2 * j + c, :], win[:, col:col + D], h[:, chunk(c)],
                                             start=True, stop=True).then_inc(proj, 1)
                    for c in range(NCH):
                        for t in range(TPC):
                            mm = nc.tensor.matmul(ps[:, 4 + c, tile(t)], h[:, tile(TPC * c + t)],
                                                  win[:, WW_V:WW_V + D], start=True, stop=True)
                        mm.then_inc(proj, 1)
                    for c in range(NCH):
                        pe.wait_ge(relu_ok, c + 1)
                        nc.tensor.matmul(ps[0:WD, 6 + c, :], win[:, WW_OFF:WW_OFF + WD], relu[:, chunk(c)],
                                         start=True, stop=True).then_inc(off_ps, 1)
                    pe.wait_ge(off_ok, NCH)
                    for t in range(NT):
                        mm = nc.tensor.matmul(ps[:, 6, t:t + 1], off[:, tile(t)],
                                              win[0:WD, WW_SM + 2:WW_SM + 3], start=True, stop=True)
                    mm.then_inc(z_ps, 1)

                    def scores(n):
                        t, i = units[n]
                        if n >= 2:
                            pe.wait_ge(p_ok, n - 1)
                        pe.wait_ge(hide_ok, n + 1)
                        w = T - t * P
                        for b in range(0, w, CH):
                            nn = min(CH, w - b)
                            bank = ps[:, 2 * (n % 2) + b // CH, 0:nn]
                            nc.tensor.matmul(bank, q_m[i][:, tile(t)], k_t[:, t * P + b:t * P + b + nn],
                                             start=True, stop=False)
                            mm = nc.tensor.matmul(bank, neg_i[:, :], hide[n % 3][:, b:b + nn],
                                                  start=False, stop=True)
                        mm.then_inc(s_ps, 1)

                    def turn(n):
                        pe.wait_ge(p_n, n + 1)
                        for g, _, b, cnt in by_unit[n]:
                            if g >= 2:
                                pe.wait_ge(pt_ok, g - 1)
                            for k in range(cnt):
                                mm = nc.tensor.transpose(ps[:, 4 + g % 2, tile(k)],
                                                         prob_q[n % 3][:, tile(b + k)], ident)
                            mm.then_inc(pt_ps, 1)

                    def values(n):
                        t, i = units[n]
                        if i == 0 and t >= 2:
                            pe.wait_ge(o_ok, t - 1)
                        for g, _, b, cnt in by_unit[n]:
                            pe.wait_ge(pt_ok, g + 1)
                            for k in range(cnt):
                                mm = nc.tensor.matmul(ps[i * WD:(i + 1) * WD, 6 + t % 2, 0:P],
                                                      v_n[:, t + b + k, i * WD:(i + 1) * WD],
                                                      prob_t[:, g % 8, tile(k)],
                                                      start=(b + k == 0), stop=(b + k == NT - t - 1),
                                                      tile_position=(0, i * WD))
                        mm.then_inc(o_ps, 1)

                    pe.wait_ge(proj_out, 7)
                    for n in range(len(units) + 2):
                        if n == 1:
                            pe.wait_ge(dx_ok, 1)
                        if n < len(units):
                            scores(n)
                        if 1 <= n <= len(units):
                            turn(n - 1)
                        if n >= 2:
                            values(n - 2)

                @block.scalar
                def _(act):
                    link = chain(act, "act_step")
                    for c in range(NCH):
                        nc.scalar.activation(relu[:, chunk(c)], h[:, chunk(c)], ACT.Relu).then_inc(relu_ok, 1)
                    act.wait_ge(proj, 4)
                    act.wait_ge(proj_out, 1)
                    for i in range(WH):
                        for c in range(NCH):
                            ins = nc.scalar.activation(q_m[i][:, chunk(c)], ps[:, 2 + c, :], ACT.Identity,
                                                       bias=bq_m[:, i:i + 1], scale=head_mask[:, i:i + 1])
                        ins.then_inc(proj_out, 1)
                    act.wait_ge(off_ps, NCH)
                    for c in range(NCH):
                        ins = nc.scalar.copy(off[:, chunk(c)], ps[0:WD, 6 + c, :]).then_inc(off_ok, 1)
                    act.wait_ge(z_ps, 1)
                    nc.scalar.activation(dx[:, 0, :], ps[:, 6, 0:NT], ACT.Sigmoid,
                                         bias=win[:, WW_SM + 3:WW_SM + 4]).then_inc(z_ps, 1)

                    def exps(n):
                        t, i = units[n]
                        w = T - t * P
                        act.wait_ge(m_ok, n + 1)
                        if n >= 3:
                            act.wait_ge(pt_ps, by_unit[n - 3][-1][0] + 1)
                        if w > CH:
                            src = ps[:, 2 * (n % 2):2 * (n % 2) + 2, :].rearrange("p a b -> p (a b)")[:, 0:w]
                        else:
                            src = ps[:, 2 * (n % 2), 0:w]
                        nc.scalar.activation(prob_q[n % 3][:, 0:w], src, ACT.Exp, bias=wbias[:, n:n + 1],
                                             scale=scale, accum_out=wsum[:, n:n + 1]).then_inc(p_ok, 1)

                    def take(n):
                        for g, _, b, cnt in by_unit[n]:
                            act.wait_ge(pt_ps, g + 1)
                            if g >= 8:
                                m = groups[g - 8][1]
                                act.wait_ge(o_ps, m + 1)
                            nc.scalar.copy(prob_t[:, g % 8, 0:cnt * P], ps[:, 4 + g % 2, 0:cnt * P]
                                           ).then_inc(pt_ok, 1)

                    for n in range(len(units) + 1):
                        if n < len(units):
                            exps(n)
                        if n >= 1:
                            take(n - 1)

                @block.vector
                def _(dve):
                    link = chain(dve, "dve_step")
                    link(nc.vector.tensor_scalar(bq_m[:, :], head_mask, win[:, WW_SM:WW_SM + 1], None, ALU.mult))
                    dve.wait_ge(proj, 2)
                    link(nc.vector.tensor_scalar(k_t[:, :], ps[:, 0:2, :].rearrange("p a b -> p (a b)"),
                                                 win[:, WW_SM + 1:WW_SM + 2], None, ALU.add))
                    nc.vector.tensor_copy(bq_m[:, :], bq_m[:, :]).then_inc(proj_out, 1)
                    dve.wait_ge(proj, 6)
                    bv = win[:, WW_BV:WW_BV + D].unsqueeze(1).broadcast_to([P, TPC, D])
                    for c in range(NCH):
                        nc.vector.tensor_tensor(v_n[:, TPC * c:TPC * (c + 1), :],
                                                ps[:, 4 + c, :].rearrange("p (t d) -> p t d", t=TPC), bv,
                                                ALU.add).then_inc(proj_out, 1)
                    dve.wait_ge(z_ps, 2)
                    for i in range(WH):
                        link(nc.vector.tensor_scalar(dx[:, 1 + i, :], dx[:, 0, :], float(T), float(WINDOWS[i]),
                                                     ALU.mult, ALU.add))
                    nc.vector.tensor_copy(dx[:, 0, :], dx[:, 1, :]).then_inc(dx_ok, 1)

                    def hide_keys(n):
                        t, i = units[n]
                        w = T - t * P
                        if n >= 3:
                            dve.wait_ge(s_ps, n - 2)
                        nc.vector.tensor_scalar(hide[n % 3][:, 0:w], rel[:, 0:w], dx[:, 1 + i, t:t + 1], None,
                                                ALU.is_gt).then_inc(hide_ok, 1)

                    def maxima(n):
                        t, i = units[n]
                        w = T - t * P
                        dve.wait_ge(s_ps, n + 1)
                        if w > CH:
                            src = ps[:, 2 * (n % 2):2 * (n % 2) + 2, :].rearrange("p a b -> p (a b)")[:, 0:w]
                        else:
                            src = ps[:, 2 * (n % 2), 0:w]
                        link(nc.vector.tensor_reduce(wmax[:, 0, n:n + 1], src, AX_X, ALU.max))
                        nc.vector.tensor_scalar(wbias[:, n:n + 1], wmax[:, 0, n:n + 1], -scale, None,
                                                ALU.mult).then_inc(m_ok, 1)

                    def normalise(n):
                        t, i = units[n]
                        w = T - t * P
                        dve.wait_ge(p_ok, n + 1)
                        link(nc.vector.reciprocal(wrec[:, n:n + 1], wsum[:, n:n + 1]))
                        nc.vector.tensor_scalar(prob_q[n % 3][:, 0:w], prob_q[n % 3][:, 0:w], wrec[:, n:n + 1],
                                                None, ALU.mult).then_inc(p_n, 1)

                    def add_out(t):
                        dve.wait_ge(o_ps, WH * (t + 1))
                        nc.vector.tensor_tensor(x_res[:, tile(t)], x_res[:, tile(t)], ps[:, 6 + t % 2, 0:P],
                                                ALU.add).then_inc(o_ok, 1)

                    hide_keys(0)
                    hide_keys(1)
                    for n in range(len(units) + 1):
                        if n < len(units):
                            maxima(n)
                        if n + 2 < len(units):
                            hide_keys(n + 2)
                        if n >= 1:
                            normalise(n - 1)
                        if n >= 6 and (n - 6) % WH == 0:
                            add_out((n - 6) // WH)
                    add_out(NT - 1)
            end_phase()

        def self_attention_phase(layer):
            steps = attention_steps()
            scale = HD ** -0.5
            heads = [slice(4 * g, 4 * g + 4) for g in range(QUADS)]
            max_units = [s for s in steps if s[0] in ("max", "maxT", "outT")]
            n_of = {("maxT", s[2]): s[1] for s in max_units if s[0] == "maxT"}
            last_item = {}
            for s in steps:
                if s[0] == "value" and s[5]:
                    last_item[s[2], s[3]] = s[1]
            closed = sorted(last_item.values())

            with phase() as block:
                wb_ok, proj, roped, took = sem("wb_ok"), sem("proj"), sem("roped"), sem("took")
                part1, part2, part3 = sem("part1"), sem("part2"), sem("part3")
                rest = sem("rest")
                spread = [sem(f"spread{g}") for g in range(QUADS)]
                v_ps, v_ok = sem("v_ps"), sem("v_ok")
                ring_in, ring_out = sem("ring_in"), sem("ring_out")
                max_ok = sem("max_ok")
                max_split = sem("max_split")
                max_rows = [sem(f"max_rows{g % 2}") for g in range(QUADS)]
                score_in, prob_ok, value_ok = sem("score_in"), sem("prob_ok"), sem("value_ok")
                ot_ok = sem("ot_ok")

                @block.sync
                def _(sp):
                    sp.dma_start(wb[:, :], layer_b[bass.ds(layer, 1), :, :].rearrange("a p n -> (a p) n")
                                 ).then_inc(wb_ok, 16)
                    sp.wait_ge(part1, 4)
                    for g in range(QUADS):
                        for want in range(3):
                            if g == 0 and want:
                                sp.wait_ge(part2 if want == 1 else part3, 4)
                            for s in range(SLOTS):
                                for dst, which, i in ((q_x, Q_PART[s], 0), (k_x, K_PART[s], 1)):
                                    if which == want:
                                        sp.dma_start(dst[s * HD:(s + 1) * HD, heads[g], :],
                                                     parts[32 * g:32 * g + 32, i, which, :]
                                                     ).then_inc(spread[g], 16)
                    for g in range(QUADS):
                        sp.wait_ge(max_split, g + 1)
                        for k in range(3):
                            sp.dma_start(q_x[MAX_ROW + k:MAX_ROW + k + 1, heads[g], :], max_p[:, k, :]
                                         ).then_inc(max_rows[g], 16)
                    sp.wait_ge(wb_ok, 16)

                @block.tensor
                def _(pe):
                    for c in range(NCH):
                        for i in range(4):
                            nc.tensor.matmul(ps[:, 4 * c + i, :], wa[:, WA_QK + i * D:WA_QK + (i + 1) * D],
                                             h[:, chunk(c)], start=True, stop=True).then_inc(proj, 1)
                    for c in range(NCH):
                        pe.wait_ge(took, 4)
                        for t in range(TPC):
                            mm = nc.tensor.matmul(ps[:, c, tile(t)], h[:, tile(TPC * c + t)],
                                                  wa[:, WA_V:WA_V + D], start=True, stop=True)
                        mm.then_inc(v_ps, 1)
                    pe.wait_ge(took, 8)
                    pe.wait_ge(v_ok, NCH)
                    ready = set()
                    for s in steps:
                        if s[0] in ("max", "maxT", "outT"):
                            n, g = s[1], s[2]
                            bank = n % 3
                            if n >= 3:
                                pe.wait_ge(ring_out, n - 2)
                        if s[0] == "max":
                            _, n, g, t, parts_, full = s
                            if g not in ready:
                                pe.wait_ge(spread[g], 16 * 2 * SLOTS)
                                ready.add(g)
                            for j, k0, width, col in parts_:
                                mm = nc.tensor.matmul(ps[:, bank, col:col + width],
                                                      q_x[0:MAX_ROW, 4 * g + j, tile(t)],
                                                      k_x[0:MAX_ROW, 4 * g + j, k0:k0 + width],
                                                      start=True, stop=bool(full))
                                if not full:
                                    mm = nc.tensor.matmul(ps[:, bank, col + width - P:col + width], id_b[:, :],
                                                          mask_q[:, :], start=False, stop=True)
                            mm.then_inc(ring_in, 1)
                        elif s[0] == "maxT":
                            pe.wait_ge(max_ok, g + 1)
                            nc.tensor.transpose(ps[0:32, bank, 0:P],
                                                max_q[:, :, :].rearrange("p j t -> p (j t)"), ident
                                                ).then_inc(ring_in, 1)
                        elif s[0] == "outT":
                            k = closed.index(last_item[g, s[3]])
                            pe.wait_ge(ot_ok, k + 1)
                            for t in range(TPC):
                                mm = nc.tensor.transpose(ps[:, bank, tile(t)], o_t[:, tile(t)], ident)
                            mm.then_inc(ring_in, 1)
                        elif s[0] == "score":
                            _, m, item, g, c, kb, pair = s
                            if (g, "rows") not in ready:
                                pe.wait_ge(max_rows[g], 48 * (g // 2 + 1))
                                ready.add((g, "rows"))
                            if m >= 2:
                                pe.wait_ge(prob_ok, m - 1)
                            q0 = max(c * CH, kb * P)
                            width = (c + 1) * CH - q0
                            for i in range(2):
                                j = 4 * g + 2 * pair + i
                                bank = ps[:, 3 + 2 * (m % 2) + i, 0:width]
                                diag = kb * P >= c * CH
                                mm = nc.tensor.matmul(bank, k_x[0:KROWS, j, tile(kb)],
                                                      q_x[0:KROWS, j, q0:q0 + width], start=True,
                                                      stop=not diag)
                                if diag:
                                    mm = nc.tensor.matmul(bank[:, 0:P], id_b[:, :], mask_t[:, :],
                                                          start=False, stop=True)
                            mm.then_inc(score_in, 1)
                        else:
                            _, item, g, c, kb, last = s
                            pe.wait_ge(prob_ok, 2 * item + 2)
                            if kb == 0 and item:
                                pe.wait_ge(ot_ok, closed.index(item - 1) + 1)
                            q0 = max(c * CH, kb * P)
                            width = (c + 1) * CH - q0
                            for j in range(4):
                                mm = nc.tensor.matmul(ps[32 * j:32 * j + 32, 7, q0 - c * CH:CH],
                                                      v_aug[:, kb, 4 * g + j, :],
                                                      prob[:, 2 * (item % 2) + j // 2, j % 2, 0:width],
                                                      start=(kb == 0), stop=last,
                                                      tile_position=(0, 32 * j))
                            mm.then_inc(value_ok, 1)

                @block.scalar
                def _(act):
                    for n in range(4):
                        c, i = n // 2, n % 2
                        act.wait_ge(roped, n + 1)
                        nc.scalar.copy(parts[:, i, 0, chunk(c)], qk[:, i, chunk(c)]).then_inc(part1, 1)
                        if n:
                            c, i = (n - 1) // 2, (n - 1) % 2
                            act.wait_ge(rest, n)
                            nc.scalar.copy(parts[:, i, 1, chunk(c)], qk[:, i, chunk(c)]).then_inc(part2, 1)
                    act.wait_ge(rest, 4)
                    nc.scalar.copy(parts[:, 1, 1, chunk(1)], qk[:, 1, chunk(1)]).then_inc(part2, 1)
                    for s in steps:
                        if s[0] == "score":
                            _, m, item, g, c, kb, pair = s
                            act.wait_ge(score_in, m + 1)
                            if item >= 2:
                                act.wait_ge(value_ok, item - 1)
                            width = (c + 1) * CH - max(c * CH, kb * P)
                            b = 3 + 2 * (m % 2)
                            nc.scalar.activation(prob[:, 2 * (item % 2) + pair, :, 0:width],
                                                 ps[:, b:b + 2, 0:width], ACT.Exp, scale=scale
                                                 ).then_inc(prob_ok, 1)
                        elif s[0] == "value" and s[5]:
                            k = closed.index(s[1])
                            act.wait_ge(value_ok, s[1] + 1)
                            if k:
                                g, c = divmod(k - 1, NCH)
                                n = next(x[1] for x in steps if x[0] == "outT" and x[2:4] == (g, c))
                                act.wait_ge(ring_in, n + 1)
                            nc.scalar.copy(o_t[:, :], ps[:, 7, :]).then_inc(ot_ok, 1)

                @block.gpsimd
                def _(pool_):
                    for n in range(4):
                        c, i = n // 2, n % 2
                        pool_.wait_ge(part2, n + 1)
                        nc.gpsimd.tensor_tensor(parts[:, i, 2, chunk(c)], qk[:, i, chunk(c)],
                                                parts[:, i, 1, chunk(c)], ALU.subtract).then_inc(part3, 1)

                @block.vector
                def _(dve):
                    link = chain(dve, "dve_step")

                    def rope(n):
                        c, i = n // 2, n % 2
                        dve.wait_ge(proj, 4 * c + 2 * i + 2)
                        b = wa[:, WA_SM + SM_BQ + 2 * i:WA_SM + SM_BQ + 2 * i + 1]
                        br = wa[:, WA_SM + SM_BQ + 2 * i + 1:WA_SM + SM_BQ + 2 * i + 2]
                        nc.vector.scalar_tensor_tensor(tmp[:, 0, :], ps[:, 4 * c + 2 * i, :], b,
                                                       cos_t[:, chunk(c)], ALU.add, ALU.mult
                                                       ).then_inc(took, 1)
                        nc.vector.scalar_tensor_tensor(tmp[:, 1, :], ps[:, 4 * c + 2 * i + 1, :], br,
                                                       sin_t[:, chunk(c)], ALU.add, ALU.mult
                                                       ).then_inc(took, 1)
                        dve.wait_ge(took, 2 * n + 2)
                        nc.vector.tensor_tensor(qk[:, i, chunk(c)], tmp[:, 0, :], tmp[:, 1, :],
                                                ALU.add).then_inc(roped, 1)
                        dve.wait_ge(roped, n + 1)

                    def remainder(n):
                        c, i = n // 2, n % 2
                        dve.wait_ge(part1, n + 1)
                        nc.vector.tensor_tensor(qk[:, i, chunk(c)], qk[:, i, chunk(c)],
                                                parts[:, i, 0, chunk(c)], ALU.subtract).then_inc(rest, 1)

                    for n in range(5):
                        if n < 4:
                            rope(n)
                        if n:
                            remainder(n - 1)
                    bv = wa[:, WA_BV:WA_BV + D].rearrange("p (h d) -> p h d", h=H).unsqueeze(1).broadcast_to([P, TPC, H, HD])
                    for c in range(NCH):
                        dve.wait_ge(v_ps, c + 1)
                        nc.vector.tensor_tensor(v_aug[:, TPC * c:TPC * (c + 1), :, 0:HD],
                                                ps[:, c, :].rearrange("p (t h d) -> p t h d", t=TPC, h=H), bv,
                                                ALU.add).then_inc(v_ok, 1)
                    for s in steps:
                        if s[0] in ("max", "maxT", "outT"):
                            n, g = s[1], s[2]
                            bank = n % 3
                            dve.wait_ge(ring_in, n + 1)
                        if s[0] == "max":
                            _, n, g, t, parts_, full = s
                            j0, _, width, _ = parts_[0]
                            src = ps[:, bank, 0:len(parts_) * width].rearrange("p (j k) -> p j k", k=width)
                            if g and t == 0:
                                dve.wait_ge(ring_in, n_of["maxT", g - 1] + 1)
                            dst = max_f if full else max_q
                            nc.vector.tensor_reduce(dst[:, j0:j0 + len(parts_), t], src, AX_X, ALU.max
                                                    ).then_inc(ring_out, 1)
                            if t == NT - 1 and not full and j0 + len(parts_) == 4:
                                dve.wait_ge(ring_out, n + 1)
                                nc.vector.tensor_tensor(max_q[:, :, TPC:NT], max_q[:, :, TPC:NT],
                                                        max_f[:, :, TPC:NT], ALU.max).then_inc(max_ok, 1)
                        elif s[0] == "maxT":
                            if g:
                                dve.wait_ge(max_rows[g - 1], 48 * ((g - 1) // 2 + 1))
                            src = ps[0:32, bank, 0:P]
                            link(nc.vector.tensor_scalar(max_p[:, 0, :], src, -1.0, None, ALU.mult))
                            nc.vector.scalar_tensor_tensor(max_s[:, 0, :], src, -1.0, max_p[:, 0, :],
                                                           ALU.mult, ALU.subtract).then_inc(ring_out, 1)
                            dve.wait_ge(ring_out, n + 1)
                            link(nc.vector.tensor_copy(max_p[:, 1, :], max_s[:, 0, :]))
                            nc.vector.tensor_tensor(max_p[:, 2, :], max_s[:, 0, :], max_p[:, 1, :],
                                                    ALU.subtract).then_inc(max_split, 1)
                        elif s[0] == "outT":
                            _, n, g, c = s
                            src = ps[:, bank, :].rearrange("p (t j d) -> p t j d", t=TPC, j=4)
                            link(nc.vector.reciprocal(den[:, :, :], src[:, :, :, HD]))
                            dst = o_n[:, TPC * c:TPC * (c + 1), 4 * g * HD:4 * (g + 1) * HD].rearrange(
                                "p t (j d) -> p t j d", j=4)
                            nc.vector.tensor_tensor(dst, src[:, :, :, 0:HD],
                                                    den[:, :, :].unsqueeze(3).broadcast_to([P, TPC, 4, HD]),
                                                    ALU.mult).then_inc(ring_out, 1)
                            dve.wait_ge(ring_out, n + 1)
            end_phase()

        def linear_phase(src_n, weight, bias):
            with phase() as block:
                turned, taken, made = sem("turned"), sem("taken"), sem("made")

                @block.tensor
                def _(pe):
                    for c in range(NCH):
                        for t in range(TPC):
                            mm = nc.tensor.transpose(ps[:, c, tile(t)], src_n[:, TPC * c + t, :], ident)
                        mm.then_inc(turned, 1)
                    for c in range(NCH):
                        pe.wait_ge(taken, c + 1)
                        nc.tensor.matmul(ps[:, 2 + c, :], weight, o_d[:, chunk(c)], start=True,
                                         stop=True).then_inc(made, 1)

                @block.scalar
                def _(act):
                    for c in range(NCH):
                        act.wait_ge(turned, c + 1)
                        nc.scalar.copy(o_d[:, chunk(c)], ps[:, c, :]).then_inc(taken, 1)

                @block.vector
                def _(dve):
                    for c in range(NCH):
                        dve.wait_ge(made, c + 1)
                        if bias is None:
                            nc.vector.tensor_tensor(x_dec[:, chunk(c)], x_dec[:, chunk(c)], ps[:, 2 + c, :], ALU.add)
                        else:
                            nc.vector.scalar_tensor_tensor(x_dec[:, chunk(c)], ps[:, 2 + c, :], bias,
                                                           x_dec[:, chunk(c)], ALU.add, ALU.add)
            end_phase()

        qc = qk[:, 0, :]
        k_bd = cen[:, 0:CH]
        mem_b = sb("mem_b", [P, P], BF16)
        v_bd = tmp[:, 0, :].rearrange("p (g n) -> p g n", g=QUADS)
        mem_sb = sb("mem_sb", [P, KEYS])
        cross_scale = HD ** -0.5

        def near_phase():
            mem4 = sq[:, 0:P]
            k_sb = sq[:, P:P + NEAR]
            e_q = [prob[:, i, 0, :] for i in range(3)]
            p_t = [prob[:, i, 1, :] for i in range(3)]
            mx = max_q[:, :, :].rearrange("p a b -> p (a b)")
            with phase() as block:
                mem_ok, q_ps, q_ok, kv_ps = sem("mem_ok"), sem("q_ps"), sem("q_ok"), sem("kv_ps")
                k_ok, v_okk = sem("k_ok"), sem("v_ok")
                s_ps, s_out, e_ok, n_ok = sem("s_ps"), sem("s_out"), sem("e_ok"), sem("n_ok")
                t_ps, t_ok, o_ps = sem("t_ps"), sem("t_ok"), sem("o_ps")

                @block.sync
                def _(sp):
                    for i in range(4):
                        sp.dma_start(mem4[:, NEAR * i:NEAR * (i + 1)], mem_t[0, :, 0:NEAR]).then_inc(mem_ok, 16)

                @block.tensor
                def _(pe):
                    for c in range(NCH):
                        nc.tensor.matmul(ps[:, c, :], wb[:, WB_QC:WB_QC + D], h[:, chunk(c)], start=True,
                                         stop=True).then_inc(q_ps, 1)
                    pe.wait_ge(mem_ok, 64)
                    nc.tensor.matmul(ps[:, 2, 0:NEAR], wb[:, WB_KC:WB_KC + D], mem4[:, 0:NEAR], start=True,
                                     stop=True).then_inc(kv_ps, 1)
                    nc.tensor.matmul(ps[:, 3, 0:D], mem4, wb[:, WB_VC:WB_VC + D], start=True,
                                     stop=True).then_inc(kv_ps, 1)
                    pe.wait_ge(q_ok, NCH)
                    pe.wait_ge(k_ok, 1)
                    pe.wait_ge(v_okk, 1)

                    def scores(t):
                        if t >= 2:
                            pe.wait_ge(s_out, t - 1)
                        nc.tensor.matmul(ps[:, t % 2, :], qc[:, tile(t)], k_bd[:, 0:H * NEAR], start=True,
                                         stop=False)
                        nc.tensor.matmul(ps[:, t % 2, :].rearrange("p (h k) -> p h k", h=H), id_b[:, :],
                                         mask_near[:, t, :].unsqueeze(1).broadcast_to([P, H, NEAR]),
                                         start=False, stop=True).then_inc(s_ps, 1)

                    def turn(t):
                        pe.wait_ge(n_ok, t + 1)
                        if t >= 2:
                            pe.wait_ge(t_ok, t - 1)
                        for g in range(QUADS):
                            mm = nc.tensor.transpose(ps[:, 2 + t % 2, tile(g)], e_q[t % 3][:, tile(g)], ident)
                        mm.then_inc(t_ps, 1)

                    def values(t):
                        pe.wait_ge(t_ok, t + 1)
                        for g in range(QUADS):
                            mm = nc.tensor.matmul(ps[:, 4 + t // TPC, tile(t % TPC)], v_bd[:, g, :],
                                                  p_t[t % 3][:, tile(g)], start=(g == 0), stop=(g == QUADS - 1))
                        mm.then_inc(o_ps, 1)

                    for t in range(NT + 2):
                        if t < NT:
                            scores(t)
                        if 1 <= t <= NT:
                            turn(t - 1)
                        if t >= 2:
                            values(t - 2)
                    for c in range(NCH):
                        pe.wait_ge(t_ok, NT + c + 1)
                        nc.tensor.matmul(ps[:, 6 + c, :], wb[:, WB_OC:WB_OC + D], o_d[:, chunk(c)], start=True,
                                         stop=True).then_inc(o_ps, 1)

                @block.scalar
                def _(act):
                    for c in range(NCH):
                        act.wait_ge(q_ps, c + 1)
                        nc.scalar.copy(qc[:, chunk(c)], ps[:, c, :]).then_inc(q_ok, 1)
                    act.wait_ge(kv_ps, 1)

                    def exps(t):
                        act.wait_ge(s_out, t + 1)
                        nc.scalar.activation(e_q[t % 3], e_q[t % 3], ACT.Exp, scale=cross_scale).then_inc(e_ok, 1)

                    def take(t):
                        act.wait_ge(t_ps, t + 1)
                        if t >= 3:
                            act.wait_ge(o_ps, t - 2)
                        nc.scalar.copy(p_t[t % 3], ps[:, 2 + t % 2, :]).then_inc(t_ok, 1)

                    for t in range(NT + 1):
                        if t < NT:
                            exps(t)
                        if t >= 1:
                            take(t - 1)
                    for c in range(NCH):
                        act.wait_ge(o_ps, TPC * (c + 1))
                        nc.scalar.copy(o_d[:, chunk(c)], ps[:, 4 + c, :]).then_inc(t_ok, 1)

                @block.vector
                def _(dve):
                    link = chain(dve, "dve_step")
                    dve.wait_ge(kv_ps, 2)
                    link(nc.vector.tensor_copy(k_sb, ps[:, 2, 0:NEAR]))
                    nc.vector.tensor_tensor(k_bd[:, 0:H * NEAR].rearrange("p (h k) -> p h k", h=H),
                                            k_sb.unsqueeze(1).broadcast_to([P, H, NEAR]),
                                            tab[:, R_HM16:R_HM16 + H].unsqueeze(2).broadcast_to([P, H, NEAR]),
                                            ALU.mult).then_inc(k_ok, 1)
                    nc.vector.tensor_tensor(v_bd, ps[:, 3, 0:D].unsqueeze(1).broadcast_to([P, QUADS, D]),
                                            tab[:, R_VMASK:R_VMASK + QUADS * D].rearrange("p (g n) -> p g n", g=QUADS),
                                            ALU.mult).then_inc(v_okk, 1)

                    def shift(t):
                        dve.wait_ge(s_ps, t + 1)
                        if t >= 3:
                            dve.wait_ge(t_ps, t - 2)
                        s3 = ps[:, t % 2, :].rearrange("p (h k) -> p h k", h=H)
                        m = mx[:, 16 * (t % 2):16 * (t % 2) + 16]
                        link(nc.vector.tensor_reduce(m, s3, AX_X, ALU.max))
                        nc.vector.tensor_tensor(e_q[t % 3].rearrange("p (h k) -> p h k", h=H), s3,
                                                m.unsqueeze(2).broadcast_to([P, H, NEAR]),
                                                ALU.subtract).then_inc(s_out, 1)

                    def normalise(t):
                        dve.wait_ge(e_ok, t + 1)
                        e3 = e_q[t % 3].rearrange("p (h k) -> p h k", h=H)
                        d = den[:, :, :].rearrange("p a b -> p (a b)")
                        link(nc.vector.tensor_reduce(d, e3, AX_X, ALU.add))
                        link(nc.vector.reciprocal(d, d))
                        nc.vector.tensor_tensor(e3, e3, d.unsqueeze(2).broadcast_to([P, H, NEAR]),
                                                ALU.mult).then_inc(n_ok, 1)
                        dve.wait_ge(n_ok, t + 1)

                    for t in range(NT + 1):
                        if t < NT:
                            shift(t)
                        if t >= 1:
                            normalise(t - 1)
                    for c in range(NCH):
                        dve.wait_ge(o_ps, NT + c + 1)
                        nc.vector.tensor_tensor(x_dec[:, chunk(c)], x_dec[:, chunk(c)], ps[:, 6 + c, :], ALU.add)
            end_phase()

        def feed_forward_phase(layer):
            gate = [sq[:, 0:CH], sq[:, CH:T], rs[:, 0:CH]]
            hid = prob[:, :, :, :].rearrange("p a b c -> p a (b c)")
            units = [(c, f) for c in range(NCH) for f in range(FT)]
            with phase() as block:
                wa_ok, up, silu, hid_ok, down = (sem(x) for x in ("wa_ok", "up", "silu", "hid_ok", "down"))

                @block.sync
                def _(sp):
                    sp.dma_start(wa[:, :], layer_a[bass.ds(layer + 1, 1), :, :].rearrange("a p n -> (a p) n")
                                 ).then_inc(wa_ok, 16)
                    sp.wait_ge(wa_ok, 16)

                @block.tensor
                def _(pe):
                    def ups(n):
                        c, f = units[n]
                        b = 2 * (n % 3)
                        if n >= 3:
                            pe.wait_ge(hid_ok, n - 2)
                        nc.tensor.matmul(ps[:, b, :], wb[:, WB_G + f * P:WB_G + (f + 1) * P], h[:, chunk(c)],
                                         start=True, stop=True).then_inc(up, 1)
                        nc.tensor.matmul(ps[:, b + 1, :], wb[:, WB_U + f * P:WB_U + (f + 1) * P], h[:, chunk(c)],
                                         start=True, stop=True).then_inc(up, 1)

                    def downs(n):
                        c, f = units[n]
                        pe.wait_ge(hid_ok, n + 1)
                        mm = nc.tensor.matmul(ps[:, 6 + c, :], wb[:, WB_DN + f * D:WB_DN + (f + 1) * D],
                                              hid[:, f, chunk(c)], start=(f == 0), stop=(f == FT - 1))
                        if f == FT - 1:
                            mm.then_inc(down, 1)

                    for n in range(len(units) + 2):
                        if n < len(units):
                            ups(n)
                        if n >= 2:
                            downs(n - 2)

                @block.scalar
                def _(act):
                    for n, (c, f) in enumerate(units):
                        act.wait_ge(up, 2 * n + 1)
                        if n >= 3:
                            act.wait_ge(hid_ok, n - 2)
                        nc.scalar.activation(gate[n % 3], ps[:, 2 * (n % 3), :], ACT.Silu).then_inc(silu, 1)

                @block.vector
                def _(dve):
                    for n, (c, f) in enumerate(units):
                        dve.wait_ge(silu, n + 1)
                        dve.wait_ge(up, 2 * n + 2)
                        nc.vector.tensor_tensor(hid[:, f, chunk(c)], gate[n % 3], ps[:, 2 * (n % 3) + 1, :],
                                                ALU.mult).then_inc(hid_ok, 1)
                    for c in range(NCH):
                        dve.wait_ge(down, c + 1)
                        nc.vector.tensor_tensor(x_dec[:, chunk(c)], x_dec[:, chunk(c)], ps[:, 6 + c, :], ALU.add)
            end_phase()

        def far_path():
            iota = tab[:, R_IOTA:R_IOTA + KEYS]
            k_far = prob[:, :, :, :].rearrange("p a b c -> p (a b c)")[:, 0:H * KEYS]
            v_far = o_t[:, 0:D]
            e_far = cen[:, 0:CH]
            pt_far = cen[:, CH:T]
            hide = h[:, 0:P]
            pad = h[:, P:2 * P]
            near_end = h[:, 2 * P:2 * P + NT]
            top = sq[:, 0:NT * H].rearrange("p (t h) -> p t h", t=NT)
            total = sq[:, NT * H:2 * NT * H].rearrange("p (t h) -> p t h", t=NT)
            new = sq[:, 2 * NT * H:2 * NT * H + 4]
            seg_r = sq[:, 3 * NT * H:3 * NT * H + NT]
            end_r = sq[:, 4 * NT * H:4 * NT * H + 1]
            hide_b = mem_b[:, 0:P]

            def start():
                with phase() as block:
                    q_ps = sem("q_ps")

                    @block.tensor
                    def _(pe):
                        for c in range(NCH):
                            nc.tensor.matmul(ps[:, c, :], wb[:, WB_QC:WB_QC + D], h[:, chunk(c)], start=True,
                                             stop=True).then_inc(q_ps, 1)

                    @block.scalar
                    def _(act):
                        for c in range(NCH):
                            act.wait_ge(q_ps, c + 1)
                            nc.scalar.copy(qc[:, chunk(c)], ps[:, c, :])

                    @block.vector
                    def _(dve):
                        nc.vector.memset(top, -float(2 ** 126))
                        nc.vector.memset(total, 0.0)
                        nc.vector.memset(o_n[:, :, :], 0.0)
                end_phase()

            def rewind():
                with phase() as block:
                    @block.vector
                    def _(dve):
                        nc.vector.tensor_copy(seg_r, seg_q[:, :])
                        nc.vector.memset(end_r, float(S_MEM - 1))
                end_phase()

            def block_phase(kb, sums):
                units = [(t, g) for t in range(NT) for g in range(QUADS)]
                with phase() as block:
                    mem_ok, kv_ps, kv_ok, hide_ok = (sem(x) for x in ("mem_ok", "kv_ps", "kv_ok", "hide_ok"))
                    s_ps, s_out, e_ok, t_ps, t_ok, o_ps, o_out = (
                        sem(x) for x in ("s_ps", "s_out", "e_ok", "t_ps", "t_ok", "o_ps", "o_out"))

                    @block.sync
                    def _(sp):
                        sp.dma_start(mem_sb[:, :], mem_t[bass.ds(kb, 1), :, :].rearrange("a p n -> (a p) n")
                                     ).then_inc(mem_ok, 16)

                    @block.tensor
                    def _(pe):
                        pe.wait_ge(mem_ok, 16)
                        nc.tensor.matmul(ps[:, 0, 0:KEYS], wb[:, WB_KC:WB_KC + D], mem_sb[:, :], start=True,
                                         stop=True)
                        nc.tensor.matmul(ps[:, 1, 0:D], mem_sb[:, :], wb[:, WB_VC:WB_VC + D], start=True,
                                         stop=True).then_inc(kv_ps, 1)
                        pe.wait_ge(kv_ok, 1)
                        for n, (t, g) in enumerate(units):
                            pe.wait_ge(hide_ok, t + 1)
                            if n:
                                pe.wait_ge(s_out, n)
                            nc.tensor.matmul(ps[:, 2, :], qc[:, tile(t)], k_far[:, g * CH:(g + 1) * CH],
                                             start=True, stop=False)
                            nc.tensor.matmul(ps[:, 2, :].rearrange("p (j k) -> p j k", j=4), id_b[:, :],
                                             hide_b.unsqueeze(1).broadcast_to([P, 4, KEYS]), start=False,
                                             stop=True).then_inc(s_ps, 1)
                            if not sums:
                                continue
                            pe.wait_ge(e_ok, n + 1)
                            if n:
                                pe.wait_ge(t_ok, n)
                            for j in range(4):
                                mm = nc.tensor.transpose(ps[:, 3, tile(j)], e_far[:, tile(j)], ident)
                            mm.then_inc(t_ps, 1)
                            pe.wait_ge(t_ok, n + 1)
                            if g == 0 and t:
                                pe.wait_ge(o_out, t)
                            for j in range(4):
                                col = (4 * g + j) * HD
                                mm = nc.tensor.matmul(ps[:, 4, col:col + HD], pt_far[:, tile(j)],
                                                      v_far[:, col:col + HD], start=True, stop=True)
                            mm.then_inc(o_ps, 1)

                    @block.scalar
                    def _(act):
                        if sums:
                            for n in range(len(units)):
                                act.wait_ge(s_out, n + 1)
                                nc.scalar.activation(e_far, e_far, ACT.Exp, scale=cross_scale).then_inc(e_ok, 1)
                                act.wait_ge(t_ps, n + 1)
                                if n:
                                    act.wait_ge(o_ps, n)
                                nc.scalar.copy(pt_far, ps[:, 3, :]).then_inc(t_ok, 1)

                    @block.vector
                    def _(dve):
                        link = chain(dve, "dve_step")
                        dve.wait_ge(kv_ps, 1)
                        link(nc.vector.tensor_copy(e_far[:, 0:KEYS], ps[:, 0, 0:KEYS]))
                        link(nc.vector.tensor_copy(v_far, ps[:, 1, 0:D]))
                        link(nc.vector.tensor_tensor(
                            k_far.rearrange("p (h k) -> p h k", h=H),
                            e_far[:, 0:KEYS].unsqueeze(1).broadcast_to([P, H, KEYS]),
                            tab[:, R_HM16:R_HM16 + H].unsqueeze(2).broadcast_to([P, H, KEYS]), ALU.mult))
                        nc.vector.tensor_copy(new[:, 0:1], end_r).then_inc(kv_ok, 1)
                        link(nc.vector.tensor_scalar(pad, iota, end_r, NEG_PAD / NEG, ALU.is_gt, ALU.mult))
                        link(nc.vector.tensor_scalar(near_end, seg_r, -float(LOOKBACK), None, ALU.add))
                        for n, (t, g) in enumerate(units):
                            if g == 0:
                                link(nc.vector.tensor_scalar(hide, iota, seg_r[:, t:t + 1], None, ALU.is_gt))
                                link(nc.vector.scalar_tensor_tensor(hide, iota, near_end[:, t:t + 1], hide,
                                                                    ALU.is_le, ALU.max))
                                link(nc.vector.tensor_tensor(hide, hide, pad, ALU.max))
                                if n:
                                    dve.wait_ge(s_ps, n)
                                nc.vector.tensor_scalar(hide_b, hide, NEG, None, ALU.mult).then_inc(hide_ok, 1)
                            dve.wait_ge(s_ps, n + 1)
                            s3 = ps[:, 2, :].rearrange("p (j k) -> p j k", j=4)
                            heads = slice(4 * g, 4 * g + 4)
                            if not sums:
                                link(nc.vector.tensor_reduce(new, s3, AX_X, ALU.max))
                                nc.vector.tensor_tensor(top[:, t, heads], top[:, t, heads], new,
                                                        ALU.max).then_inc(s_out, 1)
                                dve.wait_ge(s_out, n + 1)
                                continue
                            if n:
                                dve.wait_ge(t_ps, n)
                            e3 = e_far.rearrange("p (j k) -> p j k", j=4)
                            nc.vector.tensor_tensor(e3, s3, top[:, t, heads].unsqueeze(2).broadcast_to([P, 4, KEYS]),
                                                    ALU.subtract).then_inc(s_out, 1)
                            dve.wait_ge(e_ok, n + 1)
                            link(nc.vector.tensor_reduce(new, e3, AX_X, ALU.add))
                            link(nc.vector.tensor_tensor(total[:, t, heads], total[:, t, heads], new, ALU.add))
                            if g == QUADS - 1:
                                dve.wait_ge(o_ps, n + 1)
                                nc.vector.tensor_tensor(o_n[:, t, :], o_n[:, t, :], ps[:, 4, 0:D],
                                                        ALU.add).then_inc(o_out, 1)
                        nc.vector.tensor_scalar(seg_r, seg_r, -float(KEYS), None, ALU.add)
                        nc.vector.tensor_scalar(end_r, end_r, -float(KEYS), None, ALU.add)
                end_phase()

            def finish():
                with phase() as block:
                    @block.vector
                    def _(dve):
                        link = chain(dve, "dve_step")
                        link(nc.vector.reciprocal(total, total))
                        o4 = o_n[:, :, :].rearrange("p t (h d) -> p t h d", h=H)
                        nc.vector.tensor_tensor(o4, o4, total.unsqueeze(3).broadcast_to([P, NT, H, HD]), ALU.mult)
                end_phase()

            start()
            for sums in (False, True):
                rewind()
                with nc.Fori(0, MEM_BLOCKS) as kb:
                    block_phase(kb, sums)
            finish()
            linear_phase(o_n, wb[:, WB_OC:WB_OC + D], None)

        rt = sb("rt", [P, RT_COLS])
        exp_w = big[:, :].bitcast(F32).rearrange("p (e n) -> p e n", e=E)
        gate_rows = sb("gate_rows", [3 * E, T], BF16)
        gate_t = sb("gate_t", [E, T])
        pick_e = sb("pick_e", [3 * E, E * P], BF16)
        b2_sb = sb("b2_sb", [E, D])

        def add_phase():
            with phase() as block:
                @block.vector
                def _(dve):
                    nc.vector.tensor_tensor(x_res[:, :], x_res[:, :], h[:, :], ALU.add)
            end_phase()

        def route_phase():
            small = cen[:, 0:14 * NT * E].rearrange("p (n t e) -> p n t e", n=14, t=NT)
            prob_e, best, cand, one1, one2, rest, chosen, gates_s, gates_f, r1 = (small[:, i] for i in range(10))
            col = lambda i: small[:, 10, i, :]
            top, tie1, top2, tie2, norm = (col(i) for i in range(5))
            count = small[:, 11:13].rearrange("p n t e -> p (n t e)").rearrange("p (n k t) -> p n k t", n=8, k=TOPK)
            rank = sq[:, 0:TOPK * NT].rearrange("p (k t) -> p k t", k=TOPK)
            bpart = parts[:, 0, 0, 0:NT * 3 * E].rearrange("p (t a e) -> p t a e", t=NT, a=3)
            bone = [parts[:, 0, 1 + k, 0:NT * 3 * E].rearrange("p (t a e) -> p t a e", t=NT, a=3) for k in range(TOPK)]
            bgate = parts[:, 1, 0, 0:NT * 3 * E].rearrange("p (t a e) -> p t a e", t=NT, a=3)
            rows = [parts[0:3 * E, 1, 1, :], parts[0:3 * E, 1, 2, :], gate_rows[:, :]]
            junk = qk[:, 1, :]
            e_rev = tab[:, R_EREV:R_EREV + E].unsqueeze(1).broadcast_to([P, NT, E])
            tri, offd = tab[:, R_TRI:R_TRI + P], tab[:, R_OFFD:R_OFFD + P]

            def wide(x):
                return x.unsqueeze(2).broadcast_to([P, NT, E])

            with phase() as block:
                got, l_ps, l_ok, e_ok = sem("got"), sem("l_ps"), sem("l_ok"), sem("e_ok")
                parts_ok, t_ps, t_ok, r_ps, r_out = (sem(x) for x in ("parts_ok", "t_ps", "t_ok", "r_ps", "r_out"))
                g_ok, gt_ps = sem("g_ok"), sem("gt_ps")

                @block.sync
                def _(sp):
                    sp.dma_start(rt[:, :], router).then_inc(got, 16)
                    sp.dma_start(sq[0:3 * E, :], tables[0:3 * E, R_COLS:R_COLS + E * P]).then_inc(got, 16)
                    sp.dma_start(b2_sb[:, :], b2).then_inc(got, 16)
                    for e in range(E):
                        sp.dma_start(exp_w[:, e, 0:MF], w1[e]).then_inc(got, 16)
                        sp.dma_start(exp_w[:, e, MF:2 * MF], w2[e]).then_inc(got, 16)
                    sp.wait_ge(got, 16 * (3 + 2 * E))

                @block.tensor
                def _(pe):
                    pe.wait_ge(got, 16 * (3 + 2 * E))
                    for t in range(NT):
                        mm = nc.tensor.matmul(ps[:, 0, E * t:E * (t + 1)], h[:, tile(t)], rt[:, RT_W:RT_W + E],
                                              start=True, stop=True)
                    mm.then_inc(l_ps, 1)
                    pe.wait_ge(parts_ok, 1)
                    for b, src in enumerate((bpart, bone[0], bone[1])):
                        for t in range(NT):
                            mm = nc.tensor.transpose(ps[0:3 * E, 1 + b, :].bitcast(BF16)[:, tile(t)],
                                                     src[:, t, :, :].rearrange("p a e -> p (a e)"), id_b[:, :])
                        mm.then_inc(t_ps, 1)
                    pe.wait_ge(t_ok, 3)
                    n = 0
                    for k in range(TOPK):
                        for t in range(NT):
                            if n >= 2:
                                pe.wait_ge(r_out, n - 1)
                            for c in range(NCH):
                                mm = nc.tensor.matmul(ps[:, 4 + 2 * (n % 2) + c, :], rows[1 + k][:, tile(t)],
                                                      rows[0][:, chunk(c)], start=True, stop=True)
                            mm.then_inc(r_ps, 1)
                            n += 1
                    pe.wait_ge(g_ok, 1)
                    for t in range(NT):
                        mm = nc.tensor.transpose(ps[0:3 * E, 1, :].bitcast(BF16)[:, tile(t)],
                                                 bgate[:, t, :, :].rearrange("p a e -> p (a e)"), id_b[:, :])
                    mm.then_inc(gt_ps, 1)
                    for t in range(NT):
                        mm = nc.tensor.transpose(ps[0:E, 2 + t // TPC, tile(t % TPC)], gates_f[:, t, :], ident)
                    mm.then_inc(gt_ps, 1)

                @block.scalar
                def _(act):
                    act.wait_ge(l_ok, 1)
                    nc.scalar.activation(prob_e, best, ACT.Exp).then_inc(e_ok, 1)

                @block.vector
                def _(dve):
                    link = chain(dve, "dve_step")
                    v = nc.vector
                    dve.wait_ge(got, 16 * (3 + 2 * E))
                    link(v.tensor_copy(pick_e[:, :], sq[0:3 * E, :]))
                    dve.wait_ge(l_ps, 1)
                    link(v.tensor_tensor(prob_e, ps[:, 0, 0:NT * E].rearrange("p (t e) -> p t e", t=NT),
                                         rt[:, RT_B:RT_B + E].unsqueeze(1).broadcast_to([P, NT, E]), ALU.add))
                    link(v.tensor_reduce(top, prob_e, AX_X, ALU.max))
                    v.tensor_tensor(best, prob_e, wide(top), ALU.subtract).then_inc(l_ok, 1)
                    dve.wait_ge(e_ok, 1)
                    link(v.tensor_reduce(norm, prob_e, AX_X, ALU.add))
                    link(v.reciprocal(norm, norm))
                    link(v.tensor_tensor(prob_e, prob_e, wide(norm), ALU.mult))
                    for src, t_, tie, one in ((prob_e, top, tie1, one1), (rest, top2, tie2, one2)):
                        link(v.tensor_reduce(t_, src, AX_X, ALU.max))
                        link(v.tensor_tensor(best, src, wide(t_), ALU.is_equal))
                        link(v.tensor_tensor(cand, best, e_rev, ALU.mult))
                        link(v.tensor_reduce(tie, cand, AX_X, ALU.max))
                        link(v.tensor_tensor(one, e_rev, wide(tie), ALU.is_equal))
                        if src is prob_e:
                            link(v.scalar_tensor_tensor(rest, one1, -2.0, prob_e, ALU.mult, ALU.add))
                    link(v.tensor_tensor(chosen, one1, one2, ALU.add))
                    link(v.tensor_tensor(gates_s, prob_e, chosen, ALU.mult))
                    link(v.scalar_tensor_tensor(gates_s, chosen, -1.0, gates_s, ALU.add, ALU.add))

                    def split(dst, src):
                        link(v.tensor_copy(dst[:, :, 0, :], src))
                        link(v.tensor_tensor(r1, src, dst[:, :, 0, :], ALU.subtract))
                        link(v.tensor_copy(dst[:, :, 1, :], r1))
                        link(v.tensor_tensor(dst[:, :, 2, :], r1, dst[:, :, 1, :], ALU.subtract))

                    split(bpart, gates_s)
                    for k, one in enumerate((one1, one2)):
                        link(v.tensor_copy(bone[k], one.unsqueeze(2).broadcast_to([P, NT, 3, E])))
                    v.memset(count, 0.0).then_inc(parts_ok, 1)
                    for b in range(3):
                        dve.wait_ge(t_ps, b + 1)
                        v.tensor_copy(rows[b], ps[0:3 * E, 1 + b, :].bitcast(BF16)).then_inc(t_ok, 1)
                    dve.wait_ge(parts_ok, 1)
                    n = 0
                    for k, g in enumerate((top, top2)):
                        for t in range(NT):
                            dve.wait_ge(r_ps, n + 1)
                            if n:
                                dve.wait_ge(r_out, n)
                            r = ps[:, 4 + 2 * (n % 2):6 + 2 * (n % 2), :].rearrange("p a b -> p (a b)")
                            gi = g[:, t:t + 1]
                            here = r[:, tile(t)]
                            if t:
                                link(v.tensor_scalar(junk[:, 0:t * P], r[:, 0:t * P], gi, 0.0, ALU.is_ge, ALU.add,
                                                     accum_out=count[:, 0, k, t:t + 1]))
                            if t < NT - 1:
                                link(v.tensor_scalar(junk[:, 0:T - (t + 1) * P], r[:, (t + 1) * P:T], gi, 0.0,
                                                     ALU.is_gt, ALU.add, accum_out=count[:, 1, k, t:t + 1]))
                            link(v.scalar_tensor_tensor(junk[:, 0:P], here, gi, offd, ALU.is_gt, ALU.mult,
                                                        accum_out=count[:, 2, k, t:t + 1]))
                            v.scalar_tensor_tensor(junk[:, P:2 * P], here, gi, tri, ALU.is_equal, ALU.mult,
                                                   accum_out=count[:, 3, k, t:t + 1]).then_inc(r_out, 1)
                            n += 1
                    dve.wait_ge(r_out, n)
                    link(v.tensor_tensor(rank, count[:, 0], count[:, 1], ALU.add))
                    link(v.tensor_tensor(rank, rank, count[:, 2], ALU.add))
                    link(v.tensor_tensor(rank, rank, count[:, 3], ALU.add))
                    link(v.tensor_scalar(rank, rank, float(CAP), None, ALU.is_lt))
                    link(v.tensor_tensor(tie1, top, rank[:, 0], ALU.mult))
                    link(v.tensor_tensor(tie2, top2, rank[:, 1], ALU.mult))
                    link(v.tensor_tensor(cand, one1, wide(tie1), ALU.mult))
                    link(v.tensor_tensor(best, one2, wide(tie2), ALU.mult))
                    link(v.tensor_tensor(gates_f, cand, best, ALU.add))
                    split(bgate, gates_f)
                    v.tensor_copy(norm, norm).then_inc(g_ok, 1)
                    dve.wait_ge(gt_ps, 1)
                    v.tensor_copy(gate_rows[:, :], ps[0:3 * E, 1, :].bitcast(BF16))
                    dve.wait_ge(gt_ps, 2)
                    for c in range(NCH):
                        v.tensor_copy(gate_t[:, chunk(c)], ps[0:E, 2 + c, :])
            end_phase()

        def experts_phase():
            units = [(c, e, f) for c in range(NCH) for e in range(E) for f in range(MT)]
            act_h = [prob[:, i, 0, :] for i in range(3)]
            gated = [prob[:, i, 1, :] for i in range(3)]
            with phase() as block:
                up, gate_ps, gate_used, silu, hid_ok, down, done, stored = (
                    sem(x) for x in ("up", "gate_ps", "gate_used", "silu", "hid_ok", "down", "done", "stored"))

                @block.sync
                def _(sp):
                    for c in range(NCH):
                        sp.wait_ge(done, c + 1)
                        sp.dma_start(out[:, chunk(c)], x_res[:, chunk(c)]).then_inc(stored, 16)
                    sp.wait_ge(stored, 16 * NCH)

                @block.tensor
                def _(pe):
                    def ups(n):
                        c, e, f = units[n]
                        m = n // MT
                        if f == 0:
                            if m >= 2:
                                pe.wait_ge(hid_ok, MT * (m - 1))
                            nc.tensor.matmul(ps[:, 3 + m % 2, :], pick_e[:, e * P:(e + 1) * P],
                                             gate_rows[:, chunk(c)], start=True, stop=True).then_inc(gate_ps, 1)
                        if n >= 3:
                            pe.wait_ge(silu, n - 2)
                        nc.tensor.matmul(ps[:, n % 3, :], exp_w[:, e, f * P:(f + 1) * P], h[:, chunk(c)],
                                         start=True, stop=True).then_inc(up, 1)

                    def downs(n):
                        c, e, f = units[n]
                        if e == 0 and f == 0:
                            nc.tensor.matmul(ps[:, 6 + c, :], b2_sb[:, :], gate_t[:, chunk(c)], start=True,
                                             stop=False)
                        pe.wait_ge(hid_ok, n + 1)
                        mm = nc.tensor.matmul(ps[:, 6 + c, :], exp_w[:, e, MF + f * D:MF + (f + 1) * D],
                                              gated[n % 3], start=False, stop=(e == E - 1 and f == MT - 1))
                        mm.then_inc(down, 1)

                    for n in range(len(units) + 2):
                        if n < len(units):
                            ups(n)
                        if n >= 2:
                            downs(n - 2)

                @block.scalar
                def _(act):
                    for n, (c, e, f) in enumerate(units):
                        act.wait_ge(up, n + 1)
                        if n >= 3:
                            act.wait_ge(hid_ok, n - 2)
                        col = RT_B1 + e * MT + f
                        nc.scalar.activation(act_h[n % 3], ps[:, n % 3, :], ACT.Silu, bias=rt[:, col:col + 1]
                                             ).then_inc(silu, 1)

                @block.vector
                def _(dve):
                    for n, (c, e, f) in enumerate(units):
                        dve.wait_ge(silu, n + 1)
                        dve.wait_ge(gate_ps, n // MT + 1)
                        if n >= 3:
                            dve.wait_ge(down, n - 2)
                        nc.vector.tensor_tensor(gated[n % 3], act_h[n % 3], ps[:, 3 + (n // MT) % 2, :],
                                                ALU.mult).then_inc(hid_ok, 1)
                        if e == E - 1 and f == MT - 1:
                            dve.wait_ge(down, n + 1)
                            nc.vector.tensor_tensor(x_res[:, chunk(c)], x_res[:, chunk(c)], ps[:, 6 + c, :],
                                                    ALU.add).then_inc(done, 1)
            end_phase()

        def rows_phase():
            with phase() as block:
                @block.vector
                def _(dve):
                    nc.vector.memset(q_x[32:64, :, :], 0.0)
                    nc.vector.memset(q_x[64:96, :, :], 0.0)

                @block.gpsimd
                def _(pool_):
                    nc.gpsimd.memset(k_x[32:64, :, :], 0.0)
                    nc.gpsimd.memset(k_x[64:96, :, :], 1.0)
            end_phase()

        win = wb[:, 0:WW_COLS]
        load_phase(win)
        norm_phase(x_res, h, True, eps5)
        window_phase(win)
        norm_phase(x_res, x_dec, True, eps5)
        rows_phase()
        far = nc.values_load(flag_i[0:1, 0:1], min_val=0, max_val=1)
        with nc.Fori(0, LAYERS) as layer:
            norm_phase(x_dec, h, False, eps6, wa[:, WA_SM + SM_N1:WA_SM + SM_N1 + 1])
            self_attention_phase(layer)
            linear_phase(o_n, wb[:, WB_O:WB_O + D], wb[:, WB_SM + SM_BO:WB_SM + SM_BO + 1])
            norm_phase(x_dec, h, False, eps6, wb[:, WB_SM + SM_N2:WB_SM + SM_N2 + 1])
            with nc.If(far < 1):
                nc.gpsimd.nop()
                near_phase()
            with nc.Else():
                nc.gpsimd.nop()
                far_path()
            norm_phase(x_dec, h, False, eps6, wb[:, WB_SM + SM_N3:WB_SM + SM_N3 + 1])
            feed_forward_phase(layer)
        norm_phase(x_dec, h, False, eps6, nf_col[:, 0:1])
        add_phase()
        norm_phase(x_res, h, True, eps5)
        route_phase()
        experts_phase()


def constants():
    con = np.zeros((P, C_COLS), np.float32)
    i = np.arange(P)
    con[:, C_ID:C_ID + P] = np.eye(P)
    con[:, C_MEAN:C_MEAN + P] = 1.0 / D
    con[:, C_MASKT:C_MASKT + P] = np.where(i[:, None] > i[None, :], NEG, 0.0)
    con[:, C_MASKQ:C_MASKQ + P] = np.where(i[None, :] > i[:, None], NEG, 0.0)
    con[:, C_NEGI:C_NEGI + P] = np.eye(P) * WIN_NEG
    for w in range(WH):
        con[w * WD:(w + 1) * WD, C_HM + w] = 1.0
    ahead = np.arange(T)[None, :] - i[:, None]
    con[:, C_REL:C_REL + T] = np.where(ahead < 0, 1e9, ahead)
    con[:, C_EPS5], con[:, C_EPS6], con[:, C_ONE] = 1e-5, 1e-6, 1.0

    tab = np.zeros((P, R_COLS + E * P), np.float32)
    f = (i // 4) % HD
    inv = (1.0 / np.float32(10000.0) ** (np.arange(0, HD, 2, dtype=np.float32) / np.float32(HD))).astype(np.float32)
    angle = (np.arange(T, dtype=np.float32)[None, :] * inv[f % (HD // 2)][:, None]).astype(np.float32)
    tab[:, R_COS:R_COS + T] = np.cos(angle)
    tab[:, R_SIN:R_SIN + T] = np.sin(angle) * np.where(f < HD // 2, -1.0, 1.0)[:, None]
    for hh in range(H):
        tab[hh * HD:(hh + 1) * HD, R_HM16 + hh] = 1.0
    for g in range(QUADS):
        for j in range(4):
            c0 = R_VMASK + g * D + (4 * g + j) * HD
            tab[NEAR * j:NEAR * (j + 1), c0:c0 + HD] = 1.0
    tab[:, R_IOTA:R_IOTA + P] = i[None, :]
    tab[:, R_TRI:R_TRI + P] = i[None, :] < i[:, None]
    tab[:, R_OFFD:R_OFFD + P] = i[None, :] != i[:, None]
    tab[:, R_EREV:R_EREV + E] = E - np.arange(E)
    for e in range(E):
        for a in range(3):
            tab[a * E + e, R_COLS + e * P:R_COLS + (e + 1) * P] = 1.0
    return con, tab


def layout(v):
    a = {k: np.asarray(x) for k, x in v.items()}
    con, tab = constants()
    col = lambda x: np.asarray(x).reshape(-1, 1)
    wide = lambda x: np.broadcast_to(np.asarray(x).reshape(1, -1), (P, np.size(x)))

    win = np.zeros((P, WW_COLS), np.float32)
    wt, wbias = a["L0_attn_qkv_w"].T, a["L0_attn_qkv_b"]
    win[:, 0:3 * D] = wt
    win[:, WW_BV:WW_BV + D] = wide(wbias[2 * D:])
    win[:, WW_OFF:WW_OFF + WD] = a["L0_attn_off_w"].T
    win[:, WW_SM], win[:, WW_SM + 1] = wbias[0:D], wbias[D:2 * D]
    win[0:WD, WW_SM + 2] = a["L0_attn_lin2_w"][0]
    win[:, WW_SM + 3] = a["L0_attn_lin2_b"][0]

    g, f, j = np.meshgrid(np.arange(QUADS), np.arange(HD), np.arange(4), indexing="ij")
    order = ((4 * g + j) * HD + f).ravel()
    swapped = ((4 * g + j) * HD + (f + HD // 2) % HD).ravel()
    la = np.zeros((LAYERS + 1, P, WA_COLS), np.float32)
    lb = np.zeros((LAYERS, P, WB_COLS), np.float32)
    for n in range(LAYERS):
        w, b = a["L0_xattn_Wqkv"][n], a["L0_xattn_bqkv"][n]
        la[n] = np.concatenate(
            [w[order].T, w[swapped].T, w[D + order].T, w[D + swapped].T, w[2 * D:].T, wide(b[2 * D:]),
             col(a["L0_xattn_n1"][n]), col(b[order]), col(b[swapped]), col(b[D + order]), col(b[D + swapped])], 1)
        kv = a["L0_xattn_Wkv_c"][n]
        down = a["L0_xattn_Wd"][n].T.reshape(FT, P, D).transpose(1, 0, 2).reshape(P, FT * D)
        lb[n] = np.concatenate(
            [a["L0_xattn_Wo"][n].T, a["L0_xattn_Wq_c"][n].T, kv[:D].T, kv[D:].T, a["L0_xattn_Wo_c"][n].T,
             col(a["L0_xattn_bo"][n]), col(a["L0_xattn_n2"][n]), col(a["L0_xattn_n3"][n]),
             a["L0_xattn_Wg"][n].T, a["L0_xattn_Wu"][n].T, down], 1)
    mem = np.zeros((P, MEM_BLOCKS * KEYS), np.float32)
    mem[:, :S_MEM] = a["ctx_1024"][0].T
    router = np.concatenate([a["L0_ffn_Wr"], wide(a["L0_ffn_br"]),
                             a["L0_ffn_b1"].reshape(E * MT, P).T], 1)
    seg = a["itok_BxS_0_255"][0]
    return {
        "x_t": a["x"][0].T, "seg_row": seg[None, :], "seg_col": seg.reshape(NT, P).T,
        "consts": con, "tables": tab, "win_w": win,
        "mem_t": mem.reshape(P, MEM_BLOCKS, KEYS).transpose(1, 0, 2),
        "layer_a": la, "layer_b": lb, "router": router, "w1": a["L0_ffn_W1"],
        "w2": a["L0_ffn_W2"].reshape(E, MT, P, D).transpose(0, 2, 1, 3).reshape(E, P, MT * D),
        "b2": a["L0_ffn_b2"], "nf": col(a["L0_xattn_nf"]),
    }


def kernel(**inputs):
    import concourse.bacc as _bacc
    from concourse.bass_utils import run_bass_kernel_spmd as _run

    nc = _bacc.Bacc("TRN2", target_bir_lowering=False, num_devices=1)
    arrays, args = {}, {}
    for name, a in layout(inputs).items():
        a = np.ascontiguousarray(a)
        arrays[f"in_{name}_dram"] = a
        args[name] = nc.dram_tensor(f"in_{name}_dram", a.shape, mybir.dt.from_np(a.dtype), kind="ExternalInput").ap()
    out = nc.dram_tensor("out_dram", (P, T), F32, kind="ExternalOutput").ap()
    build(nc, out=out, **args)
    r = _run(nc, [arrays], core_ids=[0])
    return np.ascontiguousarray(r.results[0]["out_dram"].T)[None]
```

```python
from contextlib import ExitStack

import numpy as np

import concourse.bass as bass
from concourse import mybir

ALU = mybir.AluOpType
ACT = mybir.ActivationFunctionType
F32 = mybir.dt.float32
BF16 = mybir.dt.bfloat16
I32 = mybir.dt.int32
AX_X = mybir.AxisListType.X

P = 128
T = 1024
D = 128
NT = T // P
CH = 512
NCH = T // CH
TPC = CH // P
WINDOWS = (4, 16, 64, 32)
WH = len(WINDOWS)
WD = D // WH
LAYERS = 4
H = 16
HD = D // H
QUADS = H // 4
S_MEM = 6404
KEYS = P
MEM_BLOCKS = -(-S_MEM // KEYS)
NEAR = 32
LOOKBACK = 128
F = 512
FT = F // P
NEG = -float(2 ** 100)
NEG_PAD = -float(2 ** 120)
WIN_NEG = -float(2 ** 60)
E = 8
TOPK = 2
CAP = 154
MF = 512
MT = MF // P

Q_PART = (0, 1, 2, 0, 1, 0)
K_PART = (0, 0, 0, 1, 1, 2)
SLOTS = len(Q_PART)
ZERO_ROWS = 24
MAX_ROW = SLOTS * HD + ZERO_ROWS
KROWS = MAX_ROW + 3

C_ID, C_MEAN, C_MASKT, C_MASKQ, C_NEGI, C_HM, C_REL = 0, 128, 256, 384, 512, 640, 644
C_EPS5, C_EPS6, C_ONE = 644 + T, 645 + T, 646 + T
C_COLS = 647 + T
R_COS, R_SIN, R_HM16, R_VMASK, R_IOTA, R_TRI, R_OFFD = 0, T, 2 * T, 2 * T + 16, 2 * T + 16 + D * QUADS, 2 * T + 144 + D * QUADS, 2 * T + 272 + D * QUADS
R_EREV = 2 * T + 400 + D * QUADS
R_COLS = R_EREV + E
WA_QK, WA_V, WA_BV, WA_SM = 0, 4 * D, 5 * D, 6 * D
SM_N1, SM_BQ, SM_BQR, SM_BK, SM_BKR = 0, 1, 2, 3, 4
WA_COLS = 6 * D + 5
WB_O, WB_QC, WB_KC, WB_VC, WB_OC, WB_SM = 0, D, 2 * D, 3 * D, 4 * D, 5 * D
SM_BO, SM_N2, SM_N3 = 0, 1, 2
WB_G, WB_U, WB_DN = 5 * D + 3, 5 * D + 3 + F, 5 * D + 3 + 2 * F
WB_COLS = 5 * D + 3 + 3 * F
WW_Q, WW_K, WW_V, WW_BV, WW_OFF, WW_SM = 0, D, 2 * D, 3 * D, 4 * D, 4 * D + WD
WW_COLS = 4 * D + WD + 4
RT_W, RT_B, RT_B1 = 0, E, 2 * E
RT_COLS = 2 * E + E * MT


UNITS = [(g, c) for g in range(QUADS - 1) for c in range(NCH)] + [(QUADS - 1, 1), (QUADS - 1, 0)]


def attention_steps():
    maxima = []
    for u, (g, c) in enumerate(UNITS):
        mine = []
        for t in range(TPC * c, TPC * (c + 1)):
            if c:
                mine += [("max", u, t, ((j, 0, CH, 0),), 1, 0.22) for j in range(4)]
            first = c * CH
            width = P * (t % TPC + 1)
            per = CH // width
            for j0 in range(0, 4, per):
                mine.append(("max", u, t, tuple((j0 + i, first, width, i * width) for i in range(per)), 0,
                             0.055 * per + width * per * 0.215 / CH))
        if u:
            mine.insert(1, ("maxT", u - 1))
        maxima += mine
    maxima.append(("maxT", len(UNITS) - 1))
    products = []
    item = 0
    pend = None
    for u, (g, c) in enumerate(UNITS):
        blocks = TPC * (c + 1)
        for kb in range(blocks):
            share = ((c + 1) * CH - max(c * CH, kb * P)) / CH
            products += [("score", 2 * item + pair, item, u, kb, pair, share) for pair in range(2)]
            if pend:
                products.append(pend)
            pend = ("value", item, u, kb, kb == blocks - 1, share)
            item += 1
    products.append(pend)

    pe = dve = act = 0.0
    ring, probs = [], []
    rows, outs = {}, []
    steps = []
    while maxima or products or outs:
        free = ring[-3] if len(ring) >= 3 else 0.0
        options = []
        if outs:
            options.append((max(pe, free, outs[0][0]), 0, "out"))
        if maxima:
            ready = max(pe, free, dve + 0.3 if maxima[0][0] == "maxT" else 0.0)
            options.append((ready, 1, "max"))
        if products:
            q = products[0]
            if q[0] == "score":
                if q[3] in rows:
                    options.append((max(pe, rows[q[3]], probs[-2] if len(probs) >= 2 else 0.0), 2, "product"))
            else:
                options.append((max(pe, probs[2 * q[1] + 1]), 2, "product"))
        start, _, kind = min(options)
        n = len(ring)
        if kind == "out":
            _, u = outs.pop(0)
            steps.append(("outT", n, u))
            pe = start + 0.45
            dve = max(dve, pe + 0.2) + 1.1
            ring.append(dve)
        elif kind == "max" and maxima[0][0] == "max":
            _, u, t, parts, full, cost = maxima.pop(0)
            steps.append(("max", n, u, t, parts, full))
            pe = start + cost
            dve = max(dve, pe + 0.2) + 0.61
            ring.append(dve)
        elif kind == "max":
            _, u = maxima.pop(0)
            steps.append(("maxT", n, u))
            pe = start + 0.1
            dve = max(dve, pe + 0.2) + 0.7
            ring.append(dve)
            rows[u] = dve + 4.5
        elif products[0][0] == "score":
            *step, share = products.pop(0)
            steps.append(tuple(step))
            pe = start + 0.45 * share + (0.1 if share < 1 else 0.0)
            act = max(act, pe + 0.2) + 0.9 * share + 0.05
            probs.append(act + 0.1)
        else:
            *step, share = products.pop(0)
            steps.append(tuple(step))
            pe = start + 0.87 * share + 0.05
            if step[4]:
                act = max(act, pe + 0.2) + 0.6
                outs.append((act + 0.1, step[2]))
    return steps


def build(nc, x_t, seg_row, seg_col, consts, tables, win_w, mem_t, layer_a, layer_b, router, w1, w2,
          b2, nf, fill, out):
    ctx = ExitStack()

    def sb(name, shape, dt=F32):
        return ctx.enter_context(nc.sbuf_tensor(name, shape, dt))

    with ctx:
        ps = ctx.enter_context(nc.psum_tensor("ps", [P, 8, CH], F32))
        con = sb("con", [P, C_COLS])
        tab = sb("tab", [P, R_COLS])
        id_b = sb("id_b", [P, P], BF16)
        mask_t = sb("mask_t", [P, P], BF16)
        mask_q = sb("mask_q", [P, P], BF16)
        neg_i = sb("neg_i", [P, P], BF16)
        ident, mean_w = con[:, C_ID:C_ID + P], con[:, C_MEAN:C_MEAN + P]
        head_mask = con[:, C_HM:C_HM + WH]
        rel = con[:, C_REL:C_REL + T]
        eps5, eps6 = con[:, C_EPS5:C_EPS5 + 1], con[:, C_EPS6:C_EPS6 + 1]
        cos_t, sin_t = tab[:, R_COS:R_COS + T], tab[:, R_SIN:R_SIN + T]
        wa = sb("wa", [P, WA_COLS])
        wb = sb("wb", [P, WB_COLS])
        nf_col = sb("nf_col", [P, 1])
        x_res = sb("x_res", [P, T])
        x_dec = sb("x_dec", [P, T])
        h = sb("h", [P, T])
        cen = sb("cen", [P, T])
        sq = sb("sq", [P, T])
        rs = sb("rs", [P, T])
        big = sb("big", [P, 32 * T], BF16)
        q_x = big[:, 0:16 * T].rearrange("p (c h t) -> p c h t", c=NCH, h=H)
        k_x = big[:, 16 * T:32 * T].rearrange("p (c h t) -> p c h t", c=NCH, h=H)
        parts = sb("parts", [P, 2, 3, T], BF16)
        qk = sb("qk", [P, 2, T])
        tmp = sb("tmp", [P, 2, CH])
        v_aug = sb("v_aug", [P, NT, H, 32])
        prob = sb("prob", [P, 4, 2, CH])
        o_t = sb("o_t", [P, CH])
        o_n = sb("o_n", [P, NT, D])
        o_d = sb("o_d", [P, T])
        max_q = sb("max_q", [P, 2, 4, TPC])
        max_f = sb("max_f", [P, 2, 4, TPC])
        max_s = sb("max_s", [4 * TPC, P])
        max_p = sb("max_p", [4 * TPC, 2, 3, P], BF16)
        den = sb("den", [P, 4, 4])
        seg_q = sb("seg_q", [P, NT])
        mask_near = sb("mask_near", [P, NT, NEAR], BF16)
        flag = sb("flag", [1, 8])
        flag_i = sb("flag_i", [1, 1], I32)

        names = {}

        def sem(name):
            if name not in names:
                names[name] = pool[len(names)]
            return names[name]

        pool = [ctx.enter_context(nc.semaphore(f"phase_sem{i}")) for i in range(44)]
        first_sem, last_sem = pool[0].num, pool[-1].num
        loaded = ctx.enter_context(nc.semaphore("loaded"))
        experts_got = ctx.enter_context(nc.semaphore("experts_got"))
        seg_i = tmp[:, 0, 0:NT].bitcast(I32)
        seg_r = qk[0:1, 0, :].bitcast(I32)
        seg_f = qk[0:1, 1, :]

        def phase():
            names.clear()
            return nc.Block(no_gpsimd_drain=True)

        def end_phase():
            nc.all_engine_barrier(sems_to_clear=range(first_sem, last_sem + 1))

        def chain(eng, name):
            s, n = sem(name), [0]

            def link(ins):
                n[0] += 1
                ins.then_inc(s, 1)
                eng.wait_ge(s, n[0])
            return link

        def chunk(c):
            return slice(c * CH, (c + 1) * CH)

        def tile(t):
            return slice(t * P, (t + 1) * P)

        def norm(tag, src, dst, layer, eps, weight=None, made=None, order=range(NCH)):
            centred, squared, mean_ps, var_ps = (
                sem(tag + x) for x in ("_centred", "_squared", "_mean_ps", "_var_ps"))
            logged, root, ready = (sem(tag + x) for x in ("_logged", "_root", "_ready"))
            x = cen if layer else src

            def on_pe(pe):
                if layer:
                    for i, c in enumerate(order):
                        if made is not None:
                            pe.wait_ge(made, i + 1)
                        nc.tensor.matmul(ps[:, 4 + c, :], mean_w, src[:, chunk(c)], start=True,
                                         stop=True).then_inc(mean_ps, 1)
                for i, c in enumerate(order):
                    pe.wait_ge(squared, i + 1)
                    nc.tensor.matmul(ps[:, 6 + c, :], mean_w, sq[:, chunk(c)], start=True,
                                     stop=True).then_inc(var_ps, 1)

            def on_act(act):
                for i, c in enumerate(order):
                    if layer:
                        act.wait_ge(centred, i + 1)
                    elif made is not None:
                        act.wait_ge(made, i + 1)
                    nc.scalar.activation(sq[:, chunk(c)], x[:, chunk(c)], ACT.Square).then_inc(squared, 1)
                for i, c in enumerate(order):
                    act.wait_ge(var_ps, i + 1)
                    nc.scalar.activation(rs[:, chunk(c)], ps[:, 6 + c, :], ACT.Ln,
                                         bias=eps).then_inc(logged, 1)
                for i, c in enumerate(order):
                    act.wait_ge(logged, i + 1)
                    nc.scalar.activation(rs[:, chunk(c)], rs[:, chunk(c)], ACT.Exp,
                                         scale=-0.5).then_inc(root, 1)

            def on_dve(dve):
                if layer:
                    for i, c in enumerate(order):
                        dve.wait_ge(mean_ps, i + 1)
                        nc.vector.tensor_tensor(cen[:, chunk(c)], src[:, chunk(c)], ps[:, 4 + c, :],
                                                ALU.subtract).then_inc(centred, 1)
                    dve.wait_ge(centred, NCH)
                for i, c in enumerate(order):
                    dve.wait_ge(root, i + 1)
                    if weight is None:
                        nc.vector.tensor_tensor(dst[:, chunk(c)], x[:, chunk(c)], rs[:, chunk(c)],
                                                ALU.mult).then_inc(ready, 1)
                    else:
                        nc.vector.scalar_tensor_tensor(dst[:, chunk(c)], x[:, chunk(c)], weight,
                                                       rs[:, chunk(c)], ALU.mult, ALU.mult).then_inc(ready, 1)
            return (on_pe, on_act, on_dve, ready) if dst is not None else (on_pe, on_act, root)

        def load_phase(win):
            with phase() as block:
                got, cast = sem("got"), sem("cast")

                @block.sync
                def _(sp):
                    sp.dma_start(x_res[:, :], x_t).then_inc(got, 16)
                    sp.dma_start(con[:, :], consts).then_inc(got, 16)
                    sp.dma_start(win[:, :], win_w).then_inc(loaded, 16)
                    sp.dma_start(seg_i, seg_col).then_inc(loaded, 16)
                    sp.dma_start(seg_r, seg_row).then_inc(loaded, 16)
                    sp.dma_start(tab[:, :], tables[:, 0:R_COLS]).then_inc(loaded, 16)
                    sp.dma_start(nf_col[:, :], nf).then_inc(loaded, 16)
                    sp.dma_start(wa[:, :], layer_a[0]).then_inc(loaded, 16)
                    for i in range(4):
                        sp.dma_start(mem4[:, NEAR * i:NEAR * (i + 1)], mem_t[0, :, 0:NEAR]).then_inc(loaded, 16)
                    sp.wait_ge(got, 16 * 2)

                @block.gpsimd
                def _(pool_):
                    nc.gpsimd.memset(v_aug[:, :, :, :], 0.0).then_inc(cast, 1)
                    pool_.wait_ge(cast, 1)
                    nc.gpsimd.memset(v_aug[:, :, :, HD:HD + 1], 1.0)

                @block.vector
                def _(dve):
                    dve.wait_ge(got, 16 * 2)
                    nc.vector.tensor_copy(id_b[:, :], ident)
                    nc.vector.tensor_copy(mask_t[:, :], con[:, C_MASKT:C_MASKT + P])
                    nc.vector.tensor_copy(mask_q[:, :], con[:, C_MASKQ:C_MASKQ + P])
                    nc.vector.tensor_copy(neg_i[:, :], con[:, C_NEGI:C_NEGI + P])
            end_phase()

        def segments(v, link):
            v.wait_ge(loaded, 16 * 10)
            link(nc.vector.tensor_copy(seg_q[:, :], seg_i))
            for t in range(NT):
                nc.vector.tensor_scalar(mask_near[:, t, :], tab[:, R_IOTA:R_IOTA + NEAR],
                                        seg_q[:, t:t + 1], NEG, ALU.is_gt, ALU.mult)
            link(nc.vector.tensor_copy(seg_f, seg_r))
            link(nc.vector.tensor_reduce(flag[:, 0:1], seg_f, AX_X, ALU.max))
            link(nc.vector.tensor_reduce(flag[:, 1:2], seg_f, AX_X, ALU.min))
            link(nc.vector.tensor_scalar(flag[:, 2:3], flag[:, 0:1], float(NEAR - 1), None, ALU.is_gt))
            link(nc.vector.tensor_scalar(flag[:, 3:4], flag[:, 1:2], 0.0, None, ALU.is_lt))
            link(nc.vector.tensor_tensor(flag[:, 4:5], flag[:, 2:3], flag[:, 3:4], ALU.max))
            nc.vector.tensor_copy(flag_i[:, :], flag[:, 4:5])

        def window_phase(win):
            q_m = [big[:, 2 * T * i:2 * T * (i + 1)].bitcast(F32) for i in range(WH)]
            k_t = big[:, 8 * T:10 * T].bitcast(F32)
            v_n = big[:, 10 * T:12 * T].bitcast(F32).rearrange("p (t d) -> p t d", t=NT)
            relu = big[:, 12 * T:14 * T].bitcast(F32)
            prob_q = [big[:, 14 * T + 2 * T * i:16 * T + 2 * T * i].bitcast(F32) for i in range(3)]
            hide = [big[:, (20 + i) * T:(21 + i) * T] for i in range(3)]
            off = big[0:WD, 24 * T:26 * T].bitcast(F32)
            prob_t = prob[:, :, :, :].rearrange("p a b c -> p (a b) c")
            dx = sb("dx", [P, 1 + WH, NT])
            bq_m = sb("bq_m", [P, WH])
            wmax = sb("wmax", [P, 2, WH * NT])
            wbias = sb("wbias", [P, WH * NT])
            wsum = sb("wsum", [P, WH * NT])
            wrec = sb("wrec", [P, WH * NT])
            scale = 2.0 / float(np.sqrt(T))
            units = [(t, i) for t in range(NT) for i in range(WH)]

            with phase() as block:
                proj, proj_out = sem("proj"), sem("proj_out")
                relu_ok, off_ps, off_ok, z_ps, dx_ok = (sem(x) for x in ("relu_ok", "off_ps", "off_ok", "z_ps", "dx_ok"))
                norm_pe, norm_act, norm_dve, h_ok = norm("norm", x_res, h, True, eps5)
                hide_ok, s_ps, p_ok, p_n = sem("hide_ok"), sem("s_ps"), sem("p_ok"), sem("p_n")
                m_ok, pt_ps, pt_ok, o_ps, o_ok = (sem(x) for x in ("m_ok", "pt_ps", "pt_ok", "o_ps", "o_ok"))

                groups = []
                for n, (t, i) in enumerate(units):
                    w = NT - t
                    for b in range(0, w, 4):
                        groups.append((len(groups), n, b, min(4, w - b)))
                by_unit = {n: [g for g in groups if g[1] == n] for n in range(len(units))}

                @block.tensor
                def _(pe):
                    norm_pe(pe)
                    pe.wait_ge(h_ok, NCH)
                    pe.wait_ge(loaded, 16 * 10)
                    for j, col in enumerate((WW_K, WW_Q)):
                        for c in range(NCH):
                            nc.tensor.matmul(ps[:, 2 * j + c, :], win[:, col:col + D], h[:, chunk(c)],
                                             start=True, stop=True).then_inc(proj, 1)
                    for c in range(NCH):
                        for t in range(TPC):
                            mm = nc.tensor.matmul(ps[:, 4 + c, tile(t)], h[:, tile(TPC * c + t)],
                                                  win[:, WW_V:WW_V + D], start=True, stop=True)
                        mm.then_inc(proj, 1)
                    for c in range(NCH):
                        pe.wait_ge(relu_ok, c + 1)
                        nc.tensor.matmul(ps[0:WD, 6 + c, :], win[:, WW_OFF:WW_OFF + WD], relu[:, chunk(c)],
                                         start=True, stop=True).then_inc(off_ps, 1)
                    pe.wait_ge(off_ok, NCH)
                    for t in range(NT):
                        mm = nc.tensor.matmul(ps[:, 6, t:t + 1], off[:, tile(t)],
                                              win[0:WD, WW_SM + 2:WW_SM + 3], start=True, stop=True)
                    mm.then_inc(z_ps, 1)

                    def scores(n):
                        t, i = units[n]
                        if n >= 2:
                            pe.wait_ge(p_ok, n - 1)
                        pe.wait_ge(hide_ok, n + 1)
                        w = T - t * P
                        for b in range(0, w, CH):
                            nn = min(CH, w - b)
                            bank = ps[:, 2 * (n % 2) + b // CH, 0:nn]
                            nc.tensor.matmul(bank, q_m[i][:, tile(t)], k_t[:, t * P + b:t * P + b + nn],
                                             start=True, stop=False)
                            mm = nc.tensor.matmul(bank, neg_i[:, :], hide[n % 3][:, b:b + nn],
                                                  start=False, stop=True)
                        mm.then_inc(s_ps, 1)

                    def turn(n):
                        pe.wait_ge(p_n, n + 1)
                        for g, _, b, cnt in by_unit[n]:
                            if g >= 2:
                                pe.wait_ge(pt_ok, g - 1)
                            for k in range(cnt):
                                mm = nc.tensor.transpose(ps[:, 4 + g % 2, tile(k)],
                                                         prob_q[n % 3][:, tile(b + k)], ident)
                            mm.then_inc(pt_ps, 1)

                    def values(n):
                        t, i = units[n]
                        if i == 0 and t >= 2:
                            pe.wait_ge(o_ok, t - 1)
                        for g, _, b, cnt in by_unit[n]:
                            pe.wait_ge(pt_ok, g + 1)
                            for k in range(cnt):
                                mm = nc.tensor.matmul(ps[i * WD:(i + 1) * WD, 6 + t % 2, 0:P],
                                                      v_n[:, t + b + k, i * WD:(i + 1) * WD],
                                                      prob_t[:, g % 8, tile(k)],
                                                      start=(b + k == 0), stop=(b + k == NT - t - 1),
                                                      tile_position=(0, i * WD))
                        mm.then_inc(o_ps, 1)

                    pe.wait_ge(proj_out, 7)
                    pe.wait_ge(dx_ok, 1)
                    scores(0)
                    scores(1)
                    for n in range(len(units) + 1):
                        if n + 2 < len(units):
                            scores(n + 2)
                        if n < len(units):
                            turn(n)
                        if n >= 1:
                            values(n - 1)

                @block.scalar
                def _(act):
                    norm_act(act)
                    for c in range(NCH):
                        act.wait_ge(h_ok, c + 1)
                        nc.scalar.activation(relu[:, chunk(c)], h[:, chunk(c)], ACT.Relu).then_inc(relu_ok, 1)
                    act.wait_ge(proj, 4)
                    act.wait_ge(proj_out, 1)
                    for i in range(WH):
                        for c in range(NCH):
                            ins = nc.scalar.activation(q_m[i][:, chunk(c)], ps[:, 2 + c, :], ACT.Identity,
                                                       bias=bq_m[:, i:i + 1], scale=head_mask[:, i:i + 1])
                        ins.then_inc(proj_out, 1)
                    act.wait_ge(off_ps, NCH)
                    for c in range(NCH):
                        ins = nc.scalar.copy(off[:, chunk(c)], ps[0:WD, 6 + c, :]).then_inc(off_ok, 1)
                    act.wait_ge(z_ps, 1)
                    nc.scalar.activation(dx[:, 0, :], ps[:, 6, 0:NT], ACT.Sigmoid,
                                         bias=win[:, WW_SM + 3:WW_SM + 4]).then_inc(z_ps, 1)

                    def exps(n):
                        t, i = units[n]
                        w = T - t * P
                        act.wait_ge(m_ok, n + 1)
                        if n >= 3:
                            act.wait_ge(pt_ps, by_unit[n - 3][-1][0] + 1)
                        if w > CH:
                            src = ps[:, 2 * (n % 2):2 * (n % 2) + 2, :].rearrange("p a b -> p (a b)")[:, 0:w]
                        else:
                            src = ps[:, 2 * (n % 2), 0:w]
                        nc.scalar.activation(prob_q[n % 3][:, 0:w], src, ACT.Exp, bias=wbias[:, n:n + 1],
                                             scale=scale, accum_out=wsum[:, n:n + 1]).then_inc(p_ok, 1)

                    def take(n):
                        for g, _, b, cnt in by_unit[n]:
                            act.wait_ge(pt_ps, g + 1)
                            if g >= 8:
                                m = groups[g - 8][1]
                                act.wait_ge(o_ps, m + 1)
                            nc.scalar.copy(prob_t[:, g % 8, 0:cnt * P], ps[:, 4 + g % 2, 0:cnt * P]
                                           ).then_inc(pt_ok, 1)

                    for n in range(len(units) + 1):
                        if n < len(units):
                            exps(n)
                        if n >= 1:
                            take(n - 1)

                @block.vector
                def _(dve):
                    link = chain(dve, "dve_step")
                    norm_dve(dve)
                    segments(dve, link)
                    link(nc.vector.tensor_scalar(bq_m[:, :], head_mask, win[:, WW_SM:WW_SM + 1], None, ALU.mult))
                    dve.wait_ge(proj, 2)
                    link(nc.vector.tensor_scalar(k_t[:, :], ps[:, 0:2, :].rearrange("p a b -> p (a b)"),
                                                 win[:, WW_SM + 1:WW_SM + 2], None, ALU.add))
                    nc.vector.tensor_copy(bq_m[:, :], bq_m[:, :]).then_inc(proj_out, 1)
                    dve.wait_ge(proj, 6)
                    bv = win[:, WW_BV:WW_BV + D].unsqueeze(1).broadcast_to([P, TPC, D])
                    for c in range(NCH):
                        nc.vector.tensor_tensor(v_n[:, TPC * c:TPC * (c + 1), :],
                                                ps[:, 4 + c, :].rearrange("p (t d) -> p t d", t=TPC), bv,
                                                ALU.add).then_inc(proj_out, 1)
                    dve.wait_ge(z_ps, 2)
                    for i in range(WH):
                        link(nc.vector.tensor_scalar(dx[:, 1 + i, :], dx[:, 0, :], float(T), float(WINDOWS[i]),
                                                     ALU.mult, ALU.add))
                    nc.vector.tensor_copy(dx[:, 0, :], dx[:, 1, :]).then_inc(dx_ok, 1)

                    def hide_keys(n):
                        t, i = units[n]
                        w = T - t * P
                        if n >= 3:
                            dve.wait_ge(s_ps, n - 2)
                        nc.vector.tensor_scalar(hide[n % 3][:, 0:w], rel[:, 0:w], dx[:, 1 + i, t:t + 1], None,
                                                ALU.is_gt).then_inc(hide_ok, 1)

                    def maxima(n):
                        t, i = units[n]
                        w = T - t * P
                        dve.wait_ge(s_ps, n + 1)
                        if w > CH:
                            src = ps[:, 2 * (n % 2):2 * (n % 2) + 2, :].rearrange("p a b -> p (a b)")[:, 0:w]
                        else:
                            src = ps[:, 2 * (n % 2), 0:w]
                        link(nc.vector.tensor_reduce(wmax[:, 0, n:n + 1], src, AX_X, ALU.max))
                        nc.vector.tensor_scalar(wbias[:, n:n + 1], wmax[:, 0, n:n + 1], -scale, None,
                                                ALU.mult).then_inc(m_ok, 1)

                    def normalise(n):
                        t, i = units[n]
                        w = T - t * P
                        dve.wait_ge(p_ok, n + 1)
                        link(nc.vector.reciprocal(wrec[:, n:n + 1], wsum[:, n:n + 1]))
                        nc.vector.tensor_scalar(prob_q[n % 3][:, 0:w], prob_q[n % 3][:, 0:w], wrec[:, n:n + 1],
                                                None, ALU.mult).then_inc(p_n, 1)

                    def add_out(t):
                        dve.wait_ge(o_ps, WH * (t + 1))
                        nc.vector.tensor_tensor(x_res[:, tile(t)], x_res[:, tile(t)], ps[:, 6 + t % 2, 0:P],
                                                ALU.add).then_inc(o_ok, 1)

                    hide_keys(0)
                    hide_keys(1)
                    for n in range(len(units) + 1):
                        if n < len(units):
                            maxima(n)
                        if n + 2 < len(units):
                            hide_keys(n + 2)
                        if n >= 1:
                            normalise(n - 1)
                        if n >= 6 and (n - 6) % WH == 0:
                            add_out((n - 6) // WH)
                    add_out(NT - 1)
            end_phase()

        def self_attention_phase(layer):
            steps = attention_steps()
            scale = HD ** -0.5
            heads = [slice(4 * g, 4 * g + 4) for g in range(QUADS)]
            closed = [s[1] for s in steps if s[0] == "value" and s[4]]
            out_n = {s[2]: s[1] for s in steps if s[0] == "outT"}
            with phase() as block:
                wb_ok, proj, roped, took = sem("wb_ok"), sem("proj"), sem("roped"), sem("took")
                part1, part2, part3 = sem("part1"), sem("part2"), sem("part3")
                rest = sem("rest")
                spread = [sem(f"spread{c}") for c in range(NCH)]
                v_ps, v_ok = sem("v_ps"), sem("v_ok")
                ring_in, ring_out = sem("ring_in"), sem("ring_out")
                max_ok = sem("max_ok")
                max_split = sem("max_split")
                max_rows = [sem(f"max_rows{u % 2}") for u in range(len(UNITS))]
                score_in, prob_ok, value_ok = sem("score_in"), sem("prob_ok"), sem("value_ok")
                ot_ok = sem("ot_ok")
                turned, taken, made = sem("turned"), sem("taken"), sem("made")
                norm_pe, norm_act, norm_dve, h_ok = norm(
                    "norm1", x_dec, h, False, eps6, wa[:, WA_SM + SM_N1:WA_SM + SM_N1 + 1])
                turn_bank, made_bank = (4, 3), (0, 5)

                @block.sync
                def _(sp):
                    sp.dma_start(wb[:, :], layer_b[bass.ds(layer, 1), :, :].rearrange("a p n -> (a p) n")
                                 ).then_inc(wb_ok, 16)
                    for c in range(NCH):
                        for want, ready in enumerate((part1, part2, part3)):
                            sp.wait_ge(ready, 2 * (c + 1))
                            for s in range(SLOTS):
                                for dst, which, i in ((q_x, Q_PART[s], 0), (k_x, K_PART[s], 1)):
                                    if which == want:
                                        sp.dma_start(dst[s * HD:(s + 1) * HD, c, :, :],
                                                     parts[:, i, want, chunk(c)]).then_inc(spread[c], 16)
                    for u, (g, c) in enumerate(UNITS):
                        sp.wait_ge(max_split, u + 1)
                        for k in range(3):
                            sp.dma_start(q_x[MAX_ROW + k:MAX_ROW + k + 1, c, heads[g], :],
                                         max_p[:, u % 2, k, :]).then_inc(max_rows[u], 16)
                    sp.wait_ge(wb_ok, 16)

                @block.tensor
                def _(pe):
                    norm_pe(pe)
                    for c in range(NCH):
                        pe.wait_ge(h_ok, c + 1)
                        for i in range(4):
                            nc.tensor.matmul(ps[:, 4 * c + i, :], wa[:, WA_QK + i * D:WA_QK + (i + 1) * D],
                                             h[:, chunk(c)], start=True, stop=True).then_inc(proj, 1)
                    for c in range(NCH):
                        pe.wait_ge(took, 4)
                        for t in range(TPC):
                            mm = nc.tensor.matmul(ps[:, c, tile(t)], h[:, tile(TPC * c + t)],
                                                  wa[:, WA_V:WA_V + D], start=True, stop=True)
                        mm.then_inc(v_ps, 1)
                    pe.wait_ge(took, 8)
                    pe.wait_ge(v_ok, NCH)

                    def turn_output(c):
                        pe.wait_ge(prob_ok, 2 * closed[-1] + 2)
                        pe.wait_ge(ring_out, max(n for u, n in out_n.items() if UNITS[u][1] == c) + 1)
                        for t in range(TPC):
                            mm = nc.tensor.transpose(ps[:, turn_bank[c], tile(t)], o_n[:, TPC * c + t, :],
                                                     ident)
                        mm.then_inc(turned, 1)

                    ready = set()
                    for s in steps:
                        if s[0] in ("max", "maxT", "outT"):
                            n, u = s[1], s[2]
                            g, c = UNITS[u]
                            bank = n % 3
                            if n >= 3:
                                pe.wait_ge(ring_out, n - 2)
                        if s[0] == "max":
                            t, parts_, full = s[3:]
                            if c not in ready:
                                pe.wait_ge(spread[c], 16 * 2 * SLOTS)
                                ready.add(c)
                            for j, k0, width, col in parts_:
                                mm = nc.tensor.matmul(ps[:, bank, col:col + width],
                                                      q_x[0:MAX_ROW, c, 4 * g + j, tile(t % TPC)],
                                                      k_x[0:MAX_ROW, k0 // CH, 4 * g + j,
                                                          k0 % CH:k0 % CH + width],
                                                      start=True, stop=bool(full))
                                if not full:
                                    mm = nc.tensor.matmul(ps[:, bank, col + width - P:col + width], id_b[:, :],
                                                          mask_q[:, :], start=False, stop=True)
                            mm.then_inc(ring_in, 1)
                        elif s[0] == "maxT":
                            pe.wait_ge(max_ok, u + 1)
                            nc.tensor.transpose(ps[0:4 * TPC, bank, 0:P],
                                                max_q[:, u % 2, :, :].rearrange("p j t -> p (j t)"), ident
                                                ).then_inc(ring_in, 1)
                        elif s[0] == "outT":
                            if u == len(UNITS) - 1:
                                turn_output(1)
                            pe.wait_ge(ot_ok, u + 1)
                            for t in range(TPC):
                                mm = nc.tensor.transpose(ps[:, bank, tile(t)], o_t[:, tile(t)], ident)
                            mm.then_inc(ring_in, 1)
                        elif s[0] == "score":
                            _, m, item, u, kb, pair = s
                            g, c = UNITS[u]
                            if kb == 0 and pair == 0:
                                pe.wait_ge(max_rows[u], 48 * (u // 2 + 1))
                            if m >= 2:
                                pe.wait_ge(prob_ok, m - 1)
                            q0 = max(c * CH, kb * P)
                            width = (c + 1) * CH - q0
                            for i in range(2):
                                j = 4 * g + 2 * pair + i
                                bank = ps[:, 3 + 2 * (m % 2) + i, 0:width]
                                diag = kb * P >= c * CH
                                mm = nc.tensor.matmul(bank, k_x[0:KROWS, kb // TPC, j, tile(kb % TPC)],
                                                      q_x[0:KROWS, c, j, q0 - c * CH:CH], start=True,
                                                      stop=not diag)
                                if diag:
                                    mm = nc.tensor.matmul(bank[:, 0:P], id_b[:, :], mask_t[:, :],
                                                          start=False, stop=True)
                            mm.then_inc(score_in, 1)
                        else:
                            _, item, u, kb, last = s
                            g, c = UNITS[u]
                            pe.wait_ge(prob_ok, 2 * item + 2)
                            if kb == 0 and u:
                                pe.wait_ge(ot_ok, u)
                            q0 = max(c * CH, kb * P)
                            width = (c + 1) * CH - q0
                            for j in range(4):
                                mm = nc.tensor.matmul(ps[32 * j:32 * j + 32, 7, q0 - c * CH:CH],
                                                      v_aug[:, kb, 4 * g + j, :],
                                                      prob[:, 2 * (item % 2) + j // 2, j % 2, 0:width],
                                                      start=(kb == 0), stop=last,
                                                      tile_position=(0, 32 * j))
                            mm.then_inc(value_ok, 1)
                    turn_output(0)
                    for i, c in enumerate((1, 0)):
                        pe.wait_ge(taken, i + 1)
                        if i == 0:
                            pe.wait_ge(wb_ok, 16)
                        nc.tensor.matmul(ps[:, made_bank[c], :], wb[:, WB_O:WB_O + D], o_d[:, chunk(c)],
                                         start=True, stop=True).then_inc(made, 1)

                @block.scalar
                def _(act):
                    norm_act(act)
                    for n in range(4):
                        c, i = n // 2, n % 2
                        act.wait_ge(roped, n + 1)
                        nc.scalar.copy(parts[:, i, 0, chunk(c)], qk[:, i, chunk(c)]).then_inc(part1, 1)
                        if n:
                            c, i = (n - 1) // 2, (n - 1) % 2
                            act.wait_ge(rest, n)
                            nc.scalar.copy(parts[:, i, 1, chunk(c)], qk[:, i, chunk(c)]).then_inc(part2, 1)
                    act.wait_ge(rest, 4)
                    nc.scalar.copy(parts[:, 1, 1, chunk(1)], qk[:, 1, chunk(1)]).then_inc(part2, 1)
                    for s in steps:
                        if s[0] == "score":
                            _, m, item, u, kb, pair = s
                            c = UNITS[u][1]
                            act.wait_ge(score_in, m + 1)
                            if item >= 2:
                                act.wait_ge(value_ok, item - 1)
                            width = (c + 1) * CH - max(c * CH, kb * P)
                            b = 3 + 2 * (m % 2)
                            nc.scalar.activation(prob[:, 2 * (item % 2) + pair, :, 0:width],
                                                 ps[:, b:b + 2, 0:width], ACT.Exp, scale=scale
                                                 ).then_inc(prob_ok, 1)
                        elif s[0] == "value" and s[4]:
                            u = s[2]
                            act.wait_ge(value_ok, closed[u] + 1)
                            if u:
                                act.wait_ge(ring_in, out_n[u - 1] + 1)
                            nc.scalar.copy(o_t[:, :], ps[:, 7, :]).then_inc(ot_ok, 1)
                    for i, c in enumerate((1, 0)):
                        act.wait_ge(turned, i + 1)
                        nc.scalar.copy(o_d[:, chunk(c)], ps[:, turn_bank[c], :]).then_inc(taken, 1)

                @block.gpsimd
                def _(pool_):
                    for n in range(4):
                        c, i = n // 2, n % 2
                        pool_.wait_ge(part2, n + 1)
                        nc.gpsimd.tensor_tensor(parts[:, i, 2, chunk(c)], qk[:, i, chunk(c)],
                                                parts[:, i, 1, chunk(c)], ALU.subtract).then_inc(part3, 1)

                @block.vector
                def _(dve):
                    link = chain(dve, "dve_step")
                    norm_dve(dve)

                    def rope(n):
                        c, i = n // 2, n % 2
                        dve.wait_ge(proj, 4 * c + 2 * i + 2)
                        b = wa[:, WA_SM + SM_BQ + 2 * i:WA_SM + SM_BQ + 2 * i + 1]
                        br = wa[:, WA_SM + SM_BQ + 2 * i + 1:WA_SM + SM_BQ + 2 * i + 2]
                        nc.vector.scalar_tensor_tensor(tmp[:, 0, :], ps[:, 4 * c + 2 * i, :], b,
                                                       cos_t[:, chunk(c)], ALU.add, ALU.mult
                                                       ).then_inc(took, 1)
                        nc.vector.scalar_tensor_tensor(tmp[:, 1, :], ps[:, 4 * c + 2 * i + 1, :], br,
                                                       sin_t[:, chunk(c)], ALU.add, ALU.mult
                                                       ).then_inc(took, 1)
                        dve.wait_ge(took, 2 * n + 2)
                        nc.vector.tensor_tensor(qk[:, i, chunk(c)], tmp[:, 0, :], tmp[:, 1, :],
                                                ALU.add).then_inc(roped, 1)
                        dve.wait_ge(roped, n + 1)

                    def remainder(n):
                        c, i = n // 2, n % 2
                        dve.wait_ge(part1, n + 1)
                        nc.vector.tensor_tensor(qk[:, i, chunk(c)], qk[:, i, chunk(c)],
                                                parts[:, i, 0, chunk(c)], ALU.subtract).then_inc(rest, 1)

                    for n in range(5):
                        if n < 4:
                            rope(n)
                        if n:
                            remainder(n - 1)
                    bv = wa[:, WA_BV:WA_BV + D].rearrange("p (h d) -> p h d", h=H).unsqueeze(1).broadcast_to([P, TPC, H, HD])
                    for c in range(NCH):
                        dve.wait_ge(v_ps, c + 1)
                        nc.vector.tensor_tensor(v_aug[:, TPC * c:TPC * (c + 1), :, 0:HD],
                                                ps[:, c, :].rearrange("p (t h d) -> p t h d", t=TPC, h=H), bv,
                                                ALU.add).then_inc(v_ok, 1)
                    for s in steps:
                        if s[0] in ("max", "maxT", "outT"):
                            n, u = s[1], s[2]
                            g, c = UNITS[u]
                            bank = n % 3
                            dve.wait_ge(ring_in, n + 1)
                        if s[0] == "max":
                            t, parts_, full = s[3:]
                            j0, _, width, _ = parts_[0]
                            src = ps[:, bank, 0:len(parts_) * width].rearrange("p (j k) -> p j k", k=width)
                            dst = max_f if full else max_q
                            nc.vector.tensor_reduce(dst[:, u % 2, j0:j0 + len(parts_), t % TPC], src, AX_X,
                                                    ALU.max).then_inc(ring_out, 1)
                            if t % TPC == TPC - 1 and not full and j0 + len(parts_) == 4:
                                dve.wait_ge(ring_out, n + 1)
                                other = max_f if c else max_q
                                nc.vector.tensor_tensor(max_q[:, u % 2, :, :], max_q[:, u % 2, :, :],
                                                        other[:, u % 2, :, :], ALU.max).then_inc(max_ok, 1)
                        elif s[0] == "maxT":
                            if u >= 2:
                                dve.wait_ge(max_rows[u - 2], 48 * (u // 2))
                            src = ps[0:4 * TPC, bank, 0:P]
                            part = [max_p[:, u % 2, k, :] for k in range(3)]
                            link(nc.vector.tensor_scalar(part[0], src, -1.0, None, ALU.mult))
                            nc.vector.scalar_tensor_tensor(max_s[:, :], src, -1.0, part[0],
                                                           ALU.mult, ALU.subtract).then_inc(ring_out, 1)
                            dve.wait_ge(ring_out, n + 1)
                            link(nc.vector.tensor_copy(part[1], max_s[:, :]))
                            nc.vector.tensor_tensor(part[2], max_s[:, :], part[1], ALU.subtract
                                                    ).then_inc(max_split, 1)
                        elif s[0] == "outT":
                            src = ps[:, bank, :].rearrange("p (t j d) -> p t j d", t=TPC, j=4)
                            link(nc.vector.reciprocal(den[:, :, :], src[:, :, :, HD]))
                            dst = o_n[:, TPC * c:TPC * (c + 1), 4 * g * HD:4 * (g + 1) * HD].rearrange(
                                "p t (j d) -> p t j d", j=4)
                            nc.vector.tensor_tensor(dst, src[:, :, :, 0:HD],
                                                    den[:, :, :].unsqueeze(3).broadcast_to([P, TPC, 4, HD]),
                                                    ALU.mult).then_inc(ring_out, 1)
                            dve.wait_ge(ring_out, n + 1)
                    dve.wait_ge(wb_ok, 16)
                    for col, n, weight in ((WB_QC, D, SM_N2), (WB_G, 2 * F, SM_N3)):
                        nc.vector.tensor_scalar(wb[:, col:col + n], wb[:, col:col + n],
                                                wb[:, WB_SM + weight:WB_SM + weight + 1], None, ALU.mult)
                    for i, c in enumerate((1, 0)):
                        dve.wait_ge(made, i + 1)
                        nc.vector.scalar_tensor_tensor(x_dec[:, chunk(c)], ps[:, made_bank[c], :],
                                                       wb[:, WB_SM + SM_BO:WB_SM + SM_BO + 1],
                                                       x_dec[:, chunk(c)], ALU.add, ALU.add)
            end_phase()

        def linear_phase(src_n, weight, bias):
            with phase() as block:
                turned, taken, made = sem("turned"), sem("taken"), sem("made")

                @block.tensor
                def _(pe):
                    for c in range(NCH):
                        for t in range(TPC):
                            mm = nc.tensor.transpose(ps[:, c, tile(t)], src_n[:, TPC * c + t, :], ident)
                        mm.then_inc(turned, 1)
                    for c in range(NCH):
                        pe.wait_ge(taken, c + 1)
                        nc.tensor.matmul(ps[:, 2 + c, :], weight, o_d[:, chunk(c)], start=True,
                                         stop=True).then_inc(made, 1)

                @block.scalar
                def _(act):
                    for c in range(NCH):
                        act.wait_ge(turned, c + 1)
                        nc.scalar.copy(o_d[:, chunk(c)], ps[:, c, :]).then_inc(taken, 1)

                @block.vector
                def _(dve):
                    for c in range(NCH):
                        dve.wait_ge(made, c + 1)
                        if bias is None:
                            nc.vector.tensor_tensor(x_dec[:, chunk(c)], x_dec[:, chunk(c)], ps[:, 2 + c, :], ALU.add)
                        else:
                            nc.vector.scalar_tensor_tensor(x_dec[:, chunk(c)], ps[:, 2 + c, :], bias,
                                                           x_dec[:, chunk(c)], ALU.add, ALU.add)
            end_phase()

        qc = qk[:, 0, :]
        k_bd = cen[:, 0:CH]
        mem_b = sb("mem_b", [P, P], BF16)
        v_bd = tmp[:, 0, :].rearrange("p (g n) -> p g n", g=QUADS)
        mem_sb = sb("mem_sb", [P, KEYS])
        mem4 = sb("mem4", [P, 4 * NEAR])
        cross_scale = HD ** -0.5

        def near_phase():
            k_sb = mem_sb[:, 0:NEAR]
            e_q = [prob[:, i, 0, :] for i in range(3)]
            p_t = [prob[:, i, 1, :] for i in range(3)]
            mx = max_q[:, :, :, :].rearrange("p a b c -> p (a b c)")
            with phase() as block:
                q_ps, q_ok, kv_ps = sem("q_ps"), sem("q_ok"), sem("kv_ps")
                k_ok, v_ok = sem("k_ok"), sem("v_ok")
                s_ps, s_out, e_ok, n_ok = sem("s_ps"), sem("s_out"), sem("e_ok"), sem("n_ok")
                t_ps, t_ok, o_ps = sem("t_ps"), sem("t_ok"), sem("o_ps")
                norm_pe, norm_act, rs_ok = norm("norm", x_dec, None, False, eps6)

                @block.tensor
                def _(pe):
                    norm_pe(pe)
                    for c in range(NCH):
                        nc.tensor.matmul(ps[:, c, :], wb[:, WB_QC:WB_QC + D], x_dec[:, chunk(c)], start=True,
                                         stop=True).then_inc(q_ps, 1)
                    nc.tensor.matmul(ps[:, 2, 0:NEAR], wb[:, WB_KC:WB_KC + D], mem4[:, 0:NEAR], start=True,
                                     stop=True).then_inc(kv_ps, 1)
                    nc.tensor.matmul(ps[:, 3, 0:D], mem4[:, :], wb[:, WB_VC:WB_VC + D], start=True,
                                     stop=True).then_inc(kv_ps, 1)
                    pe.wait_ge(q_ok, NCH)
                    pe.wait_ge(k_ok, 1)
                    pe.wait_ge(v_ok, 1)

                    def scores(t):
                        if t >= 2:
                            pe.wait_ge(s_out, t - 1)
                        nc.tensor.matmul(ps[:, t % 2, :], qc[:, tile(t)], k_bd[:, 0:H * NEAR], start=True,
                                         stop=False)
                        nc.tensor.matmul(ps[:, t % 2, :].rearrange("p (h k) -> p h k", h=H), id_b[:, :],
                                         mask_near[:, t, :].unsqueeze(1).broadcast_to([P, H, NEAR]),
                                         start=False, stop=True).then_inc(s_ps, 1)

                    def turn(t):
                        pe.wait_ge(n_ok, t + 1)
                        if t >= 2:
                            pe.wait_ge(t_ok, t - 1)
                        for g in range(QUADS):
                            mm = nc.tensor.transpose(ps[:, 2 + t % 2, tile(g)], e_q[t % 3][:, tile(g)], ident)
                        mm.then_inc(t_ps, 1)

                    def values(t):
                        pe.wait_ge(t_ok, t + 1)
                        for g in range(QUADS):
                            mm = nc.tensor.matmul(ps[:, 4 + t // TPC, tile(t % TPC)], v_bd[:, g, :],
                                                  p_t[t % 3][:, tile(g)], start=(g == 0), stop=(g == QUADS - 1))
                        mm.then_inc(o_ps, 1)

                    scores(0)
                    scores(1)
                    for t in range(NT + 1):
                        if t + 2 < NT:
                            scores(t + 2)
                        if t < NT:
                            turn(t)
                        if t >= 1:
                            values(t - 1)
                    for c in range(NCH):
                        pe.wait_ge(t_ok, NT + c + 1)
                        nc.tensor.matmul(ps[:, 6 + c, :], wb[:, WB_OC:WB_OC + D], o_d[:, chunk(c)], start=True,
                                         stop=True).then_inc(o_ps, 1)

                @block.scalar
                def _(act):
                    norm_act(act)

                    def exps(t):
                        act.wait_ge(s_out, t + 1)
                        nc.scalar.activation(e_q[t % 3], e_q[t % 3], ACT.Exp, scale=cross_scale).then_inc(e_ok, 1)

                    def take(t):
                        act.wait_ge(t_ps, t + 1)
                        if t >= 3:
                            act.wait_ge(o_ps, t - 2)
                        nc.scalar.copy(p_t[t % 3], ps[:, 2 + t % 2, :]).then_inc(t_ok, 1)

                    for t in range(NT + 1):
                        if t < NT:
                            exps(t)
                        if t >= 1:
                            take(t - 1)
                    for c in range(NCH):
                        act.wait_ge(o_ps, TPC * (c + 1))
                        nc.scalar.copy(o_d[:, chunk(c)], ps[:, 4 + c, :]).then_inc(t_ok, 1)

                @block.vector
                def _(dve):
                    link = chain(dve, "dve_step")
                    dve.wait_ge(kv_ps, 2)
                    link(nc.vector.tensor_copy(k_sb, ps[:, 2, 0:NEAR]))
                    nc.vector.tensor_tensor(k_bd[:, 0:H * NEAR].rearrange("p (h k) -> p h k", h=H),
                                            k_sb.unsqueeze(1).broadcast_to([P, H, NEAR]),
                                            tab[:, R_HM16:R_HM16 + H].unsqueeze(2).broadcast_to([P, H, NEAR]),
                                            ALU.mult).then_inc(k_ok, 1)
                    nc.vector.tensor_tensor(v_bd, ps[:, 3, 0:D].unsqueeze(1).broadcast_to([P, QUADS, D]),
                                            tab[:, R_VMASK:R_VMASK + QUADS * D].rearrange("p (g n) -> p g n", g=QUADS),
                                            ALU.mult).then_inc(v_ok, 1)
                    for c in range(NCH):
                        dve.wait_ge(q_ps, c + 1)
                        dve.wait_ge(rs_ok, c + 1)
                        nc.vector.tensor_tensor(qc[:, chunk(c)], ps[:, c, :], rs[:, chunk(c)], ALU.mult
                                                ).then_inc(q_ok, 1)

                    def shift(t):
                        dve.wait_ge(s_ps, t + 1)
                        if t >= 3:
                            dve.wait_ge(t_ps, t - 2)
                        s3 = ps[:, t % 2, :].rearrange("p (h k) -> p h k", h=H)
                        m = mx[:, 16 * (t % 2):16 * (t % 2) + 16]
                        link(nc.vector.tensor_reduce(m, s3, AX_X, ALU.max))
                        nc.vector.tensor_tensor(e_q[t % 3].rearrange("p (h k) -> p h k", h=H), s3,
                                                m.unsqueeze(2).broadcast_to([P, H, NEAR]),
                                                ALU.subtract).then_inc(s_out, 1)

                    def normalise(t):
                        dve.wait_ge(e_ok, t + 1)
                        e3 = e_q[t % 3].rearrange("p (h k) -> p h k", h=H)
                        d = den[:, :, :].rearrange("p a b -> p (a b)")
                        link(nc.vector.tensor_reduce(d, e3, AX_X, ALU.add))
                        link(nc.vector.reciprocal(d, d))
                        nc.vector.tensor_tensor(e3, e3, d.unsqueeze(2).broadcast_to([P, H, NEAR]),
                                                ALU.mult).then_inc(n_ok, 1)
                        dve.wait_ge(n_ok, t + 1)

                    for t in range(NT + 1):
                        if t < NT:
                            shift(t)
                        if t >= 1:
                            normalise(t - 1)
                    for c in range(NCH):
                        dve.wait_ge(o_ps, NT + c + 1)
                        nc.vector.tensor_tensor(x_dec[:, chunk(c)], x_dec[:, chunk(c)], ps[:, 6 + c, :], ALU.add)
            end_phase()

        def feed_forward_phase(layer):
            gate = [cen[:, 0:CH], cen[:, CH:T], o_t[:, :]]
            up_n = [qk[:, 0, 0:CH], qk[:, 0, CH:T], qk[:, 1, 0:CH]]
            hid = prob[:, :, :, :].rearrange("p a b c -> p a (b c)")
            units = [(c, f) for c in range(NCH) for f in range(FT)]
            with phase() as block:
                wa_ok, up, scaled, silu, hid_ok, down = (
                    sem(x) for x in ("wa_ok", "up", "scaled", "silu", "hid_ok", "down"))
                norm_pe, norm_act, rs_ok = norm("norm", x_dec, None, False, eps6)

                @block.sync
                def _(sp):
                    sp.dma_start(wa[:, :], layer_a[bass.ds(layer + 1, 1), :, :].rearrange("a p n -> (a p) n")
                                 ).then_inc(wa_ok, 16)
                    sp.wait_ge(wa_ok, 16)

                @block.tensor
                def _(pe):
                    norm_pe(pe)

                    def ups(n):
                        c, f = units[n]
                        b = 2 * (n % 3)
                        if n >= 3:
                            pe.wait_ge(scaled, 2 * (n - 2))
                        nc.tensor.matmul(ps[:, b, :], wb[:, WB_G + f * P:WB_G + (f + 1) * P], x_dec[:, chunk(c)],
                                         start=True, stop=True).then_inc(up, 1)
                        nc.tensor.matmul(ps[:, b + 1, :], wb[:, WB_U + f * P:WB_U + (f + 1) * P], x_dec[:, chunk(c)],
                                         start=True, stop=True).then_inc(up, 1)

                    def downs(n):
                        c, f = units[n]
                        pe.wait_ge(hid_ok, n + 1)
                        mm = nc.tensor.matmul(ps[:, 6 + c, :], wb[:, WB_DN + f * D:WB_DN + (f + 1) * D],
                                              hid[:, f, chunk(c)], start=(f == 0), stop=(f == FT - 1))
                        if f == FT - 1:
                            mm.then_inc(down, 1)

                    for n in range(len(units) + 2):
                        if n < len(units):
                            ups(n)
                        if n >= 2:
                            downs(n - 2)

                @block.scalar
                def _(act):
                    norm_act(act)
                    for n, (c, f) in enumerate(units):
                        act.wait_ge(scaled, 2 * n + 1)
                        nc.scalar.activation(gate[n % 3], gate[n % 3], ACT.Silu).then_inc(silu, 1)

                @block.vector
                def _(dve):

                    def scale(n):
                        c, f = units[n]
                        dve.wait_ge(rs_ok, c + 1)
                        if n >= 3:
                            dve.wait_ge(hid_ok, n - 2)
                        for i, dst in enumerate((gate[n % 3], up_n[n % 3])):
                            dve.wait_ge(up, 2 * n + 1 + i)
                            nc.vector.tensor_tensor(dst, ps[:, 2 * (n % 3) + i, :], rs[:, chunk(c)],
                                                    ALU.mult).then_inc(scaled, 1)

                    for n in range(len(units) + 1):
                        if n < len(units):
                            scale(n)
                        if n:
                            c, f = units[n - 1]
                            dve.wait_ge(silu, n)
                            dve.wait_ge(scaled, 2 * n)
                            nc.vector.tensor_tensor(hid[:, f, chunk(c)], gate[(n - 1) % 3], up_n[(n - 1) % 3],
                                                    ALU.mult).then_inc(hid_ok, 1)
                    for c in range(NCH):
                        dve.wait_ge(down, c + 1)
                        nc.vector.tensor_tensor(x_dec[:, chunk(c)], x_dec[:, chunk(c)], ps[:, 6 + c, :], ALU.add)
            end_phase()

        def far_path():
            iota = tab[:, R_IOTA:R_IOTA + KEYS]
            k_far = prob[:, :, :, :].rearrange("p a b c -> p (a b c)")[:, 0:H * KEYS]
            v_far = o_t[:, 0:D]
            e_far = cen[:, 0:CH]
            pt_far = cen[:, CH:T]
            hide = h[:, 0:P]
            pad = h[:, P:2 * P]
            near_end = h[:, 2 * P:2 * P + NT]
            top = sq[:, 0:NT * H].rearrange("p (t h) -> p t h", t=NT)
            total = sq[:, NT * H:2 * NT * H].rearrange("p (t h) -> p t h", t=NT)
            new = sq[:, 2 * NT * H:2 * NT * H + 4]
            seg_r = sq[:, 3 * NT * H:3 * NT * H + NT]
            end_r = sq[:, 4 * NT * H:4 * NT * H + 1]
            hide_b = mem_b[:, 0:P]

            def start():
                with phase() as block:
                    q_ps = sem("q_ps")
                    norm_pe, norm_act, rs_ok = norm("norm", x_dec, None, False, eps6)

                    @block.tensor
                    def _(pe):
                        norm_pe(pe)
                        for c in range(NCH):
                            nc.tensor.matmul(ps[:, c, :], wb[:, WB_QC:WB_QC + D], x_dec[:, chunk(c)],
                                             start=True, stop=True).then_inc(q_ps, 1)

                    @block.scalar
                    def _(act):
                        norm_act(act)

                    @block.vector
                    def _(dve):
                        for c in range(NCH):
                            dve.wait_ge(q_ps, c + 1)
                            dve.wait_ge(rs_ok, c + 1)
                            nc.vector.tensor_tensor(qc[:, chunk(c)], ps[:, c, :], rs[:, chunk(c)], ALU.mult)
                        nc.vector.memset(top, -float(2 ** 126))
                        nc.vector.memset(total, 0.0)
                        nc.vector.memset(o_n[:, :, :], 0.0)
                end_phase()

            def rewind():
                with phase() as block:
                    @block.vector
                    def _(dve):
                        nc.vector.tensor_copy(seg_r, seg_q[:, :])
                        nc.vector.memset(end_r, float(S_MEM - 1))
                end_phase()

            def block_phase(kb, sums):
                units = [(t, g) for t in range(NT) for g in range(QUADS)]
                with phase() as block:
                    mem_ok, kv_ps, kv_ok, hide_ok = (sem(x) for x in ("mem_ok", "kv_ps", "kv_ok", "hide_ok"))
                    s_ps, s_out, e_ok, t_ps, t_ok, o_ps, o_out = (
                        sem(x) for x in ("s_ps", "s_out", "e_ok", "t_ps", "t_ok", "o_ps", "o_out"))

                    @block.sync
                    def _(sp):
                        sp.dma_start(mem_sb[:, :], mem_t[bass.ds(kb, 1), :, :].rearrange("a p n -> (a p) n")
                                     ).then_inc(mem_ok, 16)

                    @block.tensor
                    def _(pe):
                        pe.wait_ge(mem_ok, 16)
                        nc.tensor.matmul(ps[:, 0, 0:KEYS], wb[:, WB_KC:WB_KC + D], mem_sb[:, :], start=True,
                                         stop=True)
                        nc.tensor.matmul(ps[:, 1, 0:D], mem_sb[:, :], wb[:, WB_VC:WB_VC + D], start=True,
                                         stop=True).then_inc(kv_ps, 1)
                        pe.wait_ge(kv_ok, 1)
                        for n, (t, g) in enumerate(units):
                            pe.wait_ge(hide_ok, t + 1)
                            if n:
                                pe.wait_ge(s_out, n)
                            nc.tensor.matmul(ps[:, 2, :], qc[:, tile(t)], k_far[:, g * CH:(g + 1) * CH],
                                             start=True, stop=False)
                            nc.tensor.matmul(ps[:, 2, :].rearrange("p (j k) -> p j k", j=4), id_b[:, :],
                                             hide_b.unsqueeze(1).broadcast_to([P, 4, KEYS]), start=False,
                                             stop=True).then_inc(s_ps, 1)
                            if not sums:
                                continue
                            pe.wait_ge(e_ok, n + 1)
                            if n:
                                pe.wait_ge(t_ok, n)
                            for j in range(4):
                                mm = nc.tensor.transpose(ps[:, 3, tile(j)], e_far[:, tile(j)], ident)
                            mm.then_inc(t_ps, 1)
                            pe.wait_ge(t_ok, n + 1)
                            if g == 0 and t:
                                pe.wait_ge(o_out, t)
                            for j in range(4):
                                col = (4 * g + j) * HD
                                mm = nc.tensor.matmul(ps[:, 4, col:col + HD], pt_far[:, tile(j)],
                                                      v_far[:, col:col + HD], start=True, stop=True)
                            mm.then_inc(o_ps, 1)

                    @block.scalar
                    def _(act):
                        if sums:
                            for n in range(len(units)):
                                act.wait_ge(s_out, n + 1)
                                nc.scalar.activation(e_far, e_far, ACT.Exp, scale=cross_scale).then_inc(e_ok, 1)
                                act.wait_ge(t_ps, n + 1)
                                if n:
                                    act.wait_ge(o_ps, n)
                                nc.scalar.copy(pt_far, ps[:, 3, :]).then_inc(t_ok, 1)

                    @block.vector
                    def _(dve):
                        link = chain(dve, "dve_step")
                        dve.wait_ge(kv_ps, 1)
                        link(nc.vector.tensor_copy(e_far[:, 0:KEYS], ps[:, 0, 0:KEYS]))
                        link(nc.vector.tensor_copy(v_far, ps[:, 1, 0:D]))
                        link(nc.vector.tensor_tensor(
                            k_far.rearrange("p (h k) -> p h k", h=H),
                            e_far[:, 0:KEYS].unsqueeze(1).broadcast_to([P, H, KEYS]),
                            tab[:, R_HM16:R_HM16 + H].unsqueeze(2).broadcast_to([P, H, KEYS]), ALU.mult))
                        nc.vector.tensor_copy(new[:, 0:1], end_r).then_inc(kv_ok, 1)
                        link(nc.vector.tensor_scalar(pad, iota, end_r, NEG_PAD / NEG, ALU.is_gt, ALU.mult))
                        link(nc.vector.tensor_scalar(near_end, seg_r, -float(LOOKBACK), None, ALU.add))
                        for n, (t, g) in enumerate(units):
                            if g == 0:
                                link(nc.vector.tensor_scalar(hide, iota, seg_r[:, t:t + 1], None, ALU.is_gt))
                                link(nc.vector.scalar_tensor_tensor(hide, iota, near_end[:, t:t + 1], hide,
                                                                    ALU.is_le, ALU.max))
                                link(nc.vector.tensor_tensor(hide, hide, pad, ALU.max))
                                if n:
                                    dve.wait_ge(s_ps, n)
                                nc.vector.tensor_scalar(hide_b, hide, NEG, None, ALU.mult).then_inc(hide_ok, 1)
                            dve.wait_ge(s_ps, n + 1)
                            s3 = ps[:, 2, :].rearrange("p (j k) -> p j k", j=4)
                            heads = slice(4 * g, 4 * g + 4)
                            if not sums:
                                link(nc.vector.tensor_reduce(new, s3, AX_X, ALU.max))
                                nc.vector.tensor_tensor(top[:, t, heads], top[:, t, heads], new,
                                                        ALU.max).then_inc(s_out, 1)
                                dve.wait_ge(s_out, n + 1)
                                continue
                            if n:
                                dve.wait_ge(t_ps, n)
                            e3 = e_far.rearrange("p (j k) -> p j k", j=4)
                            nc.vector.tensor_tensor(e3, s3, top[:, t, heads].unsqueeze(2).broadcast_to([P, 4, KEYS]),
                                                    ALU.subtract).then_inc(s_out, 1)
                            dve.wait_ge(e_ok, n + 1)
                            link(nc.vector.tensor_reduce(new, e3, AX_X, ALU.add))
                            link(nc.vector.tensor_tensor(total[:, t, heads], total[:, t, heads], new, ALU.add))
                            if g == QUADS - 1:
                                dve.wait_ge(o_ps, n + 1)
                                nc.vector.tensor_tensor(o_n[:, t, :], o_n[:, t, :], ps[:, 4, 0:D],
                                                        ALU.add).then_inc(o_out, 1)
                        nc.vector.tensor_scalar(seg_r, seg_r, -float(KEYS), None, ALU.add)
                        nc.vector.tensor_scalar(end_r, end_r, -float(KEYS), None, ALU.add)
                end_phase()

            def finish():
                with phase() as block:
                    @block.vector
                    def _(dve):
                        link = chain(dve, "dve_step")
                        link(nc.vector.reciprocal(total, total))
                        o4 = o_n[:, :, :].rearrange("p t (h d) -> p t h d", h=H)
                        nc.vector.tensor_tensor(o4, o4, total.unsqueeze(3).broadcast_to([P, NT, H, HD]), ALU.mult)
                end_phase()

            start()
            for sums in (False, True):
                rewind()
                with nc.Fori(0, MEM_BLOCKS) as kb:
                    block_phase(kb, sums)
            finish()
            linear_phase(o_n, wb[:, WB_OC:WB_OC + D], None)

        rt = sb("rt", [P, RT_COLS])
        exp_w = big[:, :].bitcast(F32).rearrange("p (e n) -> p e n", e=E)
        gate_rows = sb("gate_rows", [3 * E, T], BF16)
        gate_t = sb("gate_t", [E, T])
        pick_e = sb("pick_e", [3 * E, E * P], BF16)
        b2_sb = sb("b2_sb", [E, D])

        def route_phase():
            small = cen[:, 0:14 * NT * E].rearrange("p (n t e) -> p n t e", n=14, t=NT)
            prob_e, best, cand, one1, one2, rest, chosen, gates_s, gates_f, r1 = (small[:, i] for i in range(10))
            col = lambda i: small[:, 10, i, :]
            top, tie1, top2, tie2, denom = (col(i) for i in range(5))
            count = small[:, 11:13].rearrange("p n t e -> p (n t e)").rearrange("p (n k t) -> p n k t", n=8, k=TOPK)
            rank = sq[:, 0:TOPK * NT].rearrange("p (k t) -> p k t", k=TOPK)
            bpart = parts[:, 0, 0, 0:NT * 3 * E].rearrange("p (t a e) -> p t a e", t=NT, a=3)
            bone = [parts[:, 0, 1 + k, 0:NT * 3 * E].rearrange("p (t a e) -> p t a e", t=NT, a=3) for k in range(TOPK)]
            bgate = parts[:, 1, 0, 0:NT * 3 * E].rearrange("p (t a e) -> p t a e", t=NT, a=3)
            rows = [parts[0:3 * E, 1, 1, :], parts[0:3 * E, 1, 2, :], gate_rows[:, :]]
            junk = qk[:, 1, :]
            pick_f = qk[0:3 * E, 0, :]
            e_rev = tab[:, R_EREV:R_EREV + E].unsqueeze(1).broadcast_to([P, NT, E])
            tri, offd = tab[:, R_TRI:R_TRI + P], tab[:, R_OFFD:R_OFFD + P]

            def wide(x):
                return x.unsqueeze(2).broadcast_to([P, NT, E])

            with phase() as block:
                l_ps, l_ok, e_ok = sem("l_ps"), sem("l_ok"), sem("e_ok")
                added = sem("added")
                norm_pe, norm_act, norm_dve, n_ok = norm("norm", x_dec, h, False, eps6, nf_col[:, 0:1])
                ln_pe, ln_act, ln_dve, h_ok = norm("ln", x_res, h, True, eps5, None, added)
                got = sem("got")
                parts_ok, t_ps, t_ok, r_ps, r_out = (sem(x) for x in ("parts_ok", "t_ps", "t_ok", "r_ps", "r_out"))
                g_ok, gt_ps = sem("g_ok"), sem("gt_ps")

                @block.sync
                def _(sp):
                    sp.dma_start(rt[:, :], router).then_inc(got, 16)
                    sp.dma_start(pick_f, tables[0:3 * E, R_COLS:R_COLS + E * P]).then_inc(got, 16)
                    sp.dma_start(b2_sb[:, :], b2).then_inc(got, 16)
                    for e in range(E):
                        sp.dma_start(exp_w[:, e, 0:MF], w1[e]).then_inc(experts_got, 16)
                        sp.dma_start(exp_w[:, e, MF:2 * MF], w2[e]).then_inc(experts_got, 16)

                @block.tensor
                def _(pe):
                    norm_pe(pe)
                    ln_pe(pe)
                    pe.wait_ge(h_ok, NCH)
                    pe.wait_ge(got, 16 * 3)
                    for t in range(NT):
                        mm = nc.tensor.matmul(ps[:, 0, E * t:E * (t + 1)], h[:, tile(t)], rt[:, RT_W:RT_W + E],
                                              start=True, stop=True)
                    mm.then_inc(l_ps, 1)
                    pe.wait_ge(parts_ok, 1)
                    for b, src in enumerate((bpart, bone[0], bone[1])):
                        for t in range(NT):
                            mm = nc.tensor.transpose(ps[0:3 * E, 1 + b, :].bitcast(BF16)[:, tile(t)],
                                                     src[:, t, :, :].rearrange("p a e -> p (a e)"), id_b[:, :])
                        mm.then_inc(t_ps, 1)
                    pe.wait_ge(t_ok, 3)
                    n = 0
                    for k in range(TOPK):
                        for t in range(NT):
                            if n >= 2:
                                pe.wait_ge(r_out, n - 1)
                            for c in range(NCH):
                                mm = nc.tensor.matmul(ps[:, 4 + 2 * (n % 2) + c, :], rows[1 + k][:, tile(t)],
                                                      rows[0][:, chunk(c)], start=True, stop=True)
                            mm.then_inc(r_ps, 1)
                            n += 1
                    pe.wait_ge(g_ok, 1)
                    for t in range(NT):
                        mm = nc.tensor.transpose(ps[0:3 * E, 1, :].bitcast(BF16)[:, tile(t)],
                                                 bgate[:, t, :, :].rearrange("p a e -> p (a e)"), id_b[:, :])
                    mm.then_inc(gt_ps, 1)
                    for t in range(NT):
                        mm = nc.tensor.transpose(ps[0:E, 2 + t // TPC, tile(t % TPC)], gates_f[:, t, :], ident)
                    mm.then_inc(gt_ps, 1)

                @block.scalar
                def _(act):
                    norm_act(act)
                    ln_act(act)
                    act.wait_ge(l_ok, 1)
                    nc.scalar.activation(prob_e, best, ACT.Exp).then_inc(e_ok, 1)

                @block.vector
                def _(dve):
                    link = chain(dve, "dve_step")
                    v = nc.vector
                    norm_dve(dve)
                    for c in range(NCH):
                        dve.wait_ge(n_ok, c + 1)
                        nc.vector.tensor_tensor(x_res[:, chunk(c)], x_res[:, chunk(c)], h[:, chunk(c)],
                                                ALU.add).then_inc(added, 1)
                    dve.wait_ge(added, NCH)
                    ln_dve(dve)
                    dve.wait_ge(h_ok, NCH)
                    dve.wait_ge(got, 16 * 3)
                    link(v.tensor_copy(pick_e[:, :], pick_f))
                    dve.wait_ge(l_ps, 1)
                    link(v.tensor_tensor(prob_e, ps[:, 0, 0:NT * E].rearrange("p (t e) -> p t e", t=NT),
                                         rt[:, RT_B:RT_B + E].unsqueeze(1).broadcast_to([P, NT, E]), ALU.add))
                    link(v.tensor_reduce(top, prob_e, AX_X, ALU.max))
                    v.tensor_tensor(best, prob_e, wide(top), ALU.subtract).then_inc(l_ok, 1)
                    dve.wait_ge(e_ok, 1)
                    link(v.tensor_reduce(denom, prob_e, AX_X, ALU.add))
                    link(v.reciprocal(denom, denom))
                    link(v.tensor_tensor(prob_e, prob_e, wide(denom), ALU.mult))
                    for src, t_, tie, one in ((prob_e, top, tie1, one1), (rest, top2, tie2, one2)):
                        link(v.tensor_reduce(t_, src, AX_X, ALU.max))
                        link(v.tensor_tensor(best, src, wide(t_), ALU.is_equal))
                        link(v.tensor_tensor(cand, best, e_rev, ALU.mult))
                        link(v.tensor_reduce(tie, cand, AX_X, ALU.max))
                        link(v.tensor_tensor(one, e_rev, wide(tie), ALU.is_equal))
                        if src is prob_e:
                            link(v.scalar_tensor_tensor(rest, one1, -2.0, prob_e, ALU.mult, ALU.add))
                    link(v.tensor_tensor(chosen, one1, one2, ALU.add))
                    link(v.tensor_tensor(gates_s, prob_e, chosen, ALU.mult))
                    link(v.scalar_tensor_tensor(gates_s, chosen, -1.0, gates_s, ALU.add, ALU.add))

                    def split(dst, src):
                        link(v.tensor_copy(dst[:, :, 0, :], src))
                        link(v.tensor_tensor(r1, src, dst[:, :, 0, :], ALU.subtract))
                        link(v.tensor_copy(dst[:, :, 1, :], r1))
                        link(v.tensor_tensor(dst[:, :, 2, :], r1, dst[:, :, 1, :], ALU.subtract))

                    split(bpart, gates_s)
                    for k, one in enumerate((one1, one2)):
                        link(v.tensor_copy(bone[k], one.unsqueeze(2).broadcast_to([P, NT, 3, E])))
                    v.memset(count, 0.0).then_inc(parts_ok, 1)
                    for b in range(3):
                        dve.wait_ge(t_ps, b + 1)
                        v.tensor_copy(rows[b], ps[0:3 * E, 1 + b, :].bitcast(BF16)).then_inc(t_ok, 1)
                    dve.wait_ge(parts_ok, 1)
                    n = 0
                    for k, g in enumerate((top, top2)):
                        for t in range(NT):
                            dve.wait_ge(r_ps, n + 1)
                            if n:
                                dve.wait_ge(r_out, n)
                            r = ps[:, 4 + 2 * (n % 2):6 + 2 * (n % 2), :].rearrange("p a b -> p (a b)")
                            gi = g[:, t:t + 1]
                            here = r[:, tile(t)]
                            if t:
                                link(v.tensor_scalar(junk[:, 0:t * P], r[:, 0:t * P], gi, 0.0, ALU.is_ge, ALU.add,
                                                     accum_out=count[:, 0, k, t:t + 1]))
                            if t < NT - 1:
                                link(v.tensor_scalar(junk[:, 0:T - (t + 1) * P], r[:, (t + 1) * P:T], gi, 0.0,
                                                     ALU.is_gt, ALU.add, accum_out=count[:, 1, k, t:t + 1]))
                            link(v.scalar_tensor_tensor(junk[:, 0:P], here, gi, offd, ALU.is_gt, ALU.mult,
                                                        accum_out=count[:, 2, k, t:t + 1]))
                            v.scalar_tensor_tensor(junk[:, P:2 * P], here, gi, tri, ALU.is_equal, ALU.mult,
                                                   accum_out=count[:, 3, k, t:t + 1]).then_inc(r_out, 1)
                            n += 1
                    dve.wait_ge(r_out, n)
                    link(v.tensor_tensor(rank, count[:, 0], count[:, 1], ALU.add))
                    link(v.tensor_tensor(rank, rank, count[:, 2], ALU.add))
                    link(v.tensor_tensor(rank, rank, count[:, 3], ALU.add))
                    link(v.tensor_scalar(rank, rank, float(CAP), None, ALU.is_lt))
                    link(v.tensor_tensor(tie1, top, rank[:, 0], ALU.mult))
                    link(v.tensor_tensor(tie2, top2, rank[:, 1], ALU.mult))
                    link(v.tensor_tensor(cand, one1, wide(tie1), ALU.mult))
                    link(v.tensor_tensor(best, one2, wide(tie2), ALU.mult))
                    link(v.tensor_tensor(gates_f, cand, best, ALU.add))
                    split(bgate, gates_f)
                    v.tensor_copy(denom, denom).then_inc(g_ok, 1)
                    dve.wait_ge(gt_ps, 1)
                    v.tensor_copy(gate_rows[:, :], ps[0:3 * E, 1, :].bitcast(BF16))
                    dve.wait_ge(gt_ps, 2)
                    for c in range(NCH):
                        v.tensor_copy(gate_t[:, chunk(c)], ps[0:E, 2 + c, :])
            end_phase()

        def experts_phase():
            units = [(c, e, f) for c in range(NCH) for e in range(E) for f in range(MT)]
            act_h = [prob[:, i, 0, :] for i in range(3)]
            gated = [prob[:, i, 1, :] for i in range(3)]
            with phase() as block:
                up, gate_ps, gate_used, silu, hid_ok, down, done, stored = (
                    sem(x) for x in ("up", "gate_ps", "gate_used", "silu", "hid_ok", "down", "done", "stored"))

                @block.sync
                def _(sp):
                    for c in range(NCH):
                        sp.wait_ge(done, c + 1)
                        sp.dma_start(out[:, chunk(c)], x_res[:, chunk(c)]).then_inc(stored, 16)
                    sp.wait_ge(stored, 16 * NCH)

                @block.tensor
                def _(pe):
                    pe.wait_ge(experts_got, 16 * 2 * E)

                    def ups(n):
                        c, e, f = units[n]
                        m = n // MT
                        if f == 0:
                            if m >= 2:
                                pe.wait_ge(hid_ok, MT * (m - 1))
                            nc.tensor.matmul(ps[:, 3 + m % 2, :], pick_e[:, e * P:(e + 1) * P],
                                             gate_rows[:, chunk(c)], start=True, stop=True).then_inc(gate_ps, 1)
                        if n >= 3:
                            pe.wait_ge(silu, n - 2)
                        nc.tensor.matmul(ps[:, n % 3, :], exp_w[:, e, f * P:(f + 1) * P], h[:, chunk(c)],
                                         start=True, stop=True).then_inc(up, 1)

                    def downs(n):
                        c, e, f = units[n]
                        if e == 0 and f == 0:
                            nc.tensor.matmul(ps[:, 6 + c, :], b2_sb[:, :], gate_t[:, chunk(c)], start=True,
                                             stop=False)
                        pe.wait_ge(hid_ok, n + 1)
                        mm = nc.tensor.matmul(ps[:, 6 + c, :], exp_w[:, e, MF + f * D:MF + (f + 1) * D],
                                              gated[n % 3], start=False, stop=(e == E - 1 and f == MT - 1))
                        mm.then_inc(down, 1)

                    for n in range(len(units) + 2):
                        if n < len(units):
                            ups(n)
                        if n >= 2:
                            downs(n - 2)

                @block.scalar
                def _(act):
                    for n, (c, e, f) in enumerate(units):
                        act.wait_ge(up, n + 1)
                        if n >= 3:
                            act.wait_ge(hid_ok, n - 2)
                        col = RT_B1 + e * MT + f
                        nc.scalar.activation(act_h[n % 3], ps[:, n % 3, :], ACT.Silu, bias=rt[:, col:col + 1]
                                             ).then_inc(silu, 1)

                @block.vector
                def _(dve):
                    for n, (c, e, f) in enumerate(units):
                        dve.wait_ge(silu, n + 1)
                        dve.wait_ge(gate_ps, n // MT + 1)
                        if n >= 3:
                            dve.wait_ge(down, n - 2)
                        nc.vector.tensor_tensor(gated[n % 3], act_h[n % 3], ps[:, 3 + (n // MT) % 2, :],
                                                ALU.mult).then_inc(hid_ok, 1)
                        if e == E - 1 and f == MT - 1:
                            dve.wait_ge(down, n + 1)
                            nc.vector.tensor_tensor(x_res[:, chunk(c)], x_res[:, chunk(c)], ps[:, 6 + c, :],
                                                    ALU.add).then_inc(done, 1)
            end_phase()

        def decoder_input_phase():
            with phase() as block:
                filled = sem("filled")
                norm_pe, norm_act, norm_dve, _ = norm("norm", x_res, x_dec, True, eps5)
                first = SLOTS * HD

                @block.sync
                def _(sp):
                    for rows, n in ((big[:, 0:16 * T], ZERO_ROWS), (big[:, 16 * T:32 * T], ZERO_ROWS + 3)):
                        dst = rows[first:first + n, :].bitcast(I32)
                        sp.dma_start(dst, fill[0:n, :]).then_inc(filled, 16)
                    sp.wait_ge(filled, 16 * 2)

                @block.tensor
                def _(pe):
                    norm_pe(pe)

                @block.scalar
                def _(act):
                    norm_act(act)

                @block.vector
                def _(dve):
                    norm_dve(dve)
            end_phase()

        win = wb[:, 0:WW_COLS]
        load_phase(win)
        window_phase(win)
        decoder_input_phase()
        far = nc.values_load(flag_i[0:1, 0:1], min_val=0, max_val=1)
        with nc.Fori(0, LAYERS) as layer:
            self_attention_phase(layer)
            with nc.If(far < 1):
                nc.gpsimd.nop()
                nc.sync.nop()
                near_phase()
            with nc.Else():
                nc.gpsimd.nop()
                nc.sync.nop()
                far_path()
            feed_forward_phase(layer)
        route_phase()
        experts_phase()


def constants():
    con = np.zeros((P, C_COLS), np.float32)
    i = np.arange(P)
    con[:, C_ID:C_ID + P] = np.eye(P)
    con[:, C_MEAN:C_MEAN + P] = 1.0 / D
    con[:, C_MASKT:C_MASKT + P] = np.where(i[:, None] > i[None, :], NEG, 0.0)
    con[:, C_MASKQ:C_MASKQ + P] = np.where(i[None, :] > i[:, None], NEG, 0.0)
    con[:, C_NEGI:C_NEGI + P] = np.eye(P) * WIN_NEG
    for w in range(WH):
        con[w * WD:(w + 1) * WD, C_HM + w] = 1.0
    ahead = np.arange(T)[None, :] - i[:, None]
    con[:, C_REL:C_REL + T] = np.where(ahead < 0, 1e9, ahead)
    con[:, C_EPS5], con[:, C_EPS6], con[:, C_ONE] = 1e-5, 1e-6, 1.0

    tab = np.zeros((P, R_COLS + E * P), np.float32)
    f = i // H
    inv = (1.0 / np.float32(10000.0) ** (np.arange(0, HD, 2, dtype=np.float32) / np.float32(HD))).astype(np.float32)
    angle = (np.arange(T, dtype=np.float32)[None, :] * inv[f % (HD // 2)][:, None]).astype(np.float32)
    tab[:, R_COS:R_COS + T] = np.cos(angle)
    tab[:, R_SIN:R_SIN + T] = np.sin(angle) * np.where(f < HD // 2, -1.0, 1.0)[:, None]
    for hh in range(H):
        tab[hh * HD:(hh + 1) * HD, R_HM16 + hh] = 1.0
    for g in range(QUADS):
        for j in range(4):
            c0 = R_VMASK + g * D + (4 * g + j) * HD
            tab[NEAR * j:NEAR * (j + 1), c0:c0 + HD] = 1.0
    tab[:, R_IOTA:R_IOTA + P] = i[None, :]
    tab[:, R_TRI:R_TRI + P] = i[None, :] < i[:, None]
    tab[:, R_OFFD:R_OFFD + P] = i[None, :] != i[:, None]
    tab[:, R_EREV:R_EREV + E] = E - np.arange(E)
    for e in range(E):
        for a in range(3):
            tab[a * E + e, R_COLS + e * P:R_COLS + (e + 1) * P] = 1.0
    return con, tab


def layout(v):
    a = {k: np.asarray(x) for k, x in v.items()}
    con, tab = constants()
    col = lambda x: np.asarray(x).reshape(-1, 1)
    wide = lambda x: np.broadcast_to(np.asarray(x).reshape(1, -1), (P, np.size(x)))

    win = np.zeros((P, WW_COLS), np.float32)
    wt, wbias = a["L0_attn_qkv_w"].T, a["L0_attn_qkv_b"]
    win[:, 0:3 * D] = wt
    win[:, WW_BV:WW_BV + D] = wide(wbias[2 * D:])
    win[:, WW_OFF:WW_OFF + WD] = a["L0_attn_off_w"].T
    win[:, WW_SM], win[:, WW_SM + 1] = wbias[0:D], wbias[D:2 * D]
    win[0:WD, WW_SM + 2] = a["L0_attn_lin2_w"][0]
    win[:, WW_SM + 3] = a["L0_attn_lin2_b"][0]

    f, head = np.meshgrid(np.arange(HD), np.arange(H), indexing="ij")
    order = (head * HD + f).ravel()
    swapped = (head * HD + (f + HD // 2) % HD).ravel()
    la = np.zeros((LAYERS + 1, P, WA_COLS), np.float32)
    lb = np.zeros((LAYERS, P, WB_COLS), np.float32)
    for n in range(LAYERS):
        w, b = a["L0_xattn_Wqkv"][n], a["L0_xattn_bqkv"][n]
        la[n] = np.concatenate(
            [w[order].T, w[swapped].T, w[D + order].T, w[D + swapped].T, w[2 * D:].T, wide(b[2 * D:]),
             col(a["L0_xattn_n1"][n]), col(b[order]), col(b[swapped]), col(b[D + order]), col(b[D + swapped])], 1)
        kv = a["L0_xattn_Wkv_c"][n]
        down = a["L0_xattn_Wd"][n].T.reshape(FT, P, D).transpose(1, 0, 2).reshape(P, FT * D)
        lb[n] = np.concatenate(
            [a["L0_xattn_Wo"][n].T, a["L0_xattn_Wq_c"][n].T, kv[:D].T, kv[D:].T, a["L0_xattn_Wo_c"][n].T,
             col(a["L0_xattn_bo"][n]), col(a["L0_xattn_n2"][n]), col(a["L0_xattn_n3"][n]),
             a["L0_xattn_Wg"][n].T, a["L0_xattn_Wu"][n].T, down], 1)
    mem = np.zeros((P, MEM_BLOCKS * KEYS), np.float32)
    mem[:, :S_MEM] = a["ctx_1024"][0].T
    router = np.concatenate([a["L0_ffn_Wr"], wide(a["L0_ffn_br"]),
                             a["L0_ffn_b1"].reshape(E * MT, P).T], 1)
    seg = a["itok_BxS_0_255"][0]
    return {
        "x_t": a["x"][0].T, "seg_row": seg[None, :], "seg_col": seg.reshape(NT, P).T,
        "consts": con, "tables": tab, "win_w": win,
        "mem_t": mem.reshape(P, MEM_BLOCKS, KEYS).transpose(1, 0, 2),
        "layer_a": la, "layer_b": lb, "router": router, "w1": a["L0_ffn_W1"],
        "w2": a["L0_ffn_W2"].reshape(E, MT, P, D).transpose(0, 2, 1, 3).reshape(E, P, MT * D),
        "b2": a["L0_ffn_b2"], "nf": col(a["L0_xattn_nf"]),
        "fill": np.repeat(np.array([[0]] * ZERO_ROWS + [[0x3F803F80]] * 3, np.int32), H * T // 2, 1),
    }


def kernel(**inputs):
    import concourse.bacc as _bacc
    from concourse.bass_utils import run_bass_kernel_spmd as _run

    nc = _bacc.Bacc("TRN2", target_bir_lowering=False, num_devices=1)
    arrays, args = {}, {}
    for name, a in layout(inputs).items():
        a = np.ascontiguousarray(a)
        arrays[f"in_{name}_dram"] = a
        args[name] = nc.dram_tensor(f"in_{name}_dram", a.shape, mybir.dt.from_np(a.dtype), kind="ExternalInput").ap()
    out = nc.dram_tensor("out_dram", (P, T), F32, kind="ExternalOutput").ap()
    build(nc, out=out, **args)
    r = _run(nc, [arrays], core_ids=[0])
    return np.ascontiguousarray(r.results[0]["out_dram"].T)[None]
```

```python
from contextlib import ExitStack

import numpy as np

import concourse.bass as bass
from concourse import mybir

ALU = mybir.AluOpType
ACT = mybir.ActivationFunctionType
F32 = mybir.dt.float32
BF16 = mybir.dt.bfloat16
I32 = mybir.dt.int32
AX_X = mybir.AxisListType.X

P = 128
T = 1024
D = 128
NT = T // P
CH = 512
NCH = T // CH
TPC = CH // P
WINDOWS = (4, 16, 64, 32)
WH = len(WINDOWS)
WD = D // WH
LAYERS = 4
LN_EXP = "natural_log_exp_and_others"
H = 16
HD = D // H
QUADS = H // 4
S_MEM = 6404
KEYS = P
MEM_BLOCKS = -(-S_MEM // KEYS)
NEAR = 32
LOOKBACK = 128
F = 512
FT = F // P
NEG = -float(2 ** 100)
NEG_PAD = -float(2 ** 120)
WIN_NEG = -float(2 ** 60)
E = 8
TOPK = 2
CAP = 154
MF = 512
MT = MF // P

Q_PART = (0, 1, 2, 0, 1, 0)
K_PART = (0, 0, 0, 1, 1, 2)
SLOTS = len(Q_PART)
ZERO_ROWS = 24
MAX_ROW = SLOTS * HD + ZERO_ROWS
KROWS = MAX_ROW + 3
IDLE_PRODUCTS = 20


def columns(*widths):
    return [sum(widths[:i]) for i in range(len(widths) + 1)]


C_ID, C_MEAN, C_MASKQ, C_NEGI, C_HM, C_REL, C_EPS5, C_EPS6, C_COLS = columns(P, P, P, P, WH, T, 1, 1)
R_COS, R_SIN, R_HM16, R_VMASK, R_IOTA, R_TRI, R_OFFD, R_EREV, R_COLS = columns(
    T, T, H, D * QUADS, P, P, P, E)
WA_QK, WA_V, WA_BV, WA_SM, WA_COLS = columns(4 * D, D, D, 5)
SM_N1, SM_BQ = 0, 1
WB_O, WB_QC, WB_KC, WB_VC, WB_OC, WB_SM, WB_G, WB_U, WB_DN, WB_COLS = columns(D, D, D, D, D, 3, F, F, F)
SM_BO, SM_N2, SM_N3 = 0, 1, 2
WW_Q, WW_K, WW_V, WW_BV, WW_OFF, WW_SM, WW_COLS = columns(D, D, D, D, WD, 4)
RT_W, RT_B, RT_B1, RT_COLS = columns(E, E, E * MT)


UNITS = [(0, 0), (1, 0), (0, 1), (2, 0), (1, 1), (2, 1), (3, 1), (3, 0)]


def attention_steps():
    maxima = []
    for u, (g, c) in enumerate(UNITS):
        mine = []
        for t in range(TPC * c, TPC * (c + 1)):
            if c:
                mine += [("max", u, t, ((j, 0, CH, 0),), 1, 0.22) for j in range(4)]
            first = c * CH
            width = P * (t % TPC + 1)
            per = CH // width
            for j0 in range(0, 4, per):
                mine.append(("max", u, t, tuple((j0 + i, first, width, i * width) for i in range(per)), 0,
                             0.055 * per + width * per * 0.215 / CH))
        if u:
            mine.insert(1, ("maxT", u - 1))
        maxima += mine
    maxima.append(("maxT", len(UNITS) - 1))
    products = []
    item = 0
    pend = None
    for u, (g, c) in enumerate(UNITS):
        blocks = TPC * (c + 1)
        for kb in range(blocks):
            share = ((c + 1) * CH - max(c * CH, kb * P)) / CH
            products += [("score", 2 * item + pair, item, u, kb, pair, share) for pair in range(2)]
            if pend:
                products.append(pend)
            pend = ("value", item, u, kb, kb == blocks - 1, share)
            item += 1
    products.append(pend)

    pe = dve = act = 0.0
    ring, probs = [], []
    rows, outs = {}, []
    steps = []
    while maxima or products or outs:
        free = ring[-3] if len(ring) >= 3 else 0.0
        options = []
        if outs:
            options.append((max(pe, free, outs[0][0]), 0, "out"))
        if maxima:
            ready = max(pe, free, dve + 0.3 if maxima[0][0] == "maxT" else 0.0)
            options.append((ready, 1, "max"))
        if products:
            q = products[0]
            if q[0] == "score":
                if q[3] in rows:
                    options.append((max(pe, rows[q[3]], probs[-2] if len(probs) >= 2 else 0.0), 2, "product"))
            else:
                diag = 0.7 if q[3] >= TPC * UNITS[q[2]][1] else 0.0
                options.append((max(pe, probs[2 * q[1] + 1] + diag), 2, "product"))
        start, _, kind = min(options)
        n = len(ring)
        if kind == "out":
            _, u = outs.pop(0)
            steps.append(("outT", n, u))
            pe = start + 0.45
            dve = max(dve, pe + 0.2) + 1.1
            ring.append(dve)
        elif kind == "max" and maxima[0][0] == "max":
            _, u, t, parts, full, cost = maxima.pop(0)
            steps.append(("max", n, u, t, parts, full))
            pe = start + cost
            dve = max(dve, pe + 0.2) + 0.61
            ring.append(dve)
        elif kind == "max":
            _, u = maxima.pop(0)
            steps.append(("maxT", n, u))
            pe = start + 0.1
            dve = max(dve, pe + 0.2) + 0.7
            ring.append(dve)
            rows[u] = dve + 4.5
        elif products[0][0] == "score":
            *step, share = products.pop(0)
            steps.append(tuple(step))
            pe = start + 0.45 * share
            act = max(act, pe + 0.2) + 0.9 * share + 0.05
            probs.append(act + 0.1)
        else:
            *step, share = products.pop(0)
            steps.append(tuple(step))
            pe = start + 0.87 * share + 0.05
            if step[4]:
                act = max(act, pe + 0.2) + 0.6
                outs.append((act + 0.1, step[2]))
    return steps


def build(nc, x_t, seg_row, seg_col, consts, tables, win_w, mem_t, layer_a, layer_b, router, w1, w2,
          b2, nf, fill, out):
    ctx = ExitStack()

    def sb(name, shape, dt=F32):
        return ctx.enter_context(nc.sbuf_tensor(name, shape, dt))

    with ctx:
        ps = ctx.enter_context(nc.psum_tensor("ps", [P, 8, CH], F32))
        con = sb("con", [P, C_COLS])
        tab = sb("tab", [P, R_COLS])
        id_b = sb("id_b", [P, P], BF16)
        mask_q = sb("mask_q", [P, P], BF16)
        neg_i = sb("neg_i", [P, P], BF16)
        ident, mean_w = con[:, C_ID:C_ID + P], con[:, C_MEAN:C_MEAN + P]
        head_mask = con[:, C_HM:C_HM + WH]
        rel = con[:, C_REL:C_REL + T]
        eps5, eps6 = con[:, C_EPS5:C_EPS5 + 1], con[:, C_EPS6:C_EPS6 + 1]
        cos_t, sin_t = tab[:, R_COS:R_COS + T], tab[:, R_SIN:R_SIN + T]
        wa = sb("wa", [P, WA_COLS])
        wb = sb("wb", [P, WB_COLS])
        nf_col = sb("nf_col", [P, 1])
        x_res = sb("x_res", [P, T])
        x_dec = sb("x_dec", [P, T])
        h = sb("h", [P, T])
        cen = sb("cen", [P, T])
        sq = sb("sq", [P, T])
        rs = sb("rs", [P, T])
        big = sb("big", [P, 32 * T], BF16)
        q_x = big[:, 0:16 * T].rearrange("p (c h t) -> p c h t", c=NCH, h=H)
        k_x = big[:, 16 * T:32 * T].rearrange("p (c h t) -> p c h t", c=NCH, h=H)
        parts = sb("parts", [P, 2, 3, T], BF16)
        qk = sb("qk", [P, 2, T])
        tmp = sb("tmp", [P, 2, CH])
        v_aug = sb("v_aug", [P, NT, H, 32])
        prob = sb("prob", [P, 4, 2, CH])
        o_t = sb("o_t", [P, CH])
        o_n = sb("o_n", [P, NT, D])
        o_d = sb("o_d", [P, T])
        max_q = sb("max_q", [P, 2, 4, TPC])
        max_f = sb("max_f", [P, 2, 4, TPC])
        max_s = sb("max_s", [4 * TPC, P])
        max_p = sb("max_p", [4 * TPC, 2, 3, P], BF16)
        den = sb("den", [P, 4, 4])
        seg_q = sb("seg_q", [P, NT])
        mask_near = sb("mask_near", [P, NT, NEAR], BF16)
        flag = sb("flag", [1, 8])
        flag_i = sb("flag_i", [1, 1], I32)

        names = {}

        def sem(name):
            if name not in names:
                names[name] = pool[len(names)]
            return names[name]

        pool = [ctx.enter_context(nc.semaphore(f"phase_sem{i}")) for i in range(44)]
        first_sem, last_sem = pool[0].num, pool[-1].num
        loaded = ctx.enter_context(nc.semaphore("loaded"))
        experts_got = ctx.enter_context(nc.semaphore("experts_got"))
        seg_i = tmp[:, 0, 0:NT].bitcast(I32)
        seg_r = qk[0:1, 0, :].bitcast(I32)
        seg_f = qk[0:1, 1, :]

        def phase():
            names.clear()
            return nc.Block(no_gpsimd_drain=True)

        def end_phase():
            nc.all_engine_barrier(sems_to_clear=range(first_sem, last_sem + 1))

        def chain(eng, name):
            s, n = sem(name), [0]

            def link(ins):
                n[0] += 1
                ins.then_inc(s, 1)
                eng.wait_ge(s, n[0])
            return link

        def keep_busy(bank):
            nc.tensor.matmul(ps[:, bank, :].rearrange("p (j k) -> p j k", j=TPC), id_b[:, :],
                             mask_q[:, :].unsqueeze(1).broadcast_to([P, TPC, P]),
                             start=True, stop=True)

        def chunk(c):
            return slice(c * CH, (c + 1) * CH)

        def tile(t):
            return slice(t * P, (t + 1) * P)

        def norm(tag, src, dst, layer, eps, weight=None, made=None):
            centred, squared, mean_ps, var_ps = (
                sem(tag + x) for x in ("_centred", "_squared", "_mean_ps", "_var_ps"))
            logged, root, ready = (sem(tag + x) for x in ("_logged", "_root", "_ready"))
            x = cen if layer else src

            def on_pe(pe):
                if layer:
                    for c in range(NCH):
                        if made is not None:
                            pe.wait_ge(made, c + 1)
                        nc.tensor.matmul(ps[:, 4 + c, :], mean_w, src[:, chunk(c)], start=True,
                                         stop=True).then_inc(mean_ps, 1)
                for c in range(NCH):
                    pe.wait_ge(squared, c + 1)
                    nc.tensor.matmul(ps[:, 6 + c, :], mean_w, sq[:, chunk(c)], start=True,
                                     stop=True).then_inc(var_ps, 1)

            def on_act(act):
                for c in range(NCH):
                    if layer:
                        act.wait_ge(centred, c + 1)
                    elif made is not None:
                        act.wait_ge(made, c + 1)
                    nc.scalar.activation(sq[:, chunk(c)], x[:, chunk(c)], ACT.Square).then_inc(squared, 1)
                for c in range(NCH):
                    act.wait_ge(var_ps, c + 1)
                    nc.scalar.activation(rs[:, chunk(c)], ps[:, 6 + c, :], ACT.Ln,
                                         bias=eps).then_inc(logged, 1)
                    act.wait_ge(logged, c + 1)
                    nc.scalar.activation(rs[:, chunk(c)], rs[:, chunk(c)], ACT.Exp,
                                         scale=-0.5).then_inc(root, 1)

            def on_dve(dve):
                if layer:
                    for c in range(NCH):
                        dve.wait_ge(mean_ps, c + 1)
                        nc.vector.tensor_tensor(cen[:, chunk(c)], src[:, chunk(c)], ps[:, 4 + c, :],
                                                ALU.subtract).then_inc(centred, 1)
                    dve.wait_ge(centred, NCH)
                for c in range(NCH):
                    dve.wait_ge(root, c + 1)
                    if weight is None:
                        nc.vector.tensor_tensor(dst[:, chunk(c)], x[:, chunk(c)], rs[:, chunk(c)],
                                                ALU.mult).then_inc(ready, 1)
                    else:
                        nc.vector.scalar_tensor_tensor(dst[:, chunk(c)], x[:, chunk(c)], weight,
                                                       rs[:, chunk(c)], ALU.mult, ALU.mult).then_inc(ready, 1)
            return (on_pe, on_act, on_dve, ready) if dst is not None else (on_pe, on_act, root)

        def load_phase(win):
            with phase() as block:
                got, cast = sem("got"), sem("cast")

                @block.sync
                def _(sp):
                    sp.dma_start(x_res[:, :], x_t).then_inc(got, 16)
                    sp.dma_start(con[:, :], consts).then_inc(got, 16)
                    sp.dma_start(win[:, :], win_w).then_inc(loaded, 16)
                    sp.dma_start(seg_i, seg_col).then_inc(loaded, 16)
                    sp.dma_start(seg_r, seg_row).then_inc(loaded, 16)
                    sp.dma_start(tab[:, :], tables[:, 0:R_COLS]).then_inc(loaded, 16)
                    sp.dma_start(nf_col[:, :], nf).then_inc(loaded, 16)
                    sp.dma_start(wa[:, :], layer_a[0]).then_inc(loaded, 16)
                    for i in range(4):
                        sp.dma_start(mem4[:, NEAR * i:NEAR * (i + 1)], mem_t[0, :, 0:NEAR]).then_inc(loaded, 16)
                    sp.wait_ge(got, 16 * 2)

                @block.scalar
                def _(act):
                    nc.scalar.preload_act_table_set(LN_EXP)

                @block.gpsimd
                def _(pool_):
                    nc.gpsimd.memset(v_aug[:, :, :, :], 0.0).then_inc(cast, 1)
                    pool_.wait_ge(cast, 1)
                    nc.gpsimd.memset(v_aug[:, :, :, HD:HD + 1], 1.0)

                @block.vector
                def _(dve):
                    dve.wait_ge(got, 16 * 2)
                    nc.vector.tensor_copy(id_b[:, :], ident)
                    nc.vector.tensor_copy(mask_q[:, :], con[:, C_MASKQ:C_MASKQ + P])
                    nc.vector.tensor_copy(neg_i[:, :], con[:, C_NEGI:C_NEGI + P])
            end_phase()

        def segments(v, link):
            v.wait_ge(loaded, 16 * 10)
            link(nc.vector.tensor_copy(seg_q[:, :], seg_i))
            for t in range(NT):
                nc.vector.tensor_scalar(mask_near[:, t, :], tab[:, R_IOTA:R_IOTA + NEAR],
                                        seg_q[:, t:t + 1], NEG, ALU.is_gt, ALU.mult)
            link(nc.vector.tensor_copy(seg_f, seg_r))
            link(nc.vector.tensor_reduce(flag[:, 0:1], seg_f, AX_X, ALU.max))
            link(nc.vector.tensor_reduce(flag[:, 1:2], seg_f, AX_X, ALU.min))
            link(nc.vector.tensor_scalar(flag[:, 2:3], flag[:, 0:1], float(NEAR - 1), None, ALU.is_gt))
            link(nc.vector.tensor_scalar(flag[:, 3:4], flag[:, 1:2], 0.0, None, ALU.is_lt))
            link(nc.vector.tensor_tensor(flag[:, 4:5], flag[:, 2:3], flag[:, 3:4], ALU.max))
            nc.vector.tensor_copy(flag_i[:, :], flag[:, 4:5])

        def window_phase(win):
            q_m = [big[:, 2 * T * i:2 * T * (i + 1)].bitcast(F32) for i in range(WH)]
            k_t = big[:, 8 * T:10 * T].bitcast(F32)
            v_n = big[:, 10 * T:12 * T].bitcast(F32).rearrange("p (t d) -> p t d", t=NT)
            relu = big[:, 12 * T:14 * T].bitcast(F32)
            prob_q = [big[:, 14 * T + 2 * T * i:16 * T + 2 * T * i].bitcast(F32) for i in range(3)]
            hide = [big[:, (20 + i) * T:(21 + i) * T] for i in range(3)]
            off = big[0:WD, 24 * T:26 * T].bitcast(F32)
            more = parts[:, :, :, :].rearrange("p a b t -> p (a b t)").bitcast(F32)
            more = more.rearrange("p (g n) -> p g n", n=CH)
            more2 = o_n[:, :, :].rearrange("p a b -> p (a b)").rearrange("p (g n) -> p g n", n=CH)
            prob_t = ([prob[:, i // 2, i % 2, :] for i in range(8)] + [more[:, i, :] for i in range(6)]
                      + [more2[:, i, :] for i in range(2)])
            slots = len(prob_t)
            dx = sb("dx", [P, 1 + WH, NT])
            bq_m = sb("bq_m", [P, WH])
            wmax = sb("wmax", [P, 2, WH * NT])
            wbias = sb("wbias", [P, WH * NT])
            wsum = sb("wsum", [P, WH * NT])
            wrec = sb("wrec", [P, WH * NT])
            scale = 2.0 / float(np.sqrt(T))
            units = [(t, i) for t in range(NT) for i in range(WH)]

            with phase() as block:
                proj, proj_out = sem("proj"), sem("proj_out")
                relu_ok, off_ps, off_ok, z_ps, dx_ok = (
                    sem(x) for x in ("relu_ok", "off_ps", "off_ok", "z_ps", "dx_ok"))
                norm_pe, norm_act, norm_dve, h_ok = norm("norm", x_res, h, True, eps5)
                hide_ok = [sem("hide_even"), sem("hide_odd")]
                s_ps, p_ok, p_n = sem("s_ps"), sem("p_ok"), sem("p_n")
                m_ok, pt_ps, pt_ok, o_ps, o_ok = (sem(x) for x in ("m_ok", "pt_ps", "pt_ok", "o_ps", "o_ok"))

                groups = []
                for n, (t, i) in enumerate(units):
                    w = NT - t
                    for b in range(0, w, 4):
                        groups.append((len(groups), n, b, min(4, w - b)))
                by_unit = {n: [g for g in groups if g[1] == n] for n in range(len(units))}

                @block.tensor
                def _(pe):
                    norm_pe(pe)
                    pe.wait_ge(h_ok, NCH)
                    pe.wait_ge(loaded, 16 * 10)
                    def project(j, col):
                        for c in range(NCH):
                            nc.tensor.matmul(ps[:, 2 * j + c, :], win[:, col:col + D], h[:, chunk(c)],
                                             start=True, stop=True).then_inc(proj, 1)

                    project(0, WW_K)
                    for c in range(NCH):
                        pe.wait_ge(relu_ok, c + 1)
                        nc.tensor.matmul(ps[0:WD, 6 + c, :], win[:, WW_OFF:WW_OFF + WD], relu[:, chunk(c)],
                                         start=True, stop=True).then_inc(off_ps, 1)
                    project(1, WW_Q)
                    pe.wait_ge(off_ok, NCH)
                    for t in range(NT):
                        mm = nc.tensor.matmul(ps[:, 6, t:t + 1], off[:, tile(t)],
                                              win[0:WD, WW_SM + 2:WW_SM + 3], start=True, stop=True)
                    mm.then_inc(z_ps, 1)
                    for c in range(NCH):
                        for t in range(TPC):
                            mm = nc.tensor.matmul(ps[:, 4 + c, tile(t)], h[:, tile(TPC * c + t)],
                                                  win[:, WW_V:WW_V + D], start=True, stop=True)
                        mm.then_inc(proj, 1)

                    def scores(n):
                        t, i = units[n]
                        if t == 0:
                            pe.wait_ge(proj_out, (2, 3, 6, 7)[i])
                        if n == 1:
                            pe.wait_ge(proj_out, 7)
                        if n >= 2:
                            pe.wait_ge(p_ok, n - 1)
                        pe.wait_ge(hide_ok[n % 2], n // 2 + 1)
                        w = T - t * P
                        for b in range(0, w, CH):
                            nn = min(CH, w - b)
                            bank = ps[:, 2 * (n % 2) + b // CH, 0:nn]
                            nc.tensor.matmul(bank, q_m[i][:, tile(t)], k_t[:, t * P + b:t * P + b + nn],
                                             start=True, stop=False)
                            mm = nc.tensor.matmul(bank, neg_i[:, :], hide[n % 3][:, b:b + nn],
                                                  start=False, stop=True)
                        mm.then_inc(s_ps, 1)

                    def turn(n):
                        pe.wait_ge(p_n, n + 1)
                        for g, _, b, cnt in by_unit[n]:
                            if g >= 2:
                                pe.wait_ge(pt_ok, g - 1)
                            for k in range(cnt):
                                mm = nc.tensor.transpose(ps[:, 4 + g % 2, tile(k)],
                                                         prob_q[n % 3][:, tile(b + k)], ident)
                            mm.then_inc(pt_ps, 1)

                    def values(t):
                        if t >= 2:
                            pe.wait_ge(o_ok, t - 1)
                        mine = [by_unit[WH * t + i] for i in range(WH)]
                        pe.wait_ge(pt_ok, mine[-1][-1][0] + 1)
                        for b in range(NT - t):
                            for i in range(WH):
                                g = mine[i][b // 4][0]
                                mm = nc.tensor.matmul(ps[i * WD:(i + 1) * WD, 6 + t % 2, 0:P],
                                                      v_n[:, t + b, i * WD:(i + 1) * WD],
                                                      prob_t[g % slots][:, tile(b % 4)],
                                                      start=(b == 0), stop=(b == NT - t - 1),
                                                      tile_position=(0, i * WD))
                        mm.then_inc(o_ps, 1)

                    pe.wait_ge(dx_ok, 1)
                    scores(0)
                    scores(1)
                    for n in range(len(units) + 1):
                        if n + 2 < len(units):
                            scores(n + 2)
                        if n < len(units):
                            turn(n)
                        if n >= WH and n % WH == 0:
                            values(n // WH - 1)

                @block.gpsimd
                def _(pool_):
                    pool_.wait_ge(dx_ok, 1)
                    for n in range(1, len(units), 2):
                        t, i = units[n]
                        w = T - t * P
                        if n >= 3:
                            pool_.wait_ge(s_ps, n - 2)
                        nc.gpsimd.tensor_scalar(hide[n % 3][:, 0:w], rel[:, 0:w], dx[:, 1 + i, t:t + 1], None,
                                                ALU.is_gt).then_inc(hide_ok[1], 1)

                @block.scalar
                def _(act):
                    norm_act(act)
                    for c in range(NCH):
                        act.wait_ge(h_ok, c + 1)
                        nc.scalar.activation(relu[:, chunk(c)], h[:, chunk(c)], ACT.Relu).then_inc(relu_ok, 1)
                    act.wait_ge(off_ps, NCH)
                    for c in range(NCH):
                        ins = nc.scalar.copy(off[:, chunk(c)], ps[0:WD, 6 + c, :]).then_inc(off_ok, 1)
                    act.wait_ge(z_ps, 1)
                    nc.scalar.activation(dx[:, 0, :], ps[:, 6, 0:NT], ACT.Sigmoid,
                                         bias=win[:, WW_SM + 3:WW_SM + 4]).then_inc(z_ps, 1)
                    nc.scalar.preload_act_table_set(LN_EXP)

                    def exps(n):
                        t, i = units[n]
                        w = T - t * P
                        act.wait_ge(m_ok, n + 1)
                        if n >= 3:
                            act.wait_ge(pt_ps, by_unit[n - 3][-1][0] + 1)
                        if w > CH:
                            src = ps[:, 2 * (n % 2):2 * (n % 2) + 2, :].rearrange("p a b -> p (a b)")[:, 0:w]
                        else:
                            src = ps[:, 2 * (n % 2), 0:w]
                        nc.scalar.activation(prob_q[n % 3][:, 0:w], src, ACT.Exp, bias=wbias[:, n:n + 1],
                                             scale=scale, accum_out=wsum[:, n:n + 1]).then_inc(p_ok, 1)

                    def take(n):
                        for g, _, b, cnt in by_unit[n]:
                            act.wait_ge(pt_ps, g + 1)
                            if g >= slots:
                                act.wait_ge(o_ps, groups[g - slots][1] // WH + 1)
                            nc.scalar.copy(prob_t[g % slots][:, 0:cnt * P], ps[:, 4 + g % 2, 0:cnt * P]
                                           ).then_inc(pt_ok, 1)

                    for n in range(len(units) + 1):
                        if n < len(units):
                            exps(n)
                        if n >= 1:
                            take(n - 1)

                @block.vector
                def _(dve):
                    link = chain(dve, "dve_step")
                    norm_dve(dve)
                    segments(dve, link)
                    link(nc.vector.tensor_scalar(bq_m[:, :], head_mask, win[:, WW_SM:WW_SM + 1], None, ALU.mult))
                    dve.wait_ge(proj, 2)
                    nc.vector.tensor_scalar(k_t[:, :], ps[:, 0:2, :].rearrange("p a b -> p (a b)"),
                                            win[:, WW_SM + 1:WW_SM + 2], None, ALU.add).then_inc(proj_out, 1)

                    def mask_q(i):
                        nc.vector.tensor_scalar(q_m[i][:, :], ps[:, 2:4, :].rearrange("p a b -> p (a b)"),
                                                head_mask[:, i:i + 1], bq_m[:, i:i + 1], ALU.mult, ALU.add
                                                ).then_inc(proj_out, 1)

                    dve.wait_ge(proj, 4)
                    mask_q(0)
                    dve.wait_ge(z_ps, 2)
                    for i in range(WH):
                        link(nc.vector.tensor_scalar(dx[:, 1 + i, :], dx[:, 0, :], float(T), float(WINDOWS[i]),
                                                     ALU.mult, ALU.add))
                    nc.vector.tensor_copy(dx[:, 0, :], dx[:, 1, :]).then_inc(dx_ok, 1)

                    def hide_keys(n):
                        t, i = units[n]
                        w = T - t * P
                        if n >= 3:
                            dve.wait_ge(s_ps, n - 2)
                        nc.vector.tensor_scalar(hide[n % 3][:, 0:w], rel[:, 0:w], dx[:, 1 + i, t:t + 1], None,
                                                ALU.is_gt).then_inc(hide_ok[0], 1)

                    hide_keys(0)
                    mask_q(1)
                    dve.wait_ge(proj, 6)
                    bv = win[:, WW_BV:WW_BV + D].unsqueeze(1).broadcast_to([P, TPC, D])
                    for c in range(NCH):
                        nc.vector.tensor_tensor(v_n[:, TPC * c:TPC * (c + 1), :],
                                                ps[:, 4 + c, :].rearrange("p (t d) -> p t d", t=TPC), bv,
                                                ALU.add).then_inc(proj_out, 1)
                    mask_q(2)
                    mask_q(3)

                    def maxima(n):
                        t, i = units[n]
                        w = T - t * P
                        dve.wait_ge(s_ps, n + 1)
                        if w > CH:
                            src = ps[:, 2 * (n % 2):2 * (n % 2) + 2, :].rearrange("p a b -> p (a b)")[:, 0:w]
                        else:
                            src = ps[:, 2 * (n % 2), 0:w]
                        link(nc.vector.tensor_reduce(wmax[:, 0, n:n + 1], src, AX_X, ALU.max))
                        nc.vector.tensor_scalar(wbias[:, n:n + 1], wmax[:, 0, n:n + 1], -scale, None,
                                                ALU.mult).then_inc(m_ok, 1)

                    def normalise(n):
                        t, i = units[n]
                        w = T - t * P
                        dve.wait_ge(p_ok, n + 1)
                        link(nc.vector.reciprocal(wrec[:, n:n + 1], wsum[:, n:n + 1]))
                        nc.vector.tensor_scalar(prob_q[n % 3][:, 0:w], prob_q[n % 3][:, 0:w], wrec[:, n:n + 1],
                                                None, ALU.mult).then_inc(p_n, 1)

                    def add_out(t):
                        dve.wait_ge(o_ps, t + 1)
                        nc.vector.tensor_tensor(x_res[:, tile(t)], x_res[:, tile(t)], ps[:, 6 + t % 2, 0:P],
                                                ALU.add).then_inc(o_ok, 1)

                    for n in range(len(units) + 1):
                        if n < len(units):
                            maxima(n)
                        if n % 2 == 0 and n + 2 < len(units):
                            hide_keys(n + 2)
                        if n >= 1:
                            normalise(n - 1)
                        if n >= 6 and (n - 6) % WH == 0:
                            add_out((n - 6) // WH)
                    add_out(NT - 1)
            end_phase()

        def self_attention_phase(layer):
            steps = attention_steps()
            scale = HD ** -0.5
            heads = [slice(4 * g, 4 * g + 4) for g in range(QUADS)]
            closed = [s[1] for s in steps if s[0] == "value" and s[4]]
            first_score = max(s[1] for s in steps[:[s[0] for s in steps].index("score")]) + 1
            out_n = {s[2]: s[1] for s in steps if s[0] == "outT"}
            diagonal = [s[1] for s in steps if s[0] == "value" and s[3] >= TPC * UNITS[s[2]][1]]
            with phase() as block:
                wb_ok, proj, took, roped = sem("wb_ok"), sem("proj"), sem("took"), sem("roped")
                part1, part2, part3 = sem("part1"), sem("part2"), sem("part3")
                rest = [sem(f"rest{c}") for c in range(NCH)]
                spread = [sem(f"spread{c}") for c in range(NCH)]
                v_ps, v_ok = sem("v_ps"), sem("v_ok")
                ring_in, ring_out = sem("ring_in"), sem("ring_out")
                max_ok, max_split = sem("max_ok"), sem("max_split")
                max_rows = [sem(f"max_rows{u % 2}") for u in range(len(UNITS))]
                score_in, prob_ok, causal_ok, value_ok = (
                    sem(x) for x in ("score_in", "prob_ok", "causal_ok", "value_ok"))
                ot_ok = sem("ot_ok")
                turned, taken, made = sem("turned"), sem("taken"), sem("made")
                norm_pe, norm_act, norm_dve, h_ok = norm(
                    "norm1", x_dec, h, False, eps6, wa[:, WA_SM + SM_N1:WA_SM + SM_N1 + 1])
                turn_bank, made_bank = (4, 3), (0, 5)

                @block.sync
                def _(sp):
                    sp.dma_start(wb[:, :], layer_b[bass.ds(layer, 1), :, :].rearrange("a p n -> (a p) n")
                                 ).then_inc(wb_ok, 16)
                    for c in range(NCH):
                        for i, (dst, part_of) in enumerate(((q_x, Q_PART), (k_x, K_PART))):
                            for want, ready in enumerate((part1, part2, part3)):
                                sp.wait_ge(ready, 2 * c + i + 1)
                                for s in range(SLOTS):
                                    if part_of[s] == want:
                                        sp.dma_start(dst[s * HD:(s + 1) * HD, c, :, :],
                                                     parts[:, i, want, chunk(c)]).then_inc(spread[c], 16)
                    for u, (g, c) in enumerate(UNITS):
                        sp.wait_ge(max_split, u + 1)
                        for k in range(3):
                            sp.dma_start(q_x[MAX_ROW + k:MAX_ROW + k + 1, c, heads[g], :],
                                         max_p[:, u % 2, k, :]).then_inc(max_rows[u], 16)
                    sp.wait_ge(wb_ok, 16)

                @block.tensor
                def _(pe):
                    norm_pe(pe)
                    for c in range(NCH):
                        pe.wait_ge(h_ok, c + 1)
                        for i in range(4):
                            nc.tensor.matmul(ps[:, 4 * c + i, :], wa[:, WA_QK + i * D:WA_QK + (i + 1) * D],
                                             h[:, chunk(c)], start=True, stop=True).then_inc(proj, 1)
                    for c in range(NCH):
                        pe.wait_ge(took, 4)
                        for t in range(TPC):
                            mm = nc.tensor.matmul(ps[:, c, tile(t)], h[:, tile(TPC * c + t)],
                                                  wa[:, WA_V:WA_V + D], start=True, stop=True)
                        mm.then_inc(v_ps, 1)

                    for _ in range(IDLE_PRODUCTS):
                        keep_busy(3)
                    pe.wait_ge(took, 8)
                    pe.wait_ge(v_ok, NCH)

                    def turn_output(c):
                        pe.wait_ge(prob_ok, 2 * closed[-1] + 2)
                        pe.wait_ge(ring_out, max(n for u, n in out_n.items() if UNITS[u][1] == c) + 1)
                        for t in range(TPC):
                            mm = nc.tensor.transpose(ps[:, turn_bank[c], tile(t)], o_n[:, TPC * c + t, :],
                                                     ident)
                        mm.then_inc(turned, 1)

                    ready = set()
                    for s in steps:
                        if s[0] in ("max", "maxT", "outT"):
                            n, u = s[1], s[2]
                            g, c = UNITS[u]
                            bank = n % 3
                            if n >= 3:
                                pe.wait_ge(ring_out, n - 2)
                        if s[0] == "max":
                            t, parts_, full = s[3:]
                            if c not in ready:
                                pe.wait_ge(spread[c], 16 * 2 * SLOTS)
                                ready.add(c)
                            for j, k0, width, col in parts_:
                                mm = nc.tensor.matmul(ps[:, bank, col:col + width],
                                                      q_x[0:MAX_ROW, c, 4 * g + j, tile(t % TPC)],
                                                      k_x[0:MAX_ROW, k0 // CH, 4 * g + j,
                                                          k0 % CH:k0 % CH + width],
                                                      start=True, stop=bool(full))
                                if not full:
                                    mm = nc.tensor.matmul(ps[:, bank, col + width - P:col + width], id_b[:, :],
                                                          mask_q[:, :], start=False, stop=True)
                            mm.then_inc(ring_in, 1)
                            if n < first_score:
                                keep_busy(7)
                        elif s[0] == "maxT":
                            pe.wait_ge(max_ok, u + 1)
                            nc.tensor.transpose(ps[0:4 * TPC, bank, 0:P],
                                                max_q[:, u % 2, :, :].rearrange("p j t -> p (j t)"), ident
                                                ).then_inc(ring_in, 1)
                        elif s[0] == "outT":
                            if u == len(UNITS) - 1:
                                turn_output(1)
                            pe.wait_ge(ot_ok, u + 1)
                            for t in range(TPC):
                                mm = nc.tensor.transpose(ps[:, bank, tile(t)], o_t[:, tile(t)], ident)
                            mm.then_inc(ring_in, 1)
                        elif s[0] == "score":
                            _, m, item, u, kb, pair = s
                            g, c = UNITS[u]
                            if kb == 0 and pair == 0:
                                pe.wait_ge(max_rows[u], 48 * (u // 2 + 1))
                            if m >= 2:
                                pe.wait_ge(prob_ok, m - 1)
                            q0 = max(c * CH, kb * P)
                            width = (c + 1) * CH - q0
                            for i in range(2):
                                j = 4 * g + 2 * pair + i
                                bank = ps[:, 3 + 2 * (m % 2) + i, 0:width]
                                mm = nc.tensor.matmul(bank, k_x[0:KROWS, kb // TPC, j, tile(kb % TPC)],
                                                      q_x[0:KROWS, c, j, q0 - c * CH:CH], start=True,
                                                      stop=True)
                            mm.then_inc(score_in, 1)
                        else:
                            _, item, u, kb, last = s
                            g, c = UNITS[u]
                            pe.wait_ge(prob_ok, 2 * item + 2)
                            if kb >= TPC * c:
                                pe.wait_ge(causal_ok, 2 * diagonal.index(item) + 2)
                            if kb == 0 and u:
                                pe.wait_ge(ot_ok, u)
                            q0 = max(c * CH, kb * P)
                            width = (c + 1) * CH - q0
                            for j in range(4):
                                mm = nc.tensor.matmul(ps[32 * j:32 * j + 32, 7, q0 - c * CH:CH],
                                                      v_aug[:, kb, 4 * g + j, :],
                                                      prob[:, 2 * (item % 2) + j // 2, j % 2, 0:width],
                                                      start=(kb == 0), stop=last,
                                                      tile_position=(0, 32 * j))
                            mm.then_inc(value_ok, 1)
                    turn_output(0)
                    for i, c in enumerate((1, 0)):
                        pe.wait_ge(taken, i + 1)
                        if i == 0:
                            pe.wait_ge(wb_ok, 16)
                        nc.tensor.matmul(ps[:, made_bank[c], :], wb[:, WB_O:WB_O + D], o_d[:, chunk(c)],
                                         start=True, stop=True).then_inc(made, 1)

                @block.scalar
                def _(act):
                    norm_act(act)
                    def first_part(n):
                        c, i = n // 2, n % 2
                        act.wait_ge(roped, n + 1)
                        nc.scalar.copy(parts[:, i, 0, chunk(c)], qk[:, i, chunk(c)]).then_inc(part1, 1)

                    def second_part(n):
                        c, i = n // 2, n % 2
                        act.wait_ge(rest[c], i + 1)
                        nc.scalar.copy(parts[:, i, 1, chunk(c)], qk[:, i, chunk(c)]).then_inc(part2, 1)

                    first_part(0)
                    second_part(0)
                    first_part(1)
                    second_part(1)
                    first_part(2)
                    first_part(3)
                    second_part(2)
                    second_part(3)
                    for s in steps:
                        if s[0] == "score":
                            _, m, item, u, kb, pair = s
                            c = UNITS[u][1]
                            act.wait_ge(score_in, m + 1)
                            if item >= 2:
                                act.wait_ge(value_ok, item - 1)
                            width = (c + 1) * CH - max(c * CH, kb * P)
                            b = 3 + 2 * (m % 2)
                            nc.scalar.activation(prob[:, 2 * (item % 2) + pair, :, 0:width],
                                                 ps[:, b:b + 2, 0:width], ACT.Exp, scale=scale
                                                 ).then_inc(prob_ok, 1)
                        elif s[0] == "value" and s[4]:
                            u = s[2]
                            act.wait_ge(value_ok, closed[u] + 1)
                            if u:
                                act.wait_ge(ring_in, out_n[u - 1] + 1)
                            nc.scalar.copy(o_t[:, :], ps[:, 7, :]).then_inc(ot_ok, 1)
                    for i, c in enumerate((1, 0)):
                        act.wait_ge(turned, i + 1)
                        nc.scalar.copy(o_d[:, chunk(c)], ps[:, turn_bank[c], :]).then_inc(taken, 1)

                @block.gpsimd
                def _(pool_):
                    def third_part(n):
                        c, i = n // 2, n % 2
                        pool_.wait_ge(part2, n + 1)
                        nc.gpsimd.tensor_tensor(parts[:, i, 2, chunk(c)], qk[:, i, chunk(c)],
                                                parts[:, i, 1, chunk(c)], ALU.subtract).then_inc(part3, 1)

                    third_part(0)
                    third_part(1)
                    for n in (2, 3):
                        pool_.wait_ge(part1, n + 1)
                        nc.gpsimd.tensor_tensor(qk[:, n - 2, chunk(1)], qk[:, n - 2, chunk(1)],
                                                parts[:, n - 2, 0, chunk(1)], ALU.subtract
                                                ).then_inc(rest[1], 1)
                    third_part(2)
                    third_part(3)
                    zero = nc.gpsimd.to_reg(0.0)
                    for s in steps:
                        if s[0] == "score" and s[4] >= TPC * UNITS[s[3]][1]:
                            _, m, item, u, kb, pair = s
                            pool_.wait_ge(prob_ok, m + 1)
                            block_p = prob[:, 2 * (item % 2) + pair, :, 0:P]
                            nc.gpsimd.affine_select(block_p, block_p, [[0, 2], [1, P]], ALU.is_ge, zero, 0, -1
                                                    ).then_inc(causal_ok, 1)

                @block.vector
                def _(dve):
                    link = chain(dve, "dve_step")
                    norm_dve(dve)

                    def rope(n):
                        c, i = n // 2, n % 2
                        dve.wait_ge(proj, 4 * c + 2 * i + 2)
                        b = wa[:, WA_SM + SM_BQ + 2 * i:WA_SM + SM_BQ + 2 * i + 1]
                        br = wa[:, WA_SM + SM_BQ + 2 * i + 1:WA_SM + SM_BQ + 2 * i + 2]
                        nc.vector.scalar_tensor_tensor(tmp[:, 0, :], ps[:, 4 * c + 2 * i, :], b,
                                                       cos_t[:, chunk(c)], ALU.add, ALU.mult
                                                       ).then_inc(took, 1)
                        nc.vector.scalar_tensor_tensor(tmp[:, 1, :], ps[:, 4 * c + 2 * i + 1, :], br,
                                                       sin_t[:, chunk(c)], ALU.add, ALU.mult
                                                       ).then_inc(took, 1)
                        dve.wait_ge(took, 2 * n + 2)
                        nc.vector.tensor_tensor(qk[:, i, chunk(c)], tmp[:, 0, :], tmp[:, 1, :],
                                                ALU.add).then_inc(roped, 1)
                        dve.wait_ge(roped, n + 1)

                    def remainder(n):
                        c, i = 0, n
                        dve.wait_ge(part1, n + 1)
                        nc.vector.tensor_tensor(qk[:, i, chunk(c)], qk[:, i, chunk(c)],
                                                parts[:, i, 0, chunk(c)], ALU.subtract).then_inc(rest[0], 1)

                    rope(0)
                    remainder(0)
                    rope(1)
                    remainder(1)
                    rope(2)
                    rope(3)
                    bv = wa[:, WA_BV:WA_BV + D].rearrange("p (h d) -> p h d", h=H)
                    bv = bv.unsqueeze(1).broadcast_to([P, TPC, H, HD])
                    for c in range(NCH):
                        dve.wait_ge(v_ps, c + 1)
                        nc.vector.tensor_tensor(v_aug[:, TPC * c:TPC * (c + 1), :, 0:HD],
                                                ps[:, c, :].rearrange("p (t h d) -> p t h d", t=TPC, h=H), bv,
                                                ALU.add).then_inc(v_ok, 1)
                    for s in steps:
                        if s[0] in ("max", "maxT", "outT"):
                            n, u = s[1], s[2]
                            g, c = UNITS[u]
                            bank = n % 3
                            dve.wait_ge(ring_in, n + 1)
                        if s[0] == "max":
                            t, parts_, full = s[3:]
                            j0, _, width, _ = parts_[0]
                            src = ps[:, bank, 0:len(parts_) * width].rearrange("p (j k) -> p j k", k=width)
                            dst = max_f if full else max_q
                            nc.vector.tensor_reduce(dst[:, u % 2, j0:j0 + len(parts_), t % TPC], src, AX_X,
                                                    ALU.max).then_inc(ring_out, 1)
                            if t % TPC == TPC - 1 and not full and j0 + len(parts_) == 4:
                                dve.wait_ge(ring_out, n + 1)
                                other = max_f if c else max_q
                                nc.vector.tensor_tensor(max_q[:, u % 2, :, :], max_q[:, u % 2, :, :],
                                                        other[:, u % 2, :, :], ALU.max).then_inc(max_ok, 1)
                        elif s[0] == "maxT":
                            if u >= 2:
                                dve.wait_ge(max_rows[u - 2], 48 * (u // 2))
                            src = ps[0:4 * TPC, bank, 0:P]
                            part = [max_p[:, u % 2, k, :] for k in range(3)]
                            link(nc.vector.tensor_scalar(part[0], src, -1.0, None, ALU.mult))
                            nc.vector.scalar_tensor_tensor(max_s[:, :], src, -1.0, part[0],
                                                           ALU.mult, ALU.subtract).then_inc(ring_out, 1)
                            dve.wait_ge(ring_out, n + 1)
                            link(nc.vector.tensor_copy(part[1], max_s[:, :]))
                            nc.vector.tensor_tensor(part[2], max_s[:, :], part[1], ALU.subtract
                                                    ).then_inc(max_split, 1)
                        elif s[0] == "outT":
                            src = ps[:, bank, :].rearrange("p (t j d) -> p t j d", t=TPC, j=4)
                            link(nc.vector.reciprocal(den[:, :, :], src[:, :, :, HD]))
                            dst = o_n[:, TPC * c:TPC * (c + 1), 4 * g * HD:4 * (g + 1) * HD].rearrange(
                                "p t (j d) -> p t j d", j=4)
                            nc.vector.tensor_tensor(dst, src[:, :, :, 0:HD],
                                                    den[:, :, :].unsqueeze(3).broadcast_to([P, TPC, 4, HD]),
                                                    ALU.mult).then_inc(ring_out, 1)
                            dve.wait_ge(ring_out, n + 1)
                    dve.wait_ge(wb_ok, 16)
                    for col, n, weight in ((WB_QC, D, SM_N2), (WB_G, 2 * F, SM_N3)):
                        nc.vector.tensor_scalar(wb[:, col:col + n], wb[:, col:col + n],
                                                wb[:, WB_SM + weight:WB_SM + weight + 1], None, ALU.mult)
                    for i, c in enumerate((1, 0)):
                        dve.wait_ge(made, i + 1)
                        nc.vector.scalar_tensor_tensor(x_dec[:, chunk(c)], ps[:, made_bank[c], :],
                                                       wb[:, WB_SM + SM_BO:WB_SM + SM_BO + 1],
                                                       x_dec[:, chunk(c)], ALU.add, ALU.add)
            end_phase()

        def linear_phase(src_n, weight, bias):
            with phase() as block:
                turned, taken, made = sem("turned"), sem("taken"), sem("made")

                @block.tensor
                def _(pe):
                    for c in range(NCH):
                        for t in range(TPC):
                            mm = nc.tensor.transpose(ps[:, c, tile(t)], src_n[:, TPC * c + t, :], ident)
                        mm.then_inc(turned, 1)
                    for c in range(NCH):
                        pe.wait_ge(taken, c + 1)
                        nc.tensor.matmul(ps[:, 2 + c, :], weight, o_d[:, chunk(c)], start=True,
                                         stop=True).then_inc(made, 1)

                @block.scalar
                def _(act):
                    for c in range(NCH):
                        act.wait_ge(turned, c + 1)
                        nc.scalar.copy(o_d[:, chunk(c)], ps[:, c, :]).then_inc(taken, 1)

                @block.vector
                def _(dve):
                    for c in range(NCH):
                        dve.wait_ge(made, c + 1)
                        if bias is None:
                            nc.vector.tensor_tensor(x_dec[:, chunk(c)], x_dec[:, chunk(c)], ps[:, 2 + c, :], ALU.add)
                        else:
                            nc.vector.scalar_tensor_tensor(x_dec[:, chunk(c)], ps[:, 2 + c, :], bias,
                                                           x_dec[:, chunk(c)], ALU.add, ALU.add)
            end_phase()

        qc = qk[:, 0, :]
        k_bd = cen[:, 0:CH]
        mem_b = sb("mem_b", [P, P], BF16)
        v_bd = tmp[:, 0, :].rearrange("p (g n) -> p g n", g=QUADS)
        mem_sb = sb("mem_sb", [P, KEYS])
        mem4 = sb("mem4", [P, 4 * NEAR])
        cross_scale = HD ** -0.5

        def near_phase():
            k_sb = mem_sb[:, 0:NEAR]
            e_q = [prob[:, i, 0, :] for i in range(3)]
            p_t = [prob[:, i, 1, :] for i in range(3)]
            mx = max_q[:, :, :, :].rearrange("p a b c -> p (a b c)")
            with phase() as block:
                q_ps, q_ok, kv_ps = sem("q_ps"), sem("q_ok"), sem("kv_ps")
                k_ok, v_ok, d_ok = sem("k_ok"), sem("v_ok"), sem("d_ok")
                sums_q = [den[:, :, :].rearrange("p a b -> p (a b)"),
                          max_f[:, 0, :, :].rearrange("p a b -> p (a b)")]
                s_ps, s_out, e_ok, n_ok = sem("s_ps"), sem("s_out"), sem("e_ok"), sem("n_ok")
                t_ps, t_ok, o_ps = sem("t_ps"), sem("t_ok"), sem("o_ps")
                norm_pe, norm_act, rs_ok = norm("norm", x_dec, None, False, eps6)

                @block.tensor
                def _(pe):
                    nc.tensor.matmul(ps[:, 2, 0:NEAR], wb[:, WB_KC:WB_KC + D], mem4[:, 0:NEAR], start=True,
                                     stop=True).then_inc(kv_ps, 1)
                    nc.tensor.matmul(ps[:, 3, 0:D], mem4[:, :], wb[:, WB_VC:WB_VC + D], start=True,
                                     stop=True).then_inc(kv_ps, 1)
                    norm_pe(pe)
                    for c in range(NCH):
                        nc.tensor.matmul(ps[:, c, :], wb[:, WB_QC:WB_QC + D], x_dec[:, chunk(c)], start=True,
                                         stop=True).then_inc(q_ps, 1)
                    pe.wait_ge(q_ok, NCH)
                    pe.wait_ge(k_ok, 1)
                    pe.wait_ge(v_ok, 1)

                    def scores(t):
                        if t >= 2:
                            pe.wait_ge(s_out, t - 1)
                        nc.tensor.matmul(ps[:, t % 2, :], qc[:, tile(t)], k_bd[:, 0:H * NEAR], start=True,
                                         stop=False)
                        nc.tensor.matmul(ps[:, t % 2, :].rearrange("p (h k) -> p h k", h=H), id_b[:, :],
                                         mask_near[:, t, :].unsqueeze(1).broadcast_to([P, H, NEAR]),
                                         start=False, stop=True).then_inc(s_ps, 1)

                    def turn(t):
                        pe.wait_ge(n_ok, t + 1)
                        if t >= 2:
                            pe.wait_ge(t_ok, t - 1)
                        for g in range(QUADS):
                            mm = nc.tensor.transpose(ps[:, 2 + t % 2, tile(g)], e_q[t % 3][:, tile(g)], ident)
                        mm.then_inc(t_ps, 1)

                    def values(t):
                        pe.wait_ge(t_ok, t + 1)
                        for g in range(QUADS):
                            mm = nc.tensor.matmul(ps[:, 4 + t // TPC, tile(t % TPC)], v_bd[:, g, :],
                                                  p_t[t % 3][:, tile(g)], start=(g == 0), stop=(g == QUADS - 1))
                        mm.then_inc(o_ps, 1)

                    scores(0)
                    scores(1)
                    for t in range(NT + 2):
                        if t + 2 < NT:
                            scores(t + 2)
                        if 1 <= t <= NT:
                            turn(t - 1)
                        if t >= 2:
                            values(t - 2)
                    for c in range(NCH):
                        pe.wait_ge(t_ok, NT + c + 1)
                        nc.tensor.matmul(ps[:, 6 + c, :], wb[:, WB_OC:WB_OC + D], o_d[:, chunk(c)], start=True,
                                         stop=True).then_inc(o_ps, 1)

                @block.scalar
                def _(act):
                    norm_act(act)

                    def exps(t):
                        act.wait_ge(s_out, t + 1)
                        nc.scalar.activation(e_q[t % 3], e_q[t % 3], ACT.Exp, scale=cross_scale).then_inc(e_ok, 1)

                    def take(t):
                        act.wait_ge(t_ps, t + 1)
                        if t >= 3:
                            act.wait_ge(o_ps, t - 2)
                        nc.scalar.copy(p_t[t % 3], ps[:, 2 + t % 2, :]).then_inc(t_ok, 1)

                    for t in range(NT + 2):
                        if t < NT:
                            exps(t)
                        if t >= 2:
                            take(t - 2)
                    for c in range(NCH):
                        act.wait_ge(o_ps, TPC * (c + 1))
                        nc.scalar.copy(o_d[:, chunk(c)], ps[:, 4 + c, :]).then_inc(t_ok, 1)

                @block.gpsimd
                def _(pool_):
                    for t in range(NT):
                        pool_.wait_ge(d_ok, t + 1)
                        e3 = e_q[t % 3].rearrange("p (h k) -> p h k", h=H)
                        nc.gpsimd.tensor_tensor(e3, e3, sums_q[t % 2].unsqueeze(2).broadcast_to([P, H, NEAR]),
                                                ALU.mult).then_inc(n_ok, 1)

                @block.vector
                def _(dve):
                    link = chain(dve, "dve_step")
                    dve.wait_ge(kv_ps, 2)
                    link(nc.vector.tensor_copy(k_sb, ps[:, 2, 0:NEAR]))
                    nc.vector.tensor_tensor(k_bd[:, 0:H * NEAR].rearrange("p (h k) -> p h k", h=H),
                                            k_sb.unsqueeze(1).broadcast_to([P, H, NEAR]),
                                            tab[:, R_HM16:R_HM16 + H].unsqueeze(2).broadcast_to([P, H, NEAR]),
                                            ALU.mult).then_inc(k_ok, 1)
                    nc.vector.tensor_tensor(v_bd, ps[:, 3, 0:D].unsqueeze(1).broadcast_to([P, QUADS, D]),
                                            tab[:, R_VMASK:R_VMASK + QUADS * D].rearrange("p (g n) -> p g n", g=QUADS),
                                            ALU.mult).then_inc(v_ok, 1)
                    for c in range(NCH):
                        dve.wait_ge(q_ps, c + 1)
                        dve.wait_ge(rs_ok, c + 1)
                        nc.vector.tensor_tensor(qc[:, chunk(c)], ps[:, c, :], rs[:, chunk(c)], ALU.mult
                                                ).then_inc(q_ok, 1)

                    def shift(t):
                        dve.wait_ge(s_ps, t + 1)
                        if t >= 3:
                            dve.wait_ge(t_ps, t - 2)
                        s3 = ps[:, t % 2, :].rearrange("p (h k) -> p h k", h=H)
                        m = mx[:, 16 * (t % 2):16 * (t % 2) + 16]
                        link(nc.vector.tensor_reduce(m, s3, AX_X, ALU.max))
                        nc.vector.tensor_tensor(e_q[t % 3].rearrange("p (h k) -> p h k", h=H), s3,
                                                m.unsqueeze(2).broadcast_to([P, H, NEAR]),
                                                ALU.subtract).then_inc(s_out, 1)

                    def sums(t):
                        dve.wait_ge(e_ok, t + 1)
                        e3 = e_q[t % 3].rearrange("p (h k) -> p h k", h=H)
                        if t >= 2:
                            dve.wait_ge(n_ok, t - 1)
                        link(nc.vector.tensor_reduce(sums_q[t % 2], e3, AX_X, ALU.add))
                        nc.vector.reciprocal(sums_q[t % 2], sums_q[t % 2]).then_inc(d_ok, 1)

                    for t in range(NT + 1):
                        if t < NT:
                            shift(t)
                        if t >= 1:
                            sums(t - 1)
                    for c in range(NCH):
                        dve.wait_ge(o_ps, NT + c + 1)
                        nc.vector.tensor_tensor(x_dec[:, chunk(c)], x_dec[:, chunk(c)], ps[:, 6 + c, :], ALU.add)
            end_phase()

        def feed_forward_phase(layer):
            gate = [cen[:, 0:CH], cen[:, CH:T], o_t[:, :]]
            up_n = [qk[:, 0, 0:CH], qk[:, 0, CH:T], qk[:, 1, 0:CH]]
            hid = prob[:, :, :, :].rearrange("p a b c -> p a (b c)")
            units = [(c, f) for c in range(NCH) for f in range(FT)]
            with phase() as block:
                wa_ok, up, scaled, silu, hid_ok, down = (
                    sem(x) for x in ("wa_ok", "up", "scaled", "silu", "hid_ok", "down"))
                norm_pe, norm_act, rs_ok = norm("norm", x_dec, None, False, eps6)

                @block.sync
                def _(sp):
                    sp.dma_start(wa[:, :], layer_a[bass.ds(layer + 1, 1), :, :].rearrange("a p n -> (a p) n")
                                 ).then_inc(wa_ok, 16)
                    sp.wait_ge(wa_ok, 16)

                @block.tensor
                def _(pe):
                    norm_pe(pe)

                    def ups(n):
                        c, f = units[n]
                        b = 2 * (n % 3)
                        if n >= 3:
                            pe.wait_ge(scaled, 2 * (n - 2))
                        nc.tensor.matmul(ps[:, b, :], wb[:, WB_G + f * P:WB_G + (f + 1) * P], x_dec[:, chunk(c)],
                                         start=True, stop=True).then_inc(up, 1)
                        nc.tensor.matmul(ps[:, b + 1, :], wb[:, WB_U + f * P:WB_U + (f + 1) * P], x_dec[:, chunk(c)],
                                         start=True, stop=True).then_inc(up, 1)

                    def downs(n):
                        c, f = units[n]
                        pe.wait_ge(hid_ok, n + 1)
                        mm = nc.tensor.matmul(ps[:, 6 + c, :], wb[:, WB_DN + f * D:WB_DN + (f + 1) * D],
                                              hid[:, f, chunk(c)], start=(f == 0), stop=(f == FT - 1))
                        if f == FT - 1:
                            mm.then_inc(down, 1)

                    for n in range(len(units) + 2):
                        if n < len(units):
                            ups(n)
                        if n >= 2:
                            downs(n - 2)

                @block.scalar
                def _(act):
                    norm_act(act)
                    for n, (c, f) in enumerate(units):
                        act.wait_ge(scaled, 2 * n + 1)
                        nc.scalar.activation(gate[n % 3], gate[n % 3], ACT.Silu).then_inc(silu, 1)
                    nc.scalar.preload_act_table_set(LN_EXP)

                @block.vector
                def _(dve):

                    def scale(n):
                        c, f = units[n]
                        dve.wait_ge(rs_ok, c + 1)
                        if n >= 3:
                            dve.wait_ge(hid_ok, n - 2)
                        for i, dst in enumerate((gate[n % 3], up_n[n % 3])):
                            dve.wait_ge(up, 2 * n + 1 + i)
                            nc.vector.tensor_tensor(dst, ps[:, 2 * (n % 3) + i, :], rs[:, chunk(c)],
                                                    ALU.mult).then_inc(scaled, 1)

                    for n in range(len(units) + 1):
                        if n < len(units):
                            scale(n)
                        if n:
                            c, f = units[n - 1]
                            dve.wait_ge(silu, n)
                            dve.wait_ge(scaled, 2 * n)
                            nc.vector.tensor_tensor(hid[:, f, chunk(c)], gate[(n - 1) % 3], up_n[(n - 1) % 3],
                                                    ALU.mult).then_inc(hid_ok, 1)
                    for c in range(NCH):
                        dve.wait_ge(down, c + 1)
                        nc.vector.tensor_tensor(x_dec[:, chunk(c)], x_dec[:, chunk(c)], ps[:, 6 + c, :], ALU.add)
            end_phase()

        def far_path():
            iota = tab[:, R_IOTA:R_IOTA + KEYS]
            k_far = prob[:, :, :, :].rearrange("p a b c -> p (a b c)")[:, 0:H * KEYS]
            v_far = o_t[:, 0:D]
            e_far = cen[:, 0:CH]
            pt_far = cen[:, CH:T]
            hide = h[:, 0:P]
            pad = h[:, P:2 * P]
            near_end = h[:, 2 * P:2 * P + NT]
            top = sq[:, 0:NT * H].rearrange("p (t h) -> p t h", t=NT)
            total = sq[:, NT * H:2 * NT * H].rearrange("p (t h) -> p t h", t=NT)
            new = sq[:, 2 * NT * H:2 * NT * H + 4]
            seg_r = sq[:, 3 * NT * H:3 * NT * H + NT]
            end_r = sq[:, 4 * NT * H:4 * NT * H + 1]
            hide_b = mem_b[:, 0:P]

            def start():
                with phase() as block:
                    q_ps = sem("q_ps")
                    norm_pe, norm_act, rs_ok = norm("norm", x_dec, None, False, eps6)

                    @block.tensor
                    def _(pe):
                        norm_pe(pe)
                        for c in range(NCH):
                            nc.tensor.matmul(ps[:, c, :], wb[:, WB_QC:WB_QC + D], x_dec[:, chunk(c)],
                                             start=True, stop=True).then_inc(q_ps, 1)

                    @block.scalar
                    def _(act):
                        norm_act(act)

                    @block.vector
                    def _(dve):
                        for c in range(NCH):
                            dve.wait_ge(q_ps, c + 1)
                            dve.wait_ge(rs_ok, c + 1)
                            nc.vector.tensor_tensor(qc[:, chunk(c)], ps[:, c, :], rs[:, chunk(c)], ALU.mult)
                        nc.vector.memset(top, -float(2 ** 126))
                        nc.vector.memset(total, 0.0)
                        nc.vector.memset(o_n[:, :, :], 0.0)
                end_phase()

            def rewind():
                with phase() as block:
                    @block.vector
                    def _(dve):
                        nc.vector.tensor_copy(seg_r, seg_q[:, :])
                        nc.vector.memset(end_r, float(S_MEM - 1))
                end_phase()

            def block_phase(kb, sums):
                units = [(t, g) for t in range(NT) for g in range(QUADS)]
                with phase() as block:
                    mem_ok, kv_ps, kv_ok, hide_ok = (sem(x) for x in ("mem_ok", "kv_ps", "kv_ok", "hide_ok"))
                    s_ps, s_out, e_ok, t_ps, t_ok, o_ps, o_out = (
                        sem(x) for x in ("s_ps", "s_out", "e_ok", "t_ps", "t_ok", "o_ps", "o_out"))

                    @block.sync
                    def _(sp):
                        sp.dma_start(mem_sb[:, :], mem_t[bass.ds(kb, 1), :, :].rearrange("a p n -> (a p) n")
                                     ).then_inc(mem_ok, 16)

                    @block.tensor
                    def _(pe):
                        pe.wait_ge(mem_ok, 16)
                        nc.tensor.matmul(ps[:, 0, 0:KEYS], wb[:, WB_KC:WB_KC + D], mem_sb[:, :], start=True,
                                         stop=True)
                        nc.tensor.matmul(ps[:, 1, 0:D], mem_sb[:, :], wb[:, WB_VC:WB_VC + D], start=True,
                                         stop=True).then_inc(kv_ps, 1)
                        pe.wait_ge(kv_ok, 1)
                        for n, (t, g) in enumerate(units):
                            pe.wait_ge(hide_ok, t + 1)
                            if n:
                                pe.wait_ge(s_out, n)
                            nc.tensor.matmul(ps[:, 2, :], qc[:, tile(t)], k_far[:, g * CH:(g + 1) * CH],
                                             start=True, stop=False)
                            nc.tensor.matmul(ps[:, 2, :].rearrange("p (j k) -> p j k", j=4), id_b[:, :],
                                             hide_b.unsqueeze(1).broadcast_to([P, 4, KEYS]), start=False,
                                             stop=True).then_inc(s_ps, 1)
                            if not sums:
                                continue
                            pe.wait_ge(e_ok, n + 1)
                            if n:
                                pe.wait_ge(t_ok, n)
                            for j in range(4):
                                mm = nc.tensor.transpose(ps[:, 3, tile(j)], e_far[:, tile(j)], ident)
                            mm.then_inc(t_ps, 1)
                            pe.wait_ge(t_ok, n + 1)
                            if g == 0 and t:
                                pe.wait_ge(o_out, t)
                            for j in range(4):
                                col = (4 * g + j) * HD
                                mm = nc.tensor.matmul(ps[:, 4, col:col + HD], pt_far[:, tile(j)],
                                                      v_far[:, col:col + HD], start=True, stop=True)
                            mm.then_inc(o_ps, 1)

                    @block.scalar
                    def _(act):
                        if sums:
                            for n in range(len(units)):
                                act.wait_ge(s_out, n + 1)
                                nc.scalar.activation(e_far, e_far, ACT.Exp, scale=cross_scale).then_inc(e_ok, 1)
                                act.wait_ge(t_ps, n + 1)
                                if n:
                                    act.wait_ge(o_ps, n)
                                nc.scalar.copy(pt_far, ps[:, 3, :]).then_inc(t_ok, 1)

                    @block.vector
                    def _(dve):
                        link = chain(dve, "dve_step")
                        dve.wait_ge(kv_ps, 1)
                        link(nc.vector.tensor_copy(e_far[:, 0:KEYS], ps[:, 0, 0:KEYS]))
                        link(nc.vector.tensor_copy(v_far, ps[:, 1, 0:D]))
                        link(nc.vector.tensor_tensor(
                            k_far.rearrange("p (h k) -> p h k", h=H),
                            e_far[:, 0:KEYS].unsqueeze(1).broadcast_to([P, H, KEYS]),
                            tab[:, R_HM16:R_HM16 + H].unsqueeze(2).broadcast_to([P, H, KEYS]), ALU.mult))
                        nc.vector.tensor_copy(new[:, 0:1], end_r).then_inc(kv_ok, 1)
                        link(nc.vector.tensor_scalar(pad, iota, end_r, NEG_PAD / NEG, ALU.is_gt, ALU.mult))
                        link(nc.vector.tensor_scalar(near_end, seg_r, -float(LOOKBACK), None, ALU.add))
                        for n, (t, g) in enumerate(units):
                            if g == 0:
                                link(nc.vector.tensor_scalar(hide, iota, seg_r[:, t:t + 1], None, ALU.is_gt))
                                link(nc.vector.scalar_tensor_tensor(hide, iota, near_end[:, t:t + 1], hide,
                                                                    ALU.is_le, ALU.max))
                                link(nc.vector.tensor_tensor(hide, hide, pad, ALU.max))
                                if n:
                                    dve.wait_ge(s_ps, n)
                                nc.vector.tensor_scalar(hide_b, hide, NEG, None, ALU.mult).then_inc(hide_ok, 1)
                            dve.wait_ge(s_ps, n + 1)
                            s3 = ps[:, 2, :].rearrange("p (j k) -> p j k", j=4)
                            heads = slice(4 * g, 4 * g + 4)
                            if not sums:
                                link(nc.vector.tensor_reduce(new, s3, AX_X, ALU.max))
                                nc.vector.tensor_tensor(top[:, t, heads], top[:, t, heads], new,
                                                        ALU.max).then_inc(s_out, 1)
                                dve.wait_ge(s_out, n + 1)
                                continue
                            if n:
                                dve.wait_ge(t_ps, n)
                            e3 = e_far.rearrange("p (j k) -> p j k", j=4)
                            nc.vector.tensor_tensor(e3, s3, top[:, t, heads].unsqueeze(2).broadcast_to([P, 4, KEYS]),
                                                    ALU.subtract).then_inc(s_out, 1)
                            dve.wait_ge(e_ok, n + 1)
                            link(nc.vector.tensor_reduce(new, e3, AX_X, ALU.add))
                            link(nc.vector.tensor_tensor(total[:, t, heads], total[:, t, heads], new, ALU.add))
                            if g == QUADS - 1:
                                dve.wait_ge(o_ps, n + 1)
                                nc.vector.tensor_tensor(o_n[:, t, :], o_n[:, t, :], ps[:, 4, 0:D],
                                                        ALU.add).then_inc(o_out, 1)
                        nc.vector.tensor_scalar(seg_r, seg_r, -float(KEYS), None, ALU.add)
                        nc.vector.tensor_scalar(end_r, end_r, -float(KEYS), None, ALU.add)
                end_phase()

            def finish():
                with phase() as block:
                    @block.vector
                    def _(dve):
                        link = chain(dve, "dve_step")
                        link(nc.vector.reciprocal(total, total))
                        o4 = o_n[:, :, :].rearrange("p t (h d) -> p t h d", h=H)
                        nc.vector.tensor_tensor(o4, o4, total.unsqueeze(3).broadcast_to([P, NT, H, HD]), ALU.mult)
                end_phase()

            start()
            for sums in (False, True):
                rewind()
                with nc.Fori(0, MEM_BLOCKS) as kb:
                    block_phase(kb, sums)
            finish()
            linear_phase(o_n, wb[:, WB_OC:WB_OC + D], None)

        rt = sb("rt", [P, RT_COLS])
        exp_w = big[:, 0:16 * T].bitcast(F32).rearrange("p (e n) -> p e n", e=E)
        gate_rows = sb("gate_rows", [3 * E, T], BF16)
        gate_t = sb("gate_t", [E, T])
        pick_e = sb("pick_e", [3 * E, E * P], BF16)
        b2_sb = sb("b2_sb", [E, D])

        units = [(c, e, f) for c in range(NCH) for e in range(E) for f in range(MT)]
        FIRST = 16
        first_h = big[:, 16 * T:32 * T].bitcast(F32).rearrange("p (n t) -> p n t", n=FIRST)
        more_h = v_aug[:, :, :, :].rearrange("p t h d -> p (t h d)").rearrange("p (n t) -> p n t", t=CH)
        early_h = ([first_h[:, n, :] for n in range(FIRST)] + [more_h[:, n, :] for n in range(8)]
                   + [x_dec[:, chunk(c)] for c in range(NCH)] + [o_d[:, chunk(c)] for c in range(NCH)]
                   + [o_n[:, TPC * c:TPC * (c + 1), :].rearrange("p t d -> p (t d)") for c in range(NCH)]
                   + [prob[:, 3, c, :] for c in range(NCH)])
        EARLY = len(early_h)

        def route_phase():
            small = cen[:, 0:14 * NT * E].rearrange("p (n t e) -> p n t e", n=14, t=NT)
            prob_e, best, cand, one1, one2, rest, chosen, gates_s, gates_f, r1 = (small[:, i] for i in range(10))
            col = lambda i: small[:, 10, i, :]
            top, tie1, top2, tie2, denom = (col(i) for i in range(5))
            count = small[:, 11:13].rearrange("p n t e -> p (n t e)").rearrange("p (n k t) -> p n k t", n=8, k=TOPK)
            rank = rs[:, 2 * P:2 * P + TOPK * NT].rearrange("p (k t) -> p k t", k=TOPK)
            bpart = parts[:, 0, 0, 0:NT * 3 * E].rearrange("p (t a e) -> p t a e", t=NT, a=3)
            bone = [parts[:, 0, 1 + k, 0:NT * 3 * E].rearrange("p (t a e) -> p t a e", t=NT, a=3)
                    for k in range(TOPK)]
            bgate = parts[:, 1, 0, 0:NT * 3 * E].rearrange("p (t a e) -> p t a e", t=NT, a=3)
            rows = [parts[0:3 * E, 1, 1, :], parts[0:3 * E, 1, 2, :], gate_rows[:, :]]
            junk = [qk[:, 1, :], sq[:, :], rs[:, 0:P], rs[:, P:2 * P]]
            pick_f = qk[0:3 * E, 0, :]

            def early_bank(n):
                return 4 + n % 4 if n < FIRST else n % 4
            e_rev = tab[:, R_EREV:R_EREV + E].unsqueeze(1).broadcast_to([P, NT, E])
            tri, offd = tab[:, R_TRI:R_TRI + P], tab[:, R_OFFD:R_OFFD + P]

            def wide(x):
                return x.unsqueeze(2).broadcast_to([P, NT, E])

            with phase() as block:
                l_ps, l_ok, e_ok = sem("l_ps"), sem("l_ok"), sem("e_ok")
                added, up, silu = sem("added"), sem("up"), sem("silu")
                norm_pe, norm_act, norm_dve, n_ok = norm("norm", x_dec, h, False, eps6, nf_col[:, 0:1])
                ln_pe, ln_act, ln_dve, h_ok = norm("ln", x_res, h, True, eps5, None, added)
                got = sem("got")
                parts_ok, t_ps, t_ok, r_ps, r_out = (sem(x) for x in ("parts_ok", "t_ps", "t_ok", "r_ps", "r_out"))
                g_ok, gt_ps = sem("g_ok"), sem("gt_ps")

                @block.sync
                def _(sp):
                    sp.dma_start(rt[:, :], router).then_inc(got, 16)
                    sp.dma_start(pick_f, tables[0:3 * E, R_COLS:R_COLS + E * P]).then_inc(got, 16)
                    sp.dma_start(b2_sb[:, :], b2).then_inc(got, 16)
                    for e in range(E):
                        sp.dma_start(exp_w[:, e, 0:MF], w1[e]).then_inc(experts_got, 16)
                        sp.dma_start(exp_w[:, e, MF:2 * MF], w2[e]).then_inc(experts_got, 16)

                @block.tensor
                def _(pe):
                    norm_pe(pe)
                    ln_pe(pe)
                    pe.wait_ge(h_ok, NCH)
                    pe.wait_ge(got, 16 * 3)
                    for t in range(NT):
                        mm = nc.tensor.matmul(ps[:, 0, E * t:E * (t + 1)], h[:, tile(t)], rt[:, RT_W:RT_W + E],
                                              start=True, stop=True)
                    mm.then_inc(l_ps, 1)

                    def up_product(n):
                        c, e, f = units[n]
                        if n >= 4:
                            pe.wait_ge(silu, n - 3)
                        nc.tensor.matmul(ps[:, early_bank(n), :], exp_w[:, e, f * P:(f + 1) * P], h[:, chunk(c)],
                                         start=True, stop=True).then_inc(up, 1)

                    pe.wait_ge(experts_got, 16 * 2 * E)
                    for n in range(FIRST):
                        up_product(n)
                    pe.wait_ge(parts_ok, 1)
                    for b, src in enumerate((bpart, bone[0], bone[1])):
                        for t in range(NT):
                            mm = nc.tensor.transpose(ps[0:3 * E, 1 + b, :].bitcast(BF16)[:, tile(t)],
                                                     src[:, t, :, :].rearrange("p a e -> p (a e)"), id_b[:, :])
                        mm.then_inc(t_ps, 1)
                    pe.wait_ge(t_ok, 3)
                    pe.wait_ge(silu, FIRST)
                    n = 0
                    for k in range(TOPK):
                        for t in range(NT):
                            if n >= 2:
                                pe.wait_ge(r_out, n - 1)
                            for c in range(NCH):
                                mm = nc.tensor.matmul(ps[:, 4 + 2 * (n % 2) + c, :], rows[1 + k][:, tile(t)],
                                                      rows[0][:, chunk(c)], start=True, stop=True)
                            mm.then_inc(r_ps, 1)
                            if FIRST + n < EARLY:
                                up_product(FIRST + n)
                            n += 1
                    pe.wait_ge(g_ok, 1)
                    pe.wait_ge(silu, EARLY)
                    for t in range(NT):
                        mm = nc.tensor.transpose(ps[0:3 * E, 1, :].bitcast(BF16)[:, tile(t)],
                                                 bgate[:, t, :, :].rearrange("p a e -> p (a e)"), id_b[:, :])
                    mm.then_inc(gt_ps, 1)
                    for t in range(NT):
                        mm = nc.tensor.transpose(ps[0:E, 2 + t // TPC, tile(t % TPC)], gates_f[:, t, :], ident)
                    mm.then_inc(gt_ps, 1)

                @block.scalar
                def _(act):
                    norm_act(act)
                    ln_act(act)
                    act.wait_ge(l_ok, 1)
                    nc.scalar.activation(prob_e, best, ACT.Exp).then_inc(e_ok, 1)
                    for n in range(EARLY):
                        c, e, f = units[n]
                        act.wait_ge(up, n + 1)
                        col = RT_B1 + e * MT + f
                        nc.scalar.activation(early_h[n], ps[:, early_bank(n), :], ACT.Silu,
                                             bias=rt[:, col:col + 1]).then_inc(silu, 1)

                @block.vector
                def _(dve):
                    link = chain(dve, "dve_step")
                    v = nc.vector
                    norm_dve(dve)
                    for c in range(NCH):
                        dve.wait_ge(n_ok, c + 1)
                        nc.vector.tensor_tensor(x_res[:, chunk(c)], x_res[:, chunk(c)], h[:, chunk(c)],
                                                ALU.add).then_inc(added, 1)
                    dve.wait_ge(added, NCH)
                    ln_dve(dve)
                    dve.wait_ge(h_ok, NCH)
                    dve.wait_ge(got, 16 * 3)
                    link(v.tensor_copy(pick_e[:, :], pick_f))
                    dve.wait_ge(l_ps, 1)
                    link(v.tensor_tensor(prob_e, ps[:, 0, 0:NT * E].rearrange("p (t e) -> p t e", t=NT),
                                         rt[:, RT_B:RT_B + E].unsqueeze(1).broadcast_to([P, NT, E]), ALU.add))
                    link(v.tensor_reduce(top, prob_e, AX_X, ALU.max))
                    v.tensor_tensor(best, prob_e, wide(top), ALU.subtract).then_inc(l_ok, 1)
                    dve.wait_ge(e_ok, 1)
                    link(v.tensor_reduce(denom, prob_e, AX_X, ALU.add))
                    link(v.reciprocal(denom, denom))
                    link(v.tensor_tensor(prob_e, prob_e, wide(denom), ALU.mult))
                    for src, t_, tie, one in ((prob_e, top, tie1, one1), (rest, top2, tie2, one2)):
                        link(v.tensor_reduce(t_, src, AX_X, ALU.max))
                        link(v.tensor_tensor(best, src, wide(t_), ALU.is_equal))
                        link(v.tensor_tensor(cand, best, e_rev, ALU.mult))
                        link(v.tensor_reduce(tie, cand, AX_X, ALU.max))
                        link(v.tensor_tensor(one, e_rev, wide(tie), ALU.is_equal))
                        if src is prob_e:
                            link(v.scalar_tensor_tensor(rest, one1, -2.0, prob_e, ALU.mult, ALU.add))
                    link(v.tensor_tensor(chosen, one1, one2, ALU.add))
                    link(v.tensor_tensor(gates_s, prob_e, chosen, ALU.mult))
                    link(v.scalar_tensor_tensor(gates_s, chosen, -1.0, gates_s, ALU.add, ALU.add))

                    def split(dst, src):
                        link(v.tensor_copy(dst[:, :, 0, :], src))
                        link(v.tensor_tensor(r1, src, dst[:, :, 0, :], ALU.subtract))
                        link(v.tensor_copy(dst[:, :, 1, :], r1))
                        link(v.tensor_tensor(dst[:, :, 2, :], r1, dst[:, :, 1, :], ALU.subtract))

                    split(bpart, gates_s)
                    for k, one in enumerate((one1, one2)):
                        link(v.tensor_copy(bone[k], one.unsqueeze(2).broadcast_to([P, NT, 3, E])))
                    v.memset(count, 0.0).then_inc(parts_ok, 1)
                    for b in range(3):
                        dve.wait_ge(t_ps, b + 1)
                        v.tensor_copy(rows[b], ps[0:3 * E, 1 + b, :].bitcast(BF16)).then_inc(t_ok, 1)
                    dve.wait_ge(parts_ok, 1)
                    n = 0
                    for k, g in enumerate((top, top2)):
                        for t in range(NT):
                            dve.wait_ge(r_ps, n + 1)
                            if n:
                                dve.wait_ge(r_out, n)
                            r = ps[:, 4 + 2 * (n % 2):6 + 2 * (n % 2), :].rearrange("p a b -> p (a b)")
                            gi = g[:, t:t + 1]
                            here = r[:, tile(t)]
                            if t:
                                v.tensor_scalar(junk[0][:, 0:t * P], r[:, 0:t * P], gi, 0.0, ALU.is_ge, ALU.add,
                                                accum_out=count[:, 0, k, t:t + 1])
                            if t < NT - 1:
                                v.tensor_scalar(junk[1][:, 0:T - (t + 1) * P], r[:, (t + 1) * P:T], gi, 0.0,
                                                ALU.is_gt, ALU.add, accum_out=count[:, 1, k, t:t + 1])
                            v.scalar_tensor_tensor(junk[2], here, gi, offd, ALU.is_gt, ALU.mult,
                                                   accum_out=count[:, 2, k, t:t + 1])
                            v.scalar_tensor_tensor(junk[3], here, gi, tri, ALU.is_equal, ALU.mult,
                                                   accum_out=count[:, 3, k, t:t + 1]).then_inc(r_out, 1)
                            n += 1
                    dve.wait_ge(r_out, n)
                    link(v.tensor_tensor(rank, count[:, 0], count[:, 1], ALU.add))
                    link(v.tensor_tensor(rank, rank, count[:, 2], ALU.add))
                    link(v.tensor_tensor(rank, rank, count[:, 3], ALU.add))
                    link(v.tensor_scalar(rank, rank, float(CAP), None, ALU.is_lt))
                    link(v.tensor_tensor(tie1, top, rank[:, 0], ALU.mult))
                    link(v.tensor_tensor(tie2, top2, rank[:, 1], ALU.mult))
                    link(v.tensor_tensor(cand, one1, wide(tie1), ALU.mult))
                    link(v.tensor_tensor(best, one2, wide(tie2), ALU.mult))
                    link(v.tensor_tensor(gates_f, cand, best, ALU.add))
                    split(bgate, gates_f)
                    v.tensor_copy(denom, denom).then_inc(g_ok, 1)
                    dve.wait_ge(gt_ps, 1)
                    v.tensor_copy(gate_rows[:, :], ps[0:3 * E, 1, :].bitcast(BF16))
                    dve.wait_ge(gt_ps, 2)
                    for c in range(NCH):
                        v.tensor_copy(gate_t[:, chunk(c)], ps[0:E, 2 + c, :])
            end_phase()

        def experts_phase():
            act_h = [early_h[n] if n < EARLY else prob[:, n % 3, 0, :] for n in range(len(units))]
            gated = [prob[:, i, 1, :] for i in range(3)]
            with phase() as block:
                up, gate_ps, silu, hid_ok, down, done, stored = (
                    sem(x) for x in ("up", "gate_ps", "silu", "hid_ok", "down", "done", "stored"))

                @block.sync
                def _(sp):
                    for c in range(NCH):
                        sp.wait_ge(done, c + 1)
                        sp.dma_start(out[:, chunk(c)], x_res[:, chunk(c)]).then_inc(stored, 16)
                    sp.wait_ge(stored, 16 * NCH)

                @block.tensor
                def _(pe):
                    pe.wait_ge(experts_got, 16 * 2 * E)

                    def ups(n):
                        c, e, f = units[n]
                        m = n // MT
                        if f == 0:
                            if m >= 2:
                                pe.wait_ge(hid_ok, MT * (m - 1))
                            nc.tensor.matmul(ps[:, 3 + m % 2, :], pick_e[:, e * P:(e + 1) * P],
                                             gate_rows[:, chunk(c)], start=True, stop=True).then_inc(gate_ps, 1)
                        if n < EARLY:
                            return
                        if n >= EARLY + 3:
                            pe.wait_ge(silu, n - 2 - EARLY)
                        nc.tensor.matmul(ps[:, n % 3, :], exp_w[:, e, f * P:(f + 1) * P], h[:, chunk(c)],
                                         start=True, stop=True).then_inc(up, 1)

                    def downs(n):
                        c, e, f = units[n]
                        if e == 0 and f == 0:
                            nc.tensor.matmul(ps[:, 6 + c, :], b2_sb[:, :], gate_t[:, chunk(c)], start=True,
                                             stop=False)
                        pe.wait_ge(hid_ok, n + 1)
                        mm = nc.tensor.matmul(ps[:, 6 + c, :], exp_w[:, e, MF + f * D:MF + (f + 1) * D],
                                              gated[n % 3], start=False, stop=(e == E - 1 and f == MT - 1))
                        mm.then_inc(down, 1)

                    for n in range(len(units) + 2):
                        if n < len(units):
                            ups(n)
                        if n >= 2:
                            downs(n - 2)

                @block.scalar
                def _(act):
                    for n in range(EARLY, len(units)):
                        c, e, f = units[n]
                        act.wait_ge(up, n + 1 - EARLY)
                        if n >= EARLY + 3:
                            act.wait_ge(hid_ok, n - 2)
                        col = RT_B1 + e * MT + f
                        nc.scalar.activation(act_h[n], ps[:, n % 3, :], ACT.Silu, bias=rt[:, col:col + 1]
                                             ).then_inc(silu, 1)

                @block.vector
                def _(dve):
                    for n, (c, e, f) in enumerate(units):
                        if n >= EARLY:
                            dve.wait_ge(silu, n + 1 - EARLY)
                        dve.wait_ge(gate_ps, n // MT + 1)
                        if n >= 3:
                            dve.wait_ge(down, n - 2)
                        nc.vector.tensor_tensor(gated[n % 3], act_h[n], ps[:, 3 + (n // MT) % 2, :],
                                                ALU.mult).then_inc(hid_ok, 1)
                        if e == E - 1 and f == MT - 1:
                            dve.wait_ge(down, n + 1)
                            nc.vector.tensor_tensor(x_res[:, chunk(c)], x_res[:, chunk(c)], ps[:, 6 + c, :],
                                                    ALU.add).then_inc(done, 1)
            end_phase()

        def decoder_input_phase():
            with phase() as block:
                filled = sem("filled")
                norm_pe, norm_act, norm_dve, _ = norm("norm", x_res, x_dec, True, eps5)
                first = SLOTS * HD

                @block.sync
                def _(sp):
                    for rows, n in ((big[:, 0:16 * T], ZERO_ROWS), (big[:, 16 * T:32 * T], ZERO_ROWS + 3)):
                        dst = rows[first:first + n, :].bitcast(I32)
                        sp.dma_start(dst, fill[0:n, :]).then_inc(filled, 16)
                    sp.wait_ge(filled, 16 * 2)

                @block.tensor
                def _(pe):
                    norm_pe(pe)

                @block.scalar
                def _(act):
                    norm_act(act)

                @block.vector
                def _(dve):
                    norm_dve(dve)
            end_phase()

        win = wb[:, 0:WW_COLS]
        load_phase(win)
        window_phase(win)
        decoder_input_phase()
        far = nc.values_load(flag_i[0:1, 0:1], min_val=0, max_val=1)
        with nc.Fori(0, LAYERS) as layer:
            self_attention_phase(layer)
            with nc.If(far < 1):
                nc.gpsimd.nop()
                nc.sync.nop()
                near_phase()
            with nc.Else():
                nc.gpsimd.nop()
                nc.sync.nop()
                far_path()
            feed_forward_phase(layer)
        route_phase()
        experts_phase()


def constants():
    con = np.zeros((P, C_COLS), np.float32)
    i = np.arange(P)
    con[:, C_ID:C_ID + P] = np.eye(P)
    con[:, C_MEAN:C_MEAN + P] = 1.0 / D
    con[:, C_MASKQ:C_MASKQ + P] = np.where(i[None, :] > i[:, None], NEG, 0.0)
    con[:, C_NEGI:C_NEGI + P] = np.eye(P) * WIN_NEG
    for w in range(WH):
        con[w * WD:(w + 1) * WD, C_HM + w] = 1.0
    ahead = np.arange(T)[None, :] - i[:, None]
    con[:, C_REL:C_REL + T] = np.where(ahead < 0, 1e9, ahead)
    con[:, C_EPS5], con[:, C_EPS6] = 1e-5, 1e-6

    tab = np.zeros((P, R_COLS + E * P), np.float32)
    f = i // H
    inv = (1.0 / np.float32(10000.0) ** (np.arange(0, HD, 2, dtype=np.float32) / np.float32(HD))).astype(np.float32)
    angle = (np.arange(T, dtype=np.float32)[None, :] * inv[f % (HD // 2)][:, None]).astype(np.float32)
    tab[:, R_COS:R_COS + T] = np.cos(angle)
    tab[:, R_SIN:R_SIN + T] = np.sin(angle) * np.where(f < HD // 2, -1.0, 1.0)[:, None]
    for hh in range(H):
        tab[hh * HD:(hh + 1) * HD, R_HM16 + hh] = 1.0
    for g in range(QUADS):
        for j in range(4):
            c0 = R_VMASK + g * D + (4 * g + j) * HD
            tab[NEAR * j:NEAR * (j + 1), c0:c0 + HD] = 1.0
    tab[:, R_IOTA:R_IOTA + P] = i[None, :]
    tab[:, R_TRI:R_TRI + P] = i[None, :] < i[:, None]
    tab[:, R_OFFD:R_OFFD + P] = i[None, :] != i[:, None]
    tab[:, R_EREV:R_EREV + E] = E - np.arange(E)
    for e in range(E):
        for a in range(3):
            tab[a * E + e, R_COLS + e * P:R_COLS + (e + 1) * P] = 1.0
    return con, tab


def layout(v):
    a = {k: np.asarray(x) for k, x in v.items()}
    con, tab = constants()
    col = lambda x: np.asarray(x).reshape(-1, 1)
    wide = lambda x: np.broadcast_to(np.asarray(x).reshape(1, -1), (P, np.size(x)))

    win = np.zeros((P, WW_COLS), np.float32)
    wt, wbias = a["L0_attn_qkv_w"].T, a["L0_attn_qkv_b"]
    win[:, 0:3 * D] = wt
    win[:, WW_BV:WW_BV + D] = wide(wbias[2 * D:])
    win[:, WW_OFF:WW_OFF + WD] = a["L0_attn_off_w"].T
    win[:, WW_SM], win[:, WW_SM + 1] = wbias[0:D], wbias[D:2 * D]
    win[0:WD, WW_SM + 2] = a["L0_attn_lin2_w"][0]
    win[:, WW_SM + 3] = a["L0_attn_lin2_b"][0]

    f, head = np.meshgrid(np.arange(HD), np.arange(H), indexing="ij")
    order = (head * HD + f).ravel()
    swapped = (head * HD + (f + HD // 2) % HD).ravel()
    la = np.zeros((LAYERS + 1, P, WA_COLS), np.float32)
    lb = np.zeros((LAYERS, P, WB_COLS), np.float32)
    for n in range(LAYERS):
        w, b = a["L0_xattn_Wqkv"][n], a["L0_xattn_bqkv"][n]
        la[n] = np.concatenate(
            [w[order].T, w[swapped].T, w[D + order].T, w[D + swapped].T, w[2 * D:].T, wide(b[2 * D:]),
             col(a["L0_xattn_n1"][n]), col(b[order]), col(b[swapped]), col(b[D + order]), col(b[D + swapped])], 1)
        kv = a["L0_xattn_Wkv_c"][n]
        down = a["L0_xattn_Wd"][n].T.reshape(FT, P, D).transpose(1, 0, 2).reshape(P, FT * D)
        lb[n] = np.concatenate(
            [a["L0_xattn_Wo"][n].T, a["L0_xattn_Wq_c"][n].T, kv[:D].T, kv[D:].T, a["L0_xattn_Wo_c"][n].T,
             col(a["L0_xattn_bo"][n]), col(a["L0_xattn_n2"][n]), col(a["L0_xattn_n3"][n]),
             a["L0_xattn_Wg"][n].T, a["L0_xattn_Wu"][n].T, down], 1)
    mem = np.zeros((P, MEM_BLOCKS * KEYS), np.float32)
    mem[:, :S_MEM] = a["ctx_1024"][0].T
    router = np.concatenate([a["L0_ffn_Wr"], wide(a["L0_ffn_br"]),
                             a["L0_ffn_b1"].reshape(E * MT, P).T], 1)
    seg = a["itok_BxS_0_255"][0]
    return {
        "x_t": a["x"][0].T, "seg_row": seg[None, :], "seg_col": seg.reshape(NT, P).T,
        "consts": con, "tables": tab, "win_w": win,
        "mem_t": mem.reshape(P, MEM_BLOCKS, KEYS).transpose(1, 0, 2),
        "layer_a": la, "layer_b": lb, "router": router, "w1": a["L0_ffn_W1"],
        "w2": a["L0_ffn_W2"].reshape(E, MT, P, D).transpose(0, 2, 1, 3).reshape(E, P, MT * D),
        "b2": a["L0_ffn_b2"], "nf": col(a["L0_xattn_nf"]),
        "fill": np.repeat(np.array([[0]] * ZERO_ROWS + [[0x3F803F80]] * 3, np.int32), H * T // 2, 1),
    }


def kernel(**inputs):
    import concourse.bacc as _bacc
    from concourse.bass_utils import run_bass_kernel_spmd as _run

    nc = _bacc.Bacc("TRN2", target_bir_lowering=False, num_devices=1)
    arrays, args = {}, {}
    for name, a in layout(inputs).items():
        a = np.ascontiguousarray(a)
        arrays[f"in_{name}_dram"] = a
        args[name] = nc.dram_tensor(f"in_{name}_dram", a.shape, mybir.dt.from_np(a.dtype), kind="ExternalInput").ap()
    out = nc.dram_tensor("out_dram", (P, T), F32, kind="ExternalOutput").ap()
    build(nc, out=out, **args)
    r = _run(nc, [arrays], core_ids=[0])
    return np.ascontiguousarray(r.results[0]["out_dram"].T)[None]
```
